# Optimizing a Trainium2 kernel written in Bass

```python
import numpy as np
import jax
import jax.numpy as jnp

def _softmax(x, axis=-1):
    return jax.nn.softmax(x, axis=axis)

def _gelu(x):
    return jax.nn.gelu(x, approximate=True)

def _silu(x):
    return jax.nn.silu(x)

def _sigmoid(x):
    return jax.nn.sigmoid(x)

def _layernorm(x, axis=-1, eps=1e-05):
    m = jnp.mean(x, axis=axis, keepdims=True)
    v = jnp.var(x, axis=axis, keepdims=True)
    return (x - m) / jnp.sqrt(v + eps)

def _scatter_add(tgt, idx, src, axis=0):
    return tgt.at[idx].add(src)

def _segment_sum(src, seg, n):
    return jax.ops.segment_sum(src, seg, n)
kernel_name = 'mk_gnn_resnorm_d4_gnn_r64_562d65'

def setup_inputs(seed: int=0):
    np.random.seed(seed)
    _w = jnp.asarray

    def _rec_inputs():
        import jax
        import jax.numpy as jnp
        _gk = jax.random.key(seed)
        x = -0.000202 + 1 * jax.random.normal(jax.random.fold_in(_gk, 1), (100000, 64), jnp.float32)
        src = jax.random.randint(jax.random.fold_in(_gk, 2), (50000,), 0, 100000, jnp.int32)
        dst = jnp.minimum((100000 * jax.random.uniform(jax.random.fold_in(_gk, 3), (50000,)) ** 2.0).astype(jnp.int32), 99999)
        _o = jnp.argsort(dst, stable=True)
        src = src[_o]
        dst = dst[_o]
        edge_attr_16 = 0.000196303 + 1.00016 * jax.random.normal(jax.random.fold_in(_gk, 12), (50000, 16), jnp.float32)
        edge_weight = jax.random.uniform(jax.random.fold_in(_gk, 14), (50000,), jnp.float32, 0.0, 1)
        edge_weight1 = jax.random.uniform(jax.random.fold_in(_gk, 15), (50000, 1), jnp.float32, 0.0, 1)
        return (x, src, dst, edge_attr_16, edge_weight, edge_weight1)
    x, src, dst, edge_attr_16, edge_weight, edge_weight1 = _rec_inputs()

    def _L0_gnn_setup():
        import jax, jax.numpy as jnp
        import numpy as np
        N_NODES = 100000
        N_EDGES = 25000
        IN_FEATS = 64
        OUT_FEATS = 64
        key = jax.random.key(seed)
        ks = jax.random.split(key, 6)
        feat = jax.random.normal(ks[0], (N_NODES, IN_FEATS), dtype=jnp.float32)
        e_feat = jax.random.uniform(ks[1], (N_EDGES, 1), dtype=jnp.float32)
        src = jax.random.randint(ks[2], (N_EDGES,), 0, N_NODES, dtype=jnp.int32)
        dst = jax.random.randint(ks[3], (N_EDGES,), 0, N_NODES, dtype=jnp.int32)
        gain = float(np.sqrt(2.0))
        bound = gain * float(np.sqrt(6.0 / (IN_FEATS + OUT_FEATS)))
        W_self = jax.random.uniform(ks[4], (OUT_FEATS, IN_FEATS), dtype=jnp.float32, minval=-bound, maxval=bound)
        W_neigh = jax.random.uniform(ks[5], (OUT_FEATS, IN_FEATS), dtype=jnp.float32, minval=-bound, maxval=bound)
        b_self = jnp.zeros((OUT_FEATS,), dtype=jnp.float32)
        b_neigh = jnp.zeros((OUT_FEATS,), dtype=jnp.float32)
        return {'feat': feat, 'e_feat': e_feat, 'src': src, 'dst': dst, 'W_self': W_self, 'b_self': b_self, 'W_neigh': W_neigh, 'b_neigh': b_neigh}
    _L0_gnn_all = _L0_gnn_setup()
    _L0_gnn_in = {k: v for k, v in _L0_gnn_all.items() if k in ('W_self', 'b_self', 'W_neigh', 'b_neigh')}
    del _L0_gnn_all

    def _L1_gnn_setup():
        import jax, jax.numpy as jnp
        import numpy as np
        N_NODES = 100000
        N_EDGES = 25000
        D_IN = 64
        HIDDEN = 64

        def _res_gated_conv(x, Wk, Wq, Wv, Ws, b, src, dst, num_nodes):
            k = x @ Wk
            q = x @ Wq
            v = x @ Wv
            msg = jax.nn.sigmoid(k[dst] + q[src]) * v[src]
            agg = jax.ops.segment_sum(msg, dst, num_segments=num_nodes)
            return agg + x @ Ws + b
        key = jax.random.key(seed)
        ks = jax.random.split(key, 16)
        scale_in = 1.0 / np.sqrt(D_IN)
        scale_h = 1.0 / np.sqrt(HIDDEN)
        x = jax.random.normal(ks[0], (N_NODES, D_IN), dtype=jnp.float32)
        edge_index = jax.random.randint(ks[1], (2, N_EDGES), 0, N_NODES, dtype=jnp.int64)

        def w(k, din, dout, s):
            return jax.random.normal(k, (din, dout), dtype=jnp.float32) * s
        inp = {'x': x, 'Wk1': w(ks[2], D_IN, HIDDEN, scale_in), 'Wq1': w(ks[3], D_IN, HIDDEN, scale_in), 'Wv1': w(ks[4], D_IN, HIDDEN, scale_in), 'Ws1': w(ks[5], D_IN, HIDDEN, scale_in), 'b1': jnp.zeros((HIDDEN,), dtype=jnp.float32), 'Wl1': w(ks[6], HIDDEN, HIDDEN, scale_h), 'bl1': jnp.zeros((HIDDEN,), dtype=jnp.float32), 'Wk2': w(ks[7], HIDDEN, HIDDEN, scale_h), 'Wq2': w(ks[8], HIDDEN, HIDDEN, scale_h), 'Wv2': w(ks[9], HIDDEN, HIDDEN, scale_h), 'Ws2': w(ks[10], HIDDEN, HIDDEN, scale_h), 'b2': jnp.zeros((HIDDEN,), dtype=jnp.float32), 'Wl2': w(ks[11], HIDDEN, HIDDEN, scale_h), 'bl2': jnp.zeros((HIDDEN,), dtype=jnp.float32), 'edge_index': edge_index}
        return inp
    _L1_gnn_all = _L1_gnn_setup()
    _L1_gnn_in = {k: v for k, v in _L1_gnn_all.items() if k in ('Wk1', 'Wq1', 'Wv1', 'Ws1', 'b1', 'Wl1', 'bl1', 'Wk2', 'Wq2', 'Wv2', 'Ws2', 'b2', 'Wl2', 'bl2')}
    del _L1_gnn_all

    def _L2_gnn_setup():
        import jax, jax.numpy as jnp
        import numpy as np
        N, E, HID, KEY, EDGE, H = (100000, 25000, 64, 64, 16, 4)
        DK, DH = (KEY // H, HID // H)
        LOG2 = float(np.log(2.0))

        def ssp(x):
            return jax.nn.softplus(x) - LOG2
        key = jax.random.key(seed)
        ks = jax.random.split(key, 24)
        s = 0.05
        inp = {'node_attr': jax.random.normal(ks[0], (N, HID), jnp.float32), 'edge_index': jax.random.randint(ks[1], (2, E), 0, N, jnp.int64), 'edge_attr': jax.random.normal(ks[2], (E, EDGE), jnp.float32), 'Wk': jax.random.normal(ks[3], (H, DK, DH), jnp.float32) * s, 'Wq': jax.random.normal(ks[4], (H, DK, DH), jnp.float32) * s, 'Wv': jax.random.normal(ks[5], (H, DH, DH), jnp.float32) * s, 'wk1_w': jax.random.normal(ks[6], (EDGE, DK), jnp.float32) * s, 'wk1_b': jnp.zeros((DK,), jnp.float32), 'wk2_w': jax.random.normal(ks[7], (DK, DK), jnp.float32) * s, 'wk2_b': jnp.zeros((DK,), jnp.float32), 'wkl_w': jax.random.normal(ks[8], (DK, DK), jnp.float32) * s, 'wkl_b': jnp.zeros((DK,), jnp.float32), 'wv1_w': jax.random.normal(ks[9], (EDGE, DH), jnp.float32) * s, 'wv1_b': jnp.zeros((DH,), jnp.float32), 'wv2_w': jax.random.normal(ks[10], (DH, DH), jnp.float32) * s, 'wv2_b': jnp.zeros((DH,), jnp.float32), 'wvl_w': jax.random.normal(ks[11], (DH, DH), jnp.float32) * s, 'wvl_b': jnp.zeros((DH,), jnp.float32), 'cen_w': jax.random.normal(ks[12], (HID, HID), jnp.float32) * s, 'cen_b': jnp.zeros((HID,), jnp.float32), 'out_w': jax.random.normal(ks[13], (HID, HID), jnp.float32) * s, 'out_b': jnp.zeros((HID,), jnp.float32), 'ln_g': jnp.ones((HID,), jnp.float32), 'ln_b': jnp.zeros((HID,), jnp.float32)}
        return inp
    _L2_gnn_all = _L2_gnn_setup()
    _L2_gnn_in = {k: v for k, v in _L2_gnn_all.items() if k in ('Wk', 'Wq', 'Wv', 'wk1_w', 'wk1_b', 'wk2_w', 'wk2_b', 'wkl_w', 'wkl_b', 'wv1_w', 'wv1_b', 'wv2_w', 'wv2_b', 'wvl_w', 'wvl_b', 'cen_w', 'cen_b', 'out_w', 'out_b', 'ln_g', 'ln_b')}
    del _L2_gnn_all

    def _L3_gnn_setup():
        import jax, jax.numpy as jnp
        import numpy as np
        N_NODES = 100000
        N_EDGES = 25000
        IN_C, HID_C, OUT_C = (64, 64, 64)

        def _segment_softmax(w, dst, n):
            m = jax.ops.segment_max(w, dst, num_segments=n)
            e = jnp.exp(w - m[dst])
            s = jax.ops.segment_sum(e, dst, num_segments=n)
            return e / (s[dst] + 1e-16)

        def _wsage_conv(x, src, dst, ew, lin_w, lin_b, W):
            n = x.shape[0]
            w = _segment_softmax(ew, dst, n)
            h = x @ lin_w.T + lin_b
            msg = w[:, None] * h[src]
            agg = jax.ops.segment_sum(msg, dst, num_segments=n)
            cnt = jax.ops.segment_sum(jnp.ones_like(w), dst, num_segments=n)
            agg = agg / jnp.maximum(cnt, 1.0)[:, None]
            return agg @ W
        key = jax.random.key(seed)
        ks = jax.random.split(key, 10)
        x = jax.random.normal(ks[0], (N_NODES, IN_C), dtype=jnp.float32)
        src = jax.random.randint(ks[1], (N_EDGES,), 0, N_NODES)
        off = jax.random.randint(ks[2], (N_EDGES,), 1, N_NODES)
        dst = (src + off) % N_NODES
        edge_index = jnp.stack([src, dst], axis=0).astype(jnp.int64)
        edge_weight = jax.random.uniform(ks[3], (N_EDGES,), dtype=jnp.float32)

        def xavier(k, shape):
            fan_in, fan_out = (shape[1], shape[0])
            a = jnp.sqrt(6.0 / (fan_in + fan_out))
            return jax.random.uniform(k, shape, dtype=jnp.float32, minval=-a, maxval=a)
        return {'x': x, 'edge_index': edge_index, 'edge_weight': edge_weight, 'lin1_w': xavier(ks[4], (HID_C, IN_C)), 'lin1_b': jnp.zeros((HID_C,), jnp.float32), 'W1': xavier(ks[5], (HID_C, HID_C)), 'lin2_w': xavier(ks[6], (OUT_C, HID_C)), 'lin2_b': jnp.zeros((OUT_C,), jnp.float32), 'W2': xavier(ks[7], (OUT_C, OUT_C))}
    _L3_gnn_all = _L3_gnn_setup()
    _L3_gnn_in = {k: v for k, v in _L3_gnn_all.items() if k in ('lin1_w', 'lin1_b', 'W1', 'lin2_w', 'lin2_b', 'W2')}
    del _L3_gnn_all
    return {'x': x, 'src': src, 'dst': dst, 'edge_attr_16': edge_attr_16, 'edge_weight': edge_weight, 'edge_weight1': edge_weight1, 'L0_gnn_W_self': _L0_gnn_in['W_self'], 'L0_gnn_b_self': _L0_gnn_in['b_self'], 'L0_gnn_W_neigh': _L0_gnn_in['W_neigh'], 'L0_gnn_b_neigh': _L0_gnn_in['b_neigh'], 'L1_gnn_Wk1': _L1_gnn_in['Wk1'], 'L1_gnn_Wq1': _L1_gnn_in['Wq1'], 'L1_gnn_Wv1': _L1_gnn_in['Wv1'], 'L1_gnn_Ws1': _L1_gnn_in['Ws1'], 'L1_gnn_b1': _L1_gnn_in['b1'], 'L1_gnn_Wl1': _L1_gnn_in['Wl1'], 'L1_gnn_bl1': _L1_gnn_in['bl1'], 'L1_gnn_Wk2': _L1_gnn_in['Wk2'], 'L1_gnn_Wq2': _L1_gnn_in['Wq2'], 'L1_gnn_Wv2': _L1_gnn_in['Wv2'], 'L1_gnn_Ws2': _L1_gnn_in['Ws2'], 'L1_gnn_b2': _L1_gnn_in['b2'], 'L1_gnn_Wl2': _L1_gnn_in['Wl2'], 'L1_gnn_bl2': _L1_gnn_in['bl2'], 'L2_gnn_Wk': _L2_gnn_in['Wk'], 'L2_gnn_Wq': _L2_gnn_in['Wq'], 'L2_gnn_Wv': _L2_gnn_in['Wv'], 'L2_gnn_wk1_w': _L2_gnn_in['wk1_w'], 'L2_gnn_wk1_b': _L2_gnn_in['wk1_b'], 'L2_gnn_wk2_w': _L2_gnn_in['wk2_w'], 'L2_gnn_wk2_b': _L2_gnn_in['wk2_b'], 'L2_gnn_wkl_w': _L2_gnn_in['wkl_w'], 'L2_gnn_wkl_b': _L2_gnn_in['wkl_b'], 'L2_gnn_wv1_w': _L2_gnn_in['wv1_w'], 'L2_gnn_wv1_b': _L2_gnn_in['wv1_b'], 'L2_gnn_wv2_w': _L2_gnn_in['wv2_w'], 'L2_gnn_wv2_b': _L2_gnn_in['wv2_b'], 'L2_gnn_wvl_w': _L2_gnn_in['wvl_w'], 'L2_gnn_wvl_b': _L2_gnn_in['wvl_b'], 'L2_gnn_cen_w': _L2_gnn_in['cen_w'], 'L2_gnn_cen_b': _L2_gnn_in['cen_b'], 'L2_gnn_out_w': _L2_gnn_in['out_w'], 'L2_gnn_out_b': _L2_gnn_in['out_b'], 'L2_gnn_ln_g': _L2_gnn_in['ln_g'], 'L2_gnn_ln_b': _L2_gnn_in['ln_b'], 'L3_gnn_lin1_w': _L3_gnn_in['lin1_w'], 'L3_gnn_lin1_b': _L3_gnn_in['lin1_b'], 'L3_gnn_W1': _L3_gnn_in['W1'], 'L3_gnn_lin2_w': _L3_gnn_in['lin2_w'], 'L3_gnn_lin2_b': _L3_gnn_in['lin2_b'], 'L3_gnn_W2': _L3_gnn_in['W2']}

def reference(x, src, dst, edge_attr_16, edge_weight, edge_weight1, L0_gnn_W_self, L0_gnn_b_self, L0_gnn_W_neigh, L0_gnn_b_neigh, L1_gnn_Wk1, L1_gnn_Wq1, L1_gnn_Wv1, L1_gnn_Ws1, L1_gnn_b1, L1_gnn_Wl1, L1_gnn_bl1, L1_gnn_Wk2, L1_gnn_Wq2, L1_gnn_Wv2, L1_gnn_Ws2, L1_gnn_b2, L1_gnn_Wl2, L1_gnn_bl2, L2_gnn_Wk, L2_gnn_Wq, L2_gnn_Wv, L2_gnn_wk1_w, L2_gnn_wk1_b, L2_gnn_wk2_w, L2_gnn_wk2_b, L2_gnn_wkl_w, L2_gnn_wkl_b, L2_gnn_wv1_w, L2_gnn_wv1_b, L2_gnn_wv2_w, L2_gnn_wv2_b, L2_gnn_wvl_w, L2_gnn_wvl_b, L2_gnn_cen_w, L2_gnn_cen_b, L2_gnn_out_w, L2_gnn_out_b, L2_gnn_ln_g, L2_gnn_ln_b, L3_gnn_lin1_w, L3_gnn_lin1_b, L3_gnn_W1, L3_gnn_lin2_w, L3_gnn_lin2_b, L3_gnn_W2):
    import jax
    import jax.numpy as jnp

    def _L0_gnn_ref(feat, e_feat, src, dst, W_self, b_self, W_neigh, b_neigh):
        import jax, jax.numpy as jnp
        import numpy as np
        N_NODES = 100000
        N_EDGES = 25000
        IN_FEATS = 64
        OUT_FEATS = 64
        msg = feat[src] * e_feat
        neigh_sum = jax.ops.segment_sum(msg, dst, num_segments=N_NODES)
        deg = jax.ops.segment_sum(jnp.ones((msg.shape[0],), dtype=feat.dtype), dst, num_segments=N_NODES)
        h_neigh = neigh_sum / jnp.maximum(deg, 1.0)[:, None]
        rst = feat @ W_self.T + b_self + (h_neigh @ W_neigh.T + b_neigh)
        return rst

    def _L1_gnn_ref(x, Wk1, Wq1, Wv1, Ws1, b1, Wl1, bl1, Wk2, Wq2, Wv2, Ws2, b2, Wl2, bl2, edge_index):
        import jax, jax.numpy as jnp
        import numpy as np
        N_NODES = 100000
        N_EDGES = 25000
        D_IN = 64
        HIDDEN = 64

        def _res_gated_conv(x, Wk, Wq, Wv, Ws, b, src, dst, num_nodes):
            k = x @ Wk
            q = x @ Wq
            v = x @ Wv
            msg = jax.nn.sigmoid(k[dst] + q[src]) * v[src]
            agg = jax.ops.segment_sum(msg, dst, num_segments=num_nodes)
            return agg + x @ Ws + b
        src, dst = (edge_index[0], edge_index[1])
        n = x.shape[0]
        h = _res_gated_conv(x, Wk1, Wq1, Wv1, Ws1, b1, src, dst, n)
        h = jax.nn.relu(h @ Wl1 + bl1)
        h = _res_gated_conv(h, Wk2, Wq2, Wv2, Ws2, b2, src, dst, n)
        h = jax.nn.relu(h @ Wl2 + bl2)
        return h

    def _L2_gnn_ref(node_attr, edge_index, edge_attr, Wk, Wq, Wv, wk1_w, wk1_b, wk2_w, wk2_b, wkl_w, wkl_b, wv1_w, wv1_b, wv2_w, wv2_b, wvl_w, wvl_b, cen_w, cen_b, out_w, out_b, ln_g, ln_b):
        import jax, jax.numpy as jnp
        import numpy as np
        N, E, HID, KEY, EDGE, H = (100000, 25000, 64, 64, 16, 4)
        DK, DH = (KEY // H, HID // H)
        LOG2 = float(np.log(2.0))

        def ssp(x):
            return jax.nn.softplus(x) - LOG2
        row, col = (edge_index[0], edge_index[1])
        x = node_attr.reshape(N, H, DH)
        h_keys = jnp.einsum('nhd,hkd->nhk', x, Wk)
        h_queries = jnp.einsum('nhd,hkd->nhk', x, Wq)
        h_values = jnp.einsum('nhd,hvd->nhv', x, Wv)
        W_k = ssp(edge_attr @ wk1_w + wk1_b) @ wk2_w + wk2_b
        keys_j = W_k[:, None, :] * h_keys[col] @ wkl_w + wkl_b
        queries_i = h_queries[row]
        qk = jnp.sum(queries_i * keys_j, -1) / jnp.sqrt(jnp.float32(DK))
        seg_max = jax.ops.segment_max(qk, row, num_segments=N)
        ex = jnp.exp(qk - seg_max[row])
        seg_sum = jax.ops.segment_sum(ex, row, num_segments=N)
        alpha = ex / (seg_sum[row] + 1e-16)
        W_v = ssp(edge_attr @ wv1_w + wv1_b) @ wv2_w + wv2_b
        msg_j = W_v[:, None, :] * h_values[col] @ wvl_w + wvl_b
        msg_j = alpha[:, :, None] * msg_j
        aggr = jax.ops.segment_sum(msg_j, row, num_segments=N).reshape(N, HID)
        out = node_attr @ cen_w + cen_b + aggr
        out = ssp(out) @ out_w + out_b
        mu = jnp.mean(out, -1, keepdims=True)
        var = jnp.var(out, -1, keepdims=True)
        return (out - mu) / jnp.sqrt(var + 1e-05) * ln_g + ln_b

    def _L3_gnn_ref(x, edge_index, edge_weight, lin1_w, lin1_b, W1, lin2_w, lin2_b, W2):
        import jax, jax.numpy as jnp
        import numpy as np
        N_NODES = 100000
        N_EDGES = 25000
        IN_C, HID_C, OUT_C = (64, 64, 64)

        def _segment_softmax(w, dst, n):
            m = jax.ops.segment_max(w, dst, num_segments=n)
            e = jnp.exp(w - m[dst])
            s = jax.ops.segment_sum(e, dst, num_segments=n)
            return e / (s[dst] + 1e-16)

        def _wsage_conv(x, src, dst, ew, lin_w, lin_b, W):
            n = x.shape[0]
            w = _segment_softmax(ew, dst, n)
            h = x @ lin_w.T + lin_b
            msg = w[:, None] * h[src]
            agg = jax.ops.segment_sum(msg, dst, num_segments=n)
            cnt = jax.ops.segment_sum(jnp.ones_like(w), dst, num_segments=n)
            agg = agg / jnp.maximum(cnt, 1.0)[:, None]
            return agg @ W
        n = x.shape[0]
        loop = jnp.arange(n, dtype=edge_index.dtype)
        src = jnp.concatenate([edge_index[0], loop])
        dst = jnp.concatenate([edge_index[1], loop])
        ew = jnp.concatenate([edge_weight, jnp.ones((n,), edge_weight.dtype)])
        h = _wsage_conv(x, src, dst, ew, lin1_w, lin1_b, W1)
        h = jax.nn.relu(h)
        out = _wsage_conv(h, src, dst, ew, lin2_w, lin2_b, W2)
        return out
    edge_index = jnp.stack([src, dst])
    x = _layernorm(x + _L0_gnn_ref(x, edge_weight1, src, dst, L0_gnn_W_self, L0_gnn_b_self, L0_gnn_W_neigh, L0_gnn_b_neigh), axis=-1)
    x = _layernorm(x + _L1_gnn_ref(x, L1_gnn_Wk1, L1_gnn_Wq1, L1_gnn_Wv1, L1_gnn_Ws1, L1_gnn_b1, L1_gnn_Wl1, L1_gnn_bl1, L1_gnn_Wk2, L1_gnn_Wq2, L1_gnn_Wv2, L1_gnn_Ws2, L1_gnn_b2, L1_gnn_Wl2, L1_gnn_bl2, edge_index), axis=-1)
    x = _layernorm(x + _L2_gnn_ref(x, edge_index, edge_attr_16, L2_gnn_Wk, L2_gnn_Wq, L2_gnn_Wv, L2_gnn_wk1_w, L2_gnn_wk1_b, L2_gnn_wk2_w, L2_gnn_wk2_b, L2_gnn_wkl_w, L2_gnn_wkl_b, L2_gnn_wv1_w, L2_gnn_wv1_b, L2_gnn_wv2_w, L2_gnn_wv2_b, L2_gnn_wvl_w, L2_gnn_wvl_b, L2_gnn_cen_w, L2_gnn_cen_b, L2_gnn_out_w, L2_gnn_out_b, L2_gnn_ln_g, L2_gnn_ln_b), axis=-1)
    x = _layernorm(x + _L3_gnn_ref(x, edge_index, edge_weight, L3_gnn_lin1_w, L3_gnn_lin1_b, L3_gnn_W1, L3_gnn_lin2_w, L3_gnn_lin2_b, L3_gnn_W2), axis=-1)
    return x

_drawn_inputs = setup_inputs


def setup_inputs(seed=0):
    import zlib

    import numpy as np

    out = dict(_drawn_inputs(seed))
    spreads = {'L0_gnn_b_self': (0.0, 0.1),
     'L0_gnn_b_neigh': (0.0, 0.1),
     'L1_gnn_b1': (0.0, 0.1),
     'L1_gnn_bl1': (0.0, 0.1),
     'L1_gnn_b2': (0.0, 0.1),
     'L1_gnn_bl2': (0.0, 0.1),
     'L2_gnn_wk1_b': (0.0, 0.8),
     'L2_gnn_wk2_b': (0.0, 2.0),
     'L2_gnn_wkl_b': (0.0, 2.0),
     'L2_gnn_wv1_b': (0.0, 2.0),
     'L2_gnn_wv2_b': (0.0, 0.8),
     'L2_gnn_wvl_b': (0.0, 2.0),
     'L2_gnn_cen_b': (0.0, 0.1),
     'L2_gnn_out_b': (0.0, 0.1),
     'L2_gnn_ln_g': (1.0, 0.2),
     'L2_gnn_ln_b': (0.0, 0.1),
     'L3_gnn_lin1_b': (0.0, 0.1),
     'L3_gnn_lin2_b': (0.0, 0.1)}
    factors = {'edge_attr_16': 8.0,
     'edge_weight': 5.185,
     'L2_gnn_Wk': 8.0,
     'L2_gnn_Wq': 8.0,
     'L2_gnn_Wv': 8.0,
     'L2_gnn_wk1_w': 8.0,
     'L2_gnn_wk2_w': 8.0,
     'L2_gnn_wkl_w': 8.0,
     'L2_gnn_wv1_w': 8.0,
     'L2_gnn_wv2_w': 8.0,
     'L2_gnn_wvl_w': 8.0}
    for name, (base, spread) in spreads.items():
        noise = np.random.default_rng([zlib.crc32(name.encode()), seed]).standard_normal(out[name].shape)
        drawn = base * np.exp(spread * noise) if base else spread * noise
        out[name] = jnp.asarray(drawn.astype(out[name].dtype))
    for name, factor in factors.items():
        out[name] = (out[name] * factor).astype(out[name].dtype)
    return out
```

```python
from contextlib import ExitStack

import concourse.bass as bass
from concourse import mybir

P = 128
D = 64
G = 4
R = 8
CHUNK = P * R
H = 4
DH = D // H
EF = 16
SCRAP = 5 * P
BIG = float(2 ** 100)
LN_EPS = 1e-5
GT = 8

F32 = mybir.dt.float32
I32 = mybir.dt.int32
ALU = mybir.AluOpType
ACT = mybir.ActivationFunctionType
AX_X = mybir.AxisListType.X


def over_pairs(eng, count, body):
    assert count % 2 == 0 and count >= 8
    for n in (0, 1):
        body(n, 0, n, True, False)
    with eng.Fori(1, count // 2 - 2) as i:
        for s in (0, 1):
            body(i * 2 + s, i, s, False, False)
    for n in range(count - 4, count):
        body(n, n // 2, n % 2, False, n >= count - 2)


def hold(eng, passed):
    eng.sem_inc(passed, 1)


def last_use(i, s):
    return i + s


class Steps:

    def __init__(self, eng, sem, steps):
        self.eng, self.sem, self.steps = eng, sem, steps

    def turn(self, n):
        self.base, self.k = n * self.steps, 0

    def then(self, ins):
        self.k += 1
        ins.then_inc(self.sem, 1)
        self.eng.wait_ge(self.sem, self.base + self.k)

    def end(self):
        assert self.k == self.steps, (self.k, self.steps)


def bcast(ap, n):
    return ap.unsqueeze(2).broadcast_to([ap.shape[0], ap.shape[1], n])


def gnn_program(nc, a, out):
    N = a["x"].shape[0]
    E = a["src"].shape[0]
    TILES = -(-(-(-E // P)) // GT) * GT
    BLOCKS = TILES // G
    FULL, REST = E // TILES, E % TILES
    CHUNKS = -(-N // CHUNK)
    NT = N + SCRAP
    assert N >= CHUNK and NT * 2 < 2 ** 24

    def dram(name, shape):
        return nc.dram_tensor(name, shape, F32).ap()

    mean_tab = dram("mean_tab", [NT, 66])
    gate1_tab = dram("gate1_tab", [2 * NT, D])
    gate2_tab = dram("gate2_tab", [2 * NT, D])
    attn_x = dram("attn_x", [N, D])
    attn_tab = dram("attn_tab", [NT, 72])
    sage1_tab = dram("sage1_tab", [2 * NT, 65])
    sage2_tab = dram("sage2_tab", [2 * NT, 65])

    ctx = ExitStack()
    with ctx:
        def sb(name, shape, dt=F32):
            return ctx.enter_context(nc.sbuf_tensor(name, shape, dt))

        bank = [ctx.enter_context(nc.psum_tensor(f"bank{i}", [P, 512], F32)) for i in range(8)]

        ident = sb("ident", [P, P])
        earlier = sb("earlier", [P, G, G * P])
        scrap_row = sb("scrap_row", [P, G])
        src_g, dst_g = sb("src_g", [P, TILES], I32), sb("dst_g", [P, TILES], I32)
        src_g2, dst_g2 = sb("src_g2", [P, TILES], I32), sb("dst_g2", [P, TILES], I32)
        src_key, dst_key = sb("src_key", [P, TILES]), sb("dst_key", [P, TILES])
        src_put, dst_put = sb("src_put", [P, TILES], I32), sb("dst_put", [P, TILES], I32)
        dst_put2 = sb("dst_put2", [P, TILES], I32)
        w_mean, w_edge, w_exp = sb("w_mean", [P, TILES]), sb("w_edge", [P, TILES]), sb("w_exp", [P, TILES])
        w_one = sb("w_one", [P, TILES])
        edge_kv = sb("edge_kv", [P, TILES, 2 * EF])
        degree = sb("degree", [P, CHUNKS * R])
        self_exp = sb("self_exp", [P, CHUNKS * R])
        w_self = sb("w_self", [P, D])
        w_gate = [sb(f"w_gate{i}", [P, P]) for i in (1, 2)]
        w_mix = [sb(f"w_mix{i}", [P, D]) for i in (1, 2)]
        w_att = sb("w_att", [P, 196])
        w_att_out = sb("w_att_out", [P, D])
        w_out = sb("w_out", [D, D])
        w_sage = [sb(f"w_sage{i}", [D + 1, D]) for i in (1, 2)]
        rows = sb("rows", [P, 10, D])
        B_MEAN, B_MIX1, B_MIX2, B_CEN, B_VL, B_OUT, B_LNG, B_LNB, B_TMP, B_TMP2 = range(10)
        half, eps, minus_big = sb("half", [P, 1]), sb("eps", [P, 1]), sb("minus_big", [P, 1])
        st = dict(locals())

        prepare_weights(nc, a, st)
        prepare_edges(nc, a, st)

        mean_and_weight_max(nc, a, st)
        dense_mean(nc, a, st)
        gated_sums(nc, st, "g1", gate1_tab, w_gate[0])
        dense_gate(nc, st, "dg1", gate1_tab, 0, None, gate2_tab)
        gated_sums(nc, st, "g2", gate2_tab, w_gate[1])
        dense_gate(nc, st, "dg2", gate2_tab, 1, gate1_tab, attn_x)
        attention_sums(nc, st)
        dense_attention(nc, st)
        sage_sums(nc, st, "s1", sage1_tab)
        dense_sage(nc, st, "ds1", sage1_tab, 0, None, sage2_tab)
        sage_sums(nc, st, "s2", sage2_tab)
        dense_sage(nc, st, "ds2", sage2_tab, 1, sage1_tab, out)


class Phase:

    def __init__(self, nc, tag):
        self.nc, self.tag, self.ctx, self.all_sems = nc, tag, ExitStack(), []
        self.passed = self.sem("passed")

    def __enter__(self):
        return self

    def __exit__(self, *e):
        self.ctx.__exit__(*e)
        self.nc.clear_and_free_semaphores(self.all_sems)
        self.nc.all_engine_barrier()

    def sb(self, name, shape, dt=F32):
        return self.ctx.enter_context(self.nc.sbuf_tensor(f"{self.tag}_{name}", shape, dt))

    def sem(self, name):
        self.all_sems.append(self.nc.alloc_semaphore(f"{self.tag}_{name}"))
        return self.all_sems[-1]

    def sems(self, names):
        return [self.sem(n) for n in names.split()]


def prepare_weights(nc, a, st):
    ident, rows, bank = st["ident"], st["rows"], st["bank"]
    R_ = {k: st[k] for k in st if k.startswith("B_")}
    with Phase(nc, "pw") as ph:
        sem = ph.sem
        names = ["self", "neigh", "ws1", "wl1", "ws2", "wl2", "lin1", "w1", "lin2", "w2"]
        drams = ["L0_gnn_W_self", "L0_gnn_W_neigh", "L1_gnn_Ws1", "L1_gnn_Wl1", "L1_gnn_Ws2", "L1_gnn_Wl2",
                 "L3_gnn_lin1_w", "L3_gnn_W1", "L3_gnn_lin2_w", "L3_gnn_W2"]
        W = {n: ph.sb(n, [D, D]) for n in names}
        BQ, BK, BV, BWL, BVL = (ph.sb(n, [D, D]) for n in ("bq", "bk", "bv", "bwl", "bvl"))
        CR, OW = ph.sb("cr", [D, D]), ph.sb("ow", [D, D])
        SA = ph.sb("sa", [D, D])
        cols = ph.sb("cols", [D, 8])
        headc = ph.sb("headc", [D, H])
        loaded, zeroed, made, mm, ev, idz = (sem(n) for n in ("loaded", "zeroed", "made", "mm", "ev", "idz"))
        block = ph.ctx.enter_context(nc.Block())
        col_names = ["L1_gnn_b1", "L1_gnn_b2", "L3_gnn_lin1_b", "L3_gnn_lin2_b", "L2_gnn_out_b"]
        row_names = [("L0_gnn_b_self", R_["B_TMP"]), ("L0_gnn_b_neigh", R_["B_TMP2"]), ("L1_gnn_bl1", R_["B_MIX1"]),
                     ("L1_gnn_bl2", R_["B_MIX2"]), ("L2_gnn_cen_b", R_["B_CEN"]),
                     ("L2_gnn_ln_g", R_["B_LNG"]), ("L2_gnn_ln_b", R_["B_LNB"])]
        n_loads = [0]

        @block.sync
        def _(sp):
            def load(dst, src):
                sp.dma_start(dst, src).then_inc(loaded, 16)
                n_loads[0] += 16

            for n, d in zip(names, drams):
                load(W[n][:], a[d])
            for k, n in enumerate(col_names):
                load(cols[:, k:k + 1], a[n].unsqueeze(1))
            for n, k in row_names:
                load(rows[:, k, :], a[n].unsqueeze(0).broadcast_to([P, D]))
            for i in (1, 2):
                wg = st["w_gate"][i - 1]
                load(wg[0:D, 0:D], a[f"L1_gnn_Wk{i}"])
                load(wg[D:P, 0:D], a[f"L1_gnn_Wq{i}"])
                load(wg[D:P, D:P], a[f"L1_gnn_Wv{i}"])
            load(st["w_att_out"][0:D, :], a["L2_gnn_cen_w"])
            load(OW[:], a["L2_gnn_out_w"])
            sp.wait_ge(zeroed, 1)
            for h in range(H):
                o = slice(h * DH, (h + 1) * DH)
                load(BQ[o, o], a["L2_gnn_Wq"][h])
                load(BK[o, o], a["L2_gnn_Wk"][h])
                load(BV[o, o], a["L2_gnn_Wv"][h])
                load(BWL[o, o], a["L2_gnn_wkl_w"])
                load(BVL[o, o], a["L2_gnn_wvl_w"])
                load(headc[o, h:h + 1], a["L2_gnn_wkl_b"].unsqueeze(1))
                load(rows[:, R_["B_VL"], o], a["L2_gnn_wvl_b"].unsqueeze(0).broadcast_to([P, DH]))

        @block.gpsimd
        def _(pool):
            nc.gpsimd.memset(ident[:], 0.0).then_inc(idz, 1)
            pool.wait_ge(idz, 1)
            nc.gpsimd.affine_select(out=ident[:], in_=ident[:], compare_op=ALU.not_equal, fill=1.0, base=0,
                                    pattern=[[-1, P]], channel_multiplier=1).then_inc(idz, 1)

        evac = [0]

        @block.vector
        def _(dve):
            for t in (BQ[:], BK[:], BV[:], BWL[:], BVL[:], headc[:], st["w_gate"][0][0:D, D:P],
                      st["w_gate"][1][0:D, D:P], st["w_att"][:]):
                ins = nc.vector.memset(t, 0.0)
            nc.vector.memset(st["half"][:], 0.5)
            nc.vector.memset(st["eps"][:], LN_EPS)
            nc.vector.memset(st["minus_big"][:], -BIG)
            ins = nc.vector.memset(CR[:], -1.0 / D)
            ins.then_inc(zeroed, 1)
            dve.wait_ge(zeroed, 1)
            dve.wait_ge(idz, 2)
            dve.wait_ge(loaded, n_loads[0])
            nc.vector.tensor_tensor(CR[:], CR[:], ident[0:D, 0:D], ALU.add).then_inc(made, 1)
            nc.vector.tensor_tensor(rows[:, R_["B_TMP"], :], rows[:, R_["B_TMP"], :], rows[:, R_["B_TMP2"], :],
                                    ALU.add).then_inc(made, 1)
            dve.wait_ge(made, 2)
            nc.vector.reduce_sum(rows[:, R_["B_TMP2"], 0:1], rows[:, R_["B_TMP"], :], AX_X).then_inc(made, 1)
            dve.wait_ge(made, 3)
            nc.vector.tensor_scalar(rows[:, R_["B_TMP2"], 1:2], rows[:, R_["B_TMP2"], 0:1], -1.0 / D, None,
                                    ALU.mult).then_inc(made, 1)
            dve.wait_ge(made, 4)
            nc.vector.tensor_scalar(rows[:, R_["B_MEAN"], :], rows[:, R_["B_TMP"], :],
                                    rows[:, R_["B_TMP2"], 1:2], None, ALU.add).then_inc(made, 1)

            def take(dst, src, add=None, scale=None):
                evac[0] += 1
                dve.wait_ge(mm, evac[0])
                if add is not None:
                    ins = nc.vector.tensor_tensor(dst, src, add, ALU.add)
                elif scale is not None:
                    ins = nc.vector.tensor_scalar(dst, src, scale, None, ALU.mult)
                else:
                    ins = nc.vector.tensor_copy(dst, src)
                ins.then_inc(ev, 1)

            b = bank[0]
            take(SA[:], b[0:D, 0:D], add=ident[0:D, 0:D])
            take(st["w_self"][0:D, :], b[0:D, 0:D])
            take(st["w_self"][D:P, :], b[0:D, 0:D])
            for i in (0, 1):
                take(SA[:], b[0:D, 0:D])
                take(st["w_mix"][i][0:D, :], b[0:D, 0:D])
                take(st["w_mix"][i][D:P, :], b[0:D, 0:D])
                bi = R_["B_MIX1"] + i
                take(rows[:, bi, :], b[:, 0:D], add=rows[:, bi, :])
            for i in (0, 1):
                take(st["w_sage"][i][0:D, :], b[0:D, 0:D])
                take(st["w_sage"][i][D:D + 1, :], b[0:1, 0:D])
            take(SA[:], b[0:D, 0:D])
            take(st["w_att"][D:P, 0:D], b[0:D, 0:D], scale=0.25)
            take(st["w_att"][D:P, D:D + H], b[0:D, 0:H], scale=0.25)
            take(st["w_att"][0:D, D + H:2 * D + H], b[0:D, 0:D])
            take(st["w_att"][0:D, 2 * D + H:3 * D + H], b[0:D, 0:D])
            take(st["w_att_out"][D:P, :], b[0:D, 0:D])
            take(SA[:], b[0:D, 0:D])
            take(st["w_out"][:], b[0:D, 0:D])
            take(rows[:, R_["B_OUT"], :], b[:, 0:D])

        @block.tensor
        def _(pe):
            n = [0]
            b = bank[0]
            pe.wait_ge(made, 5)

            def mul(out, lhsT, rhs):
                if n[0]:
                    pe.wait_ge(ev, n[0])
                nc.tensor.matmul(out, lhsT, rhs, start=True, stop=True).then_inc(mm, 1)
                n[0] += 1

            idn = ident[0:D, 0:D]
            mul(b[0:D, 0:D], idn, W["self"][:])
            mul(b[0:D, 0:D], SA[:], CR[:])
            mul(b[0:D, 0:D], W["neigh"][:], CR[:])
            for i in (1, 2):
                mul(b[0:D, 0:D], W[f"ws{i}"][:], idn)
                mul(b[0:D, 0:D], SA[:], W[f"wl{i}"][:])
                mul(b[0:D, 0:D], idn, W[f"wl{i}"][:])
                mul(b[:, 0:D], cols[:, i - 1:i].broadcast_to([D, P]), W[f"wl{i}"][:])
            for i in (1, 2):
                mul(b[0:D, 0:D], W[f"lin{i}"][:], W[f"w{i}"][:])
                mul(b[:, 0:D], cols[:, i + 1:i + 2].broadcast_to([D, P]), W[f"w{i}"][:])
            mul(b[0:D, 0:D], BWL[:], idn)
            mul(b[0:D, 0:D], BQ[:], SA[:])
            mul(b[0:D, 0:H], BQ[:], headc[:])
            mul(b[0:D, 0:D], BK[:], idn)
            mul(b[0:D, 0:D], BV[:], idn)
            mul(b[0:D, 0:D], idn, BVL[:])
            mul(b[0:D, 0:D], OW[:], idn)
            mul(b[0:D, 0:D], SA[:], CR[:])
            mul(b[:, 0:D], cols[:, 4:5].broadcast_to([D, P]), CR[:])


def prepare_edges(nc, a, st):
    FULL, REST, BLOCKS, TILES, N, NT = (st[k] for k in ("FULL", "REST", "BLOCKS", "TILES", "N", "NT"))
    bank, ident, earlier = st["bank"], st["ident"], st["earlier"]
    with Phase(nc, "pe") as ph:
        sem = ph.sem
        src_i, dst_i = ph.sb("src_i", [P, TILES], I32), ph.sb("dst_i", [P, TILES], I32)
        iota_i = ph.sb("iota_i", [P, G], I32)
        ZR = 32
        init = ph.sb("init", [P, ZR, 72])
        init_m = ph.sb("init_m", [P, ZR, 66])
        cleared, loaded, masks, inited, stored = ph.sems("cleared loaded masks inited stored")
        block = ph.ctx.enter_context(nc.Block())
        n_loads = [0]

        @block.sync
        def _(sp):
            sp.wait_ge(cleared, 1)
            for dst, name in ((src_i, "src"), (st["src_g"], "src"), (dst_i, "dst"), (st["dst_g"], "dst"),
                              (st["w_mean"], "edge_weight1"), (st["w_edge"], "edge_weight")):
                v = a[name] if len(a[name].shape) == 1 else a[name].rearrange("e o -> (e o)")
                sp.dma_start(dst[0:FULL, :], v[0:FULL * TILES].rearrange("(p t) -> p t", t=TILES)).then_inc(loaded, 16)
                n_loads[0] += 16
                if REST:
                    sp.dma_start(dst[FULL:FULL + 1, 0:REST], v[FULL * TILES:E_of(a)].unsqueeze(0)).then_inc(loaded, 16)
                    n_loads[0] += 16

            sp.wait_ge(inited, 1)
            n = [0]

            def fill(tab, src, width, rows):
                per = rows // P
                body = tab[0:per * P].rearrange("(p r) w -> p (r w)", p=P)
                for r in range(0, per, ZR):
                    k = min(ZR, per - r)
                    sp.dma_start(body[:, r * width:(r + k) * width],
                                 src[:, 0:k, :].rearrange("p r w -> p (r w)")).then_inc(stored, 16)
                    n[0] += 16
                if rows > per * P:
                    sp.dma_start(tab[per * P:rows], src[0:rows - per * P, 0, :]).then_inc(stored, 16)
                    n[0] += 16

            fill(st["mean_tab"], init_m, 66, NT)
            fill(st["attn_tab"], init, 72, NT)
            for tab, width in ((st["gate1_tab"], D), (st["gate2_tab"], D), (st["sage1_tab"], 65),
                               (st["sage2_tab"], 65)):
                v = tab[2 * N:2 * NT].rearrange("(p r) w -> p r w", p=P)
                sp.dma_start(v, init[:, 0:2 * SCRAP // P, 0:width]).then_inc(stored, 16)
                n[0] += 16
            sp.wait_ge(stored, n[0])

        @block.gpsimd
        def _(pool):
            nc.gpsimd.memset(earlier[:], 1.0).then_inc(masks, 1)
            nc.gpsimd.iota(iota_i[:], pattern=[[P, G]], base=N, channel_multiplier=1).then_inc(masks, 1)
            pool.wait_ge(masks, 1)
            for q in range(G):
                nc.gpsimd.affine_select(out=earlier[:, q, :], in_=earlier[:, q, :], compare_op=ALU.is_gt,
                                        fill=0.0, base=q * P, pattern=[[-1, G * P]],
                                        channel_multiplier=1).then_inc(masks, 1)

        @block.vector
        def _(dve):
            for t, v in ((src_i, N + G * P), (dst_i, N + G * P), (st["src_g"], 0), (st["dst_g"], 0),
                         (st["w_mean"], 0.0), (st["w_edge"], 0.0)):
                ins = nc.vector.memset(t[:], v)
            nc.vector.memset(st["w_one"][:], 1.0)
            ins = nc.vector.memset(init[:], 0.0)
            ins.then_inc(cleared, 1)
            dve.wait_ge(cleared, 1)
            nc.vector.memset(init[:, :, 68:72], -BIG)
            nc.vector.memset(init_m[:, :, 0:65], 0.0)
            nc.vector.memset(init_m[:, :, 65:66], 1.0).then_inc(inited, 1)
            dve.wait_ge(loaded, n_loads[0])
            dve.wait_ge(masks, 2)
            nc.vector.tensor_copy(st["scrap_row"][:], iota_i[:])
            nc.vector.tensor_copy(st["src_key"][:], src_i[:])
            nc.vector.tensor_copy(st["dst_key"][:], dst_i[:])
            nc.vector.tensor_scalar(st["src_g2"][:], st["src_g"][:], 2.0, None, ALU.mult)
            nc.vector.tensor_scalar(st["dst_g2"][:], st["dst_g"][:], 2.0, None, ALU.mult)


def E_of(a):
    return a["src"].shape[0]


class Blocks:

    def __init__(self, nc, ph, st, key, width):
        self.nc, self.st, self.key, self.width = nc, st, key, width
        self.keys = [ph.sb(f"keys{s}", [P, G]) for s in (0, 1)]
        self.match = [ph.sb(f"match{s}", [P, G, G * P]) for s in (0, 1)]
        self.payload = [ph.sb(f"payload{s}", [P, G, width]) for s in (0, 1)]

    def turn_keys(self, bank, s):
        for q in range(G):
            ins = self.nc.tensor.transpose(bank[:, q * P:(q + 1) * P],
                                           self.keys[s][:, q:q + 1].broadcast_to([P, P]), self.st["ident"][:])
        return ins

    def make_match(self, bank, s):
        for q in range(G):
            ins = self.nc.vector.tensor_scalar(self.match[s][:, q, :], bank[:], self.keys[s][:, q:q + 1], None,
                                               ALU.is_equal)
        return ins

    def segment_sums(self, bank, s):
        w = self.width
        for u in range(G):
            for t in range(G):
                ins = self.nc.tensor.matmul(bank[:, u * w:(u + 1) * w], self.match[s][:, t, u * P:(u + 1) * P],
                                            self.payload[s][:, t, :], start=(t == 0), stop=(t == G - 1))
        return ins

    def stage(self, n, s, copies):
        cols = bass.ds(n * G, G)
        ins = self.nc.vector.tensor_copy(self.keys[s][:], self.key[:, cols])
        for dst, src in copies:
            ins = self.nc.vector.tensor_copy(dst[:], src[:, cols])
        return ins


class Leaders:

    def __init__(self, nc, ph, st, tag):
        self.nc, self.st = nc, st
        self.before, self.lead, self.diff = (ph.sb(f"{tag}_{n}", [P, G]) for n in ("before", "lead", "diff"))
        self.junk = ph.sb(f"{tag}_junk", [P, G, G * P])

    STEPS = 4

    def find(self, steps, match, keys, outs):
        nc, scrap = self.nc, self.st["scrap_row"]
        for q in range(G):
            w = (q + 1) * P
            ins = nc.vector.tensor_tensor_reduce(self.junk[:, q, 0:w], match[:, q, 0:w], self.st["earlier"][:, q, 0:w],
                                                 1.0, 0.0, ALU.mult, ALU.add, self.before[:, q:q + 1])
        steps.then(ins)
        steps.then(nc.vector.tensor_scalar(self.lead[:], self.before[:], 0.0, None, ALU.is_equal))
        steps.then(nc.vector.tensor_tensor(self.diff[:], keys[:], scrap[:], ALU.subtract))
        steps.then(nc.vector.tensor_tensor(self.diff[:], self.diff[:], self.lead[:], ALU.mult))
        for dst in outs:
            ins = nc.vector.tensor_tensor(dst, self.diff[:], scrap[:], ALU.add)
        return ins


def gather_rows(nc, out_cols, table, index, sem, passed):
    hold(nc.gpsimd, passed)
    for dst, q in out_cols:
        nc.gpsimd.indirect_dma_start(dst, None, table, bass.IndirectOffsetOnAxis(ap=index[:, q:q + 1], axis=0)
                                     ).then_inc(sem, 16)


def mean_and_weight_max(nc, a, st):
    BLOCKS, bank, x = st["BLOCKS"], st["bank"], a["x"]
    with Phase(nc, "mean") as ph:
        bl = Blocks(nc, ph, st, st["dst_key"], 65)
        ld = Leaders(nc, ph, st, "dst")
        xs = [ph.sb(f"xs{s}", [P, G, D]) for s in (0, 1)]
        state, new = ([ph.sb(f"{n}{s}", [P, G, 66]) for s in (0, 1)] for n in ("state", "new"))
        weight = [ph.sb(f"weight{s}", [P, G]) for s in (0, 1)]
        src_i, dst_i, put_i = ([ph.sb(f"{n}{s}", [P, G], I32) for s in (0, 1)] for n in ("src_i", "dst_i", "put_i"))
        top, junk = ph.sb("top", [P, G]), ph.sb("junk", [P, G, G * P])
        staged, turned, matched, paid, summed, topped, updated, chain = ph.sems(
            "staged turned matched paid summed topped updated chain")
        gathered, state_in, scattered = ([ph.sem(f"{n}{s}") for s in (0, 1)] for n in
                                         ("gathered", "state_in", "scattered"))
        mlp = EdgeMlp(nc, a, ph, st)
        block = ph.ctx.enter_context(nc.Block())
        key_t, weight_t, sums = bank[0:2], bank[2:4], bank[4:6]

        @block.sync
        def _(sp):
            mlp.load(sp)

        @block.gpsimd
        def _(pool):
            def x_rows(i, s, part):
                gather_rows(nc, [(xs[s][:, q, :], q) for q in part], x, src_i[s], gathered[s], ph.passed)

            def step(n, i, s, first, last):
                more = not (last and s == 1)
                if more:
                    pool.wait_ge(staged, n + 2)
                    if not n_is(n, 0, first):
                        pool.wait_ge(paid, n)
                    x_rows(i, 1 - s, (0, 1))
                if not (first and s == 0):
                    pool.wait_ge(scattered[1 - s], 64 * last_use(i, s))
                gather_rows(nc, [(state[s][:, q, :], q) for q in range(G)], st["mean_tab"], dst_i[s], state_in[s], ph.passed)
                if more:
                    x_rows(i, 1 - s, (2, 3))
                pool.wait_ge(updated, n + 1)
                hold(pool, ph.passed)
                for q in range(G):
                    nc.gpsimd.indirect_dma_start(
                        st["mean_tab"], bass.IndirectOffsetOnAxis(ap=put_i[s][:, q:q + 1], axis=0),
                        new[s][:, q, :], None).then_inc(scattered[s], 16)

            pool.wait_ge(staged, 1)
            x_rows(0, 0, range(G))
            over_pairs(pool, BLOCKS, step)
            for s in (0, 1):
                pool.wait_ge(scattered[s], 64 * (BLOCKS // 2))

        @block.vector
        def _(dve):
            steps = Steps(dve, chain, Leaders.STEPS)

            def stage(n, s):
                bl.stage(n, s, ((weight[s], st["w_edge"]), (src_i[s], st["src_g"]), (dst_i[s], st["dst_g"]))
                         ).then_inc(staged, 1)

            def step(n, i, s, first, last):
                steps.turn(n)
                dve.wait_ge(turned, n + 1)
                if not first:
                    dve.wait_ge(summed, n - 1)
                bl.make_match(key_t[s], s).then_inc(matched, 1)
                dve.wait_ge(gathered[s], 64 * (i + 1))
                nc.vector.tensor_tensor(bl.payload[s][:, :, 0:D], xs[s][:],
                                        bcast(st["w_mean"][:, bass.ds(n * G, G)], D), ALU.mult).then_inc(paid, 1)
                dve.wait_ge(matched, n + 1)
                hold(dve, ph.passed)
                for q in range(G):
                    ins = nc.vector.tensor_tensor_reduce(junk[:, q, :], bl.match[s][:, q, :], weight_t[s][:], 1.0, 1.0,
                                                         ALU.mult, ALU.max, top[:, q:q + 1])
                ins.then_inc(topped, 1)
                if not first:
                    dve.wait_ge(scattered[s], 64 * i)
                ld.find(steps, bl.match[s], bl.keys[s], (
                    put_i[s][:], st["dst_put"][:, bass.ds(n * G, G)]))
                steps.end()
                mlp.vector(dve, i, s, first)
                dve.wait_ge(summed, n + 1)
                dve.wait_ge(state_in[s], 64 * (i + 1))
                dve.wait_ge(topped, n + 1)
                nc.vector.tensor_tensor(new[s][:, :, 0:65], sums[s][:, 0:G * 65].rearrange("p (t w) -> p t w", w=65),
                                        state[s][:, :, 0:65], ALU.add)
                nc.vector.tensor_tensor(new[s][:, :, 65], state[s][:, :, 65], top[:], ALU.max).then_inc(updated, 1)
                if not last:
                    stage(n + 2, s)

            mlp.clear(dve)
            for s in (0, 1):
                nc.vector.memset(bl.payload[s][:], 1.0)
                stage(s, s)
            over_pairs(dve, BLOCKS, step)
            mlp.last_keep(dve)
            nc.vector.tensor_scalar(st["dst_put2"][:], st["dst_put"][:], 2.0, 1.0, ALU.mult, ALU.add)

        @block.scalar
        def _(act):
            act.preload_act_table_set("natural_log_exp_and_others")

            def step(n, i, s, first, last):
                mlp.scalar(act, i, s, first)

            over_pairs(act, BLOCKS, step)

        @block.tensor
        def _(pe):
            def turn(n, s):
                pe.wait_ge(staged, n + 1)
                bl.turn_keys(key_t[s], s)
                for q in range(G):
                    ins = nc.tensor.transpose(weight_t[s][:, q * P:(q + 1) * P],
                                              weight[s][:, q:q + 1].broadcast_to([P, P]), st["ident"][:])
                ins.then_inc(turned, 1)

            def step(n, i, s, first, last):
                if not (last and s == 1):
                    turn(n + 1, 1 - s)
                mlp.tensor_before(pe, i, s, first)
                pe.wait_ge(matched, n + 1)
                pe.wait_ge(paid, n + 1)
                if not first:
                    pe.wait_ge(updated, n - 1)
                bl.segment_sums(sums[s], s).then_inc(summed, 1)
                mlp.tensor_after(pe, i, s, first)

            turn(0, 0)
            over_pairs(pe, BLOCKS, step)


def n_is(n, value, first):
    return first and n == value


class EdgeMlp:

    def __init__(self, nc, a, ph, st):
        self.nc, self.a, self.st = nc, a, st
        assert GT == 2 * G
        self.attr = ph.sb("attr", [P, st["TILES"] * EF])
        self.w1, self.w2 = ph.sb("mlp_w1", [P, 2, P]), ph.sb("mlp_w2", [P, 2, P])
        self.b1, self.b2 = ph.sb("mlp_b1", [P, 2]), ph.sb("mlp_b2", [P, GT, 2, EF])
        self.stage_t, self.attr_t = ph.sb("mlp_stage", [P, P]), ph.sb("mlp_attr_t", [P, P])
        self.z, self.e, self.soft = (ph.sb(f"mlp_{n}", [P, 2, P]) for n in ("z", "e", "soft"))
        (self.cleared, self.loaded, self.staged, self.turned, self.copied, self.first_mm, self.z_done, self.ln_done,
         self.soft_done, self.second_mm, self.kept, self.chain) = ph.sems(
            "mcleared mloaded mstaged mturned mcopied mfirst_mm mz_done mln_done msoft_done msecond_mm mkept mchain")
        self.loads = 0

    def load(self, sp):
        st, a = self.st, self.a
        FULL, REST, TILES = st["FULL"], st["REST"], st["TILES"]

        def load(dst, src):
            sp.dma_start(dst, src).then_inc(self.loaded, 16)
            self.loads += 16

        sp.wait_ge(self.cleared, 1)
        v = a["edge_attr_16"]
        load(self.attr[0:FULL, :], v[0:FULL * TILES].rearrange("(p t) f -> p (t f)", t=TILES))
        if REST:
            load(self.attr[FULL:FULL + 1, 0:REST * EF], v[FULL * TILES:E_of(a)].rearrange("(o t) f -> o (t f)", o=1))
        for t in range(GT):
            o = slice(t * EF, (t + 1) * EF)
            for k, n in ((0, "k"), (1, "v")):
                load(self.w1[o, k, o], a[f"L2_gnn_w{n}1_w"])
                load(self.w2[o, k, o], a[f"L2_gnn_w{n}2_w"])
                load(self.b1[o, k:k + 1], a[f"L2_gnn_w{n}1_b"].unsqueeze(1))
                load(self.b2[:, t, k, :], a[f"L2_gnn_w{n}2_b"].unsqueeze(0).broadcast_to([P, EF]))

    def clear(self, dve):
        nc = self.nc
        nc.vector.memset(self.w1[:], 0.0)
        nc.vector.memset(self.w2[:], 0.0)
        nc.vector.memset(self.attr[:], 0.0).then_inc(self.cleared, 1)

    def vector(self, dve, g, s, first):
        nc, bank = self.nc, self.st["bank"]
        if s == 0:
            if first:
                dve.wait_ge(self.loaded, self.loads)
            else:
                dve.wait_ge(self.turned, g)
            nc.vector.tensor_copy(self.stage_t[:], self.attr[:, bass.ds(g * P, P)]).then_inc(self.staged, 1)
            if not first:
                dve.wait_ge(self.second_mm, g)
                self.keep(g - 1)
        else:
            dve.wait_ge(self.ln_done, g + 1)
            nc.vector.scalar_tensor_tensor(out=self.soft[:], in0=self.z[:], scalar=0.0, in1=self.e[:], op0=ALU.max,
                                           op1=ALU.add).then_inc(self.soft_done, 1)

    def keep(self, g):
        bank = self.st["bank"][6]
        for k in (0, 1):
            ins = self.nc.vector.tensor_tensor(
                self.st["edge_kv"][:, bass.ds(g * GT, GT), k * EF:(k + 1) * EF],
                bank[:, k * P:(k + 1) * P].rearrange("p (t f) -> p t f", f=EF), self.b2[:, :, k, :], ALU.add)
        ins.then_inc(self.kept, 1)

    def scalar(self, act, g, s, first):
        nc, bank = self.nc, self.st["bank"]
        if s == 0:
            act.wait_ge(self.turned, g + 1)
            nc.scalar.activation(self.attr_t[:], bank[7][:, 2 * P:3 * P], ACT.Copy).then_inc(self.copied, 1)
        else:
            act.wait_ge(self.first_mm, g + 1)
            if not first:
                act.wait_ge(self.soft_done, g)
            for k in (0, 1):
                ins = nc.scalar.activation(self.z[:, k, :], bank[7][:, k * P:(k + 1) * P], ACT.Identity,
                                           bias=self.b1[:, k:k + 1])
            ins.then_inc(self.z_done, 1)
            act.wait_ge(self.z_done, g + 1)
            nc.scalar.activation(self.e[:], self.z[:], ACT.Abs).then_inc(self.chain, 1)
            act.wait_ge(self.chain, g * 2 + 1)
            nc.scalar.activation(self.e[:], self.e[:], ACT.Exp, scale=-1.0).then_inc(self.chain, 1)
            act.wait_ge(self.chain, g * 2 + 2)
            nc.scalar.activation(self.e[:], self.e[:], ACT.Ln, bias=self.st["half"][:], scale=0.5
                                 ).then_inc(self.ln_done, 1)

    def tensor_before(self, pe, g, s, first):
        nc, bank = self.nc, self.st["bank"]
        if s == 0:
            pe.wait_ge(self.staged, g + 1)
            if not first:
                pe.wait_ge(self.z_done, g)
            nc.tensor.transpose(bank[7][:, 2 * P:3 * P], self.stage_t[:], self.st["ident"][:]).then_inc(self.turned, 1)

    def tensor_after(self, pe, g, s, first):
        nc, bank = self.nc, self.st["bank"]
        if s == 0:
            pe.wait_ge(self.copied, g + 1)
            for k in (0, 1):
                ins = nc.tensor.matmul(bank[7][:, k * P:(k + 1) * P], self.w1[:, k, :], self.attr_t[:], start=True,
                                       stop=True)
            ins.then_inc(self.first_mm, 1)
        else:
            pe.wait_ge(self.soft_done, g + 1)
            if not first:
                pe.wait_ge(self.kept, g)
            for k in (0, 1):
                ins = nc.tensor.matmul(bank[6][:, k * P:(k + 1) * P], self.soft[:, k, :], self.w2[:, k, :], start=True,
                                       stop=True)
            ins.then_inc(self.second_mm, 1)

    def last_keep(self, dve):
        dve.wait_ge(self.second_mm, self.st["BLOCKS"] // 2)
        self.keep(self.st["BLOCKS"] // 2 - 1)


def gated_sums(nc, st, tag, table, weight):
    BLOCKS, bank, ident = st["BLOCKS"], st["bank"], st["ident"]
    lead = tag == "g1"
    with Phase(nc, tag) as ph:
        bl = Blocks(nc, ph, st, st["dst_key"], D)
        ends = [ph.sb(f"ends{s}", [P, G, P]) for s in (0, 1)]
        ends_t = [ph.sb(f"ends_t{s}", [P, G * P]) for s in (0, 1)]
        gate = [ph.sb(f"gate{s}", [P, G, D]) for s in (0, 1)]
        sums_sb = [ph.sb(f"sums_sb{s}", [P, G * D]) for s in (0, 1)]
        src_i, dst_i, put_i = ([ph.sb(f"{n}{s}", [P, G], I32) for s in (0, 1)] for n in ("src_i", "dst_i", "put_i"))
        (staged, turned, matched, ends_turned, ends_copied, produced, gated, paid, summed, copied) = ph.sems(
            "staged turned matched ends_turned ends_copied produced gated paid summed copied")
        gathered, scattered = ([ph.sem(f"{n}{s}") for s in (0, 1)] for n in ("gathered", "scattered"))
        key_t, ends_b, kqv_b, sums = bank[0:2], bank[2], bank[3:5], bank[5:7]
        if lead:
            src_keys = ph.sb("src_keys", [P, G])
            src_match = ph.sb("src_match", [P, G, G * P])
            ld = Leaders(nc, ph, st, "src")
            src_staged, src_turned, chain = ph.sems("src_staged src_turned chain")
        block = ph.ctx.enter_context(nc.Block())

        @block.gpsimd
        def _(pool):
            def rows_of(s):
                gather_rows(nc, [(ends[s][:, q, 0:D], q) for q in range(G)], table, dst_i[s], gathered[s], ph.passed)
                gather_rows(nc, [(ends[s][:, q, D:P], q) for q in range(G)], table, src_i[s], gathered[s], ph.passed)

            def step(n, i, s, first, last):
                if not (last and s == 1):
                    pool.wait_ge(staged, n + 2)
                    if not n_is(n, 0, first):
                        pool.wait_ge(ends_turned, n)
                    rows_of(1 - s)
                pool.wait_ge(copied, n + 1)
                if not (first and s == 0):
                    pool.wait_ge(scattered[1 - s], 64 * last_use(i, s))
                hold(pool, ph.passed)
                for q in range(G):
                    nc.gpsimd.indirect_dma_start(
                        table, bass.IndirectOffsetOnAxis(ap=put_i[s][:, q:q + 1], axis=0),
                        sums_sb[s][:, q * D:(q + 1) * D], None, compute_op=ALU.add).then_inc(scattered[s], 16)

            pool.wait_ge(staged, 1)
            rows_of(0)
            over_pairs(pool, BLOCKS, step)
            for s in (0, 1):
                pool.wait_ge(scattered[s], 64 * (BLOCKS // 2))

        @block.vector
        def _(dve):
            if lead:
                steps = Steps(dve, chain, Leaders.STEPS + 1)

            def stage(n, s):
                bl.stage(n, s, ((src_i[s], st["src_g2"]), (dst_i[s], st["dst_g2"]))).then_inc(staged, 1)

            def step(n, i, s, first, last):
                dve.wait_ge(turned, n + 1)
                if not first:
                    dve.wait_ge(summed, n - 1)
                bl.make_match(key_t[s], s).then_inc(matched, 1)
                dve.wait_ge(gated, n + 1)
                nc.vector.tensor_tensor(bl.payload[s][:], gate[s][:],
                                        kqv_b[s][:].rearrange("p (t w) -> p t w", w=P)[:, :, D:P], ALU.mult
                                        ).then_inc(paid, 1)
                if lead:
                    steps.turn(n)
                    dve.wait_ge(src_turned, n + 1)
                    for q in range(G):
                        w = (q + 1) * P
                        ins = nc.vector.tensor_scalar(src_match[:, q, 0:w], bank[7][:, 0:w], src_keys[:, q:q + 1],
                                                      None, ALU.is_equal)
                    steps.then(ins)
                    ld.find(steps, src_match, src_keys, (st["src_put"][:, bass.ds(n * G, G)],))
                    steps.end()
                    if not (last and s == 1):
                        nc.vector.tensor_copy(src_keys[:], st["src_key"][:, bass.ds(n * G + G, G)]
                                              ).then_inc(src_staged, 1)
                if not last:
                    dve.wait_ge(matched, n + 1)
                    stage(n + 2, s)

            if lead:
                nc.vector.tensor_copy(src_keys[:], st["src_key"][:, 0:G]).then_inc(src_staged, 1)
            for s in (0, 1):
                stage(s, s)
            over_pairs(dve, BLOCKS, step)

        @block.scalar
        def _(act):
            def step(n, i, s, first, last):
                act.wait_ge(ends_turned, n + 1)
                if not first:
                    act.wait_ge(produced, n - 1)
                nc.scalar.activation(ends_t[s][:], ends_b[:], ACT.Copy).then_inc(ends_copied, 1)
                act.wait_ge(produced, n + 1)
                if not first:
                    act.wait_ge(paid, n - 1)
                nc.scalar.activation(gate[s][:], kqv_b[s][:].rearrange("p (t w) -> p t w", w=P)[:, :, 0:D],
                                     ACT.Sigmoid).then_inc(gated, 1)
                act.wait_ge(summed, n + 1)
                if not first:
                    act.wait_ge(scattered[s], 64 * i)
                nc.scalar.activation(put_i[s][:], st["dst_put2"][:, bass.ds(n * G, G)], ACT.Copy)
                nc.scalar.activation(sums_sb[s][:], sums[s][:, 0:G * D], ACT.Copy).then_inc(copied, 1)

            over_pairs(act, BLOCKS, step)

        @block.tensor
        def _(pe):
            def turn(n, s):
                pe.wait_ge(staged, n + 1)
                bl.turn_keys(key_t[s], s).then_inc(turned, 1)

            def step(n, i, s, first, last):
                if not (last and s == 1):
                    turn(n + 1, 1 - s)
                pe.wait_ge(gathered[s], 128 * (i + 1))
                if not n_is(n, 0, first):
                    pe.wait_ge(ends_copied, n)
                for q in range(G):
                    ins = nc.tensor.transpose(ends_b[:, q * P:(q + 1) * P], ends[s][:, q, :], ident[:])
                ins.then_inc(ends_turned, 1)
                pe.wait_ge(ends_copied, n + 1)
                if not first:
                    pe.wait_ge(paid, n - 1)
                for q in range(G):
                    ins = nc.tensor.matmul(kqv_b[s][:, q * P:(q + 1) * P], ends_t[s][:, q * P:(q + 1) * P], weight[:],
                                           start=True, stop=True)
                ins.then_inc(produced, 1)
                if lead:
                    pe.wait_ge(src_staged, n + 1)
                    for q in range(G):
                        ins = nc.tensor.transpose(bank[7][:, q * P:(q + 1) * P],
                                                  src_keys[:, q:q + 1].broadcast_to([P, P]), ident[:])
                    ins.then_inc(src_turned, 1)
                pe.wait_ge(matched, n + 1)
                pe.wait_ge(paid, n + 1)
                if not first:
                    pe.wait_ge(copied, n - 1)
                bl.segment_sums(sums[s], s).then_inc(summed, 1)

            turn(0, 0)
            over_pairs(pe, BLOCKS, step)


def sage_sums(nc, st, tag, table):
    BLOCKS, bank = st["BLOCKS"], st["bank"]
    W = D + 1
    with Phase(nc, tag) as ph:
        bl = Blocks(nc, ph, st, st["dst_key"], W)
        xs = [ph.sb(f"xs{s}", [P, G, W]) for s in (0, 1)]
        sums_sb = [ph.sb(f"sums_sb{s}", [P, G * W]) for s in (0, 1)]
        src_i, put_i = ([ph.sb(f"{n}{s}", [P, G], I32) for s in (0, 1)] for n in ("src_i", "put_i"))
        staged, turned, matched, paid, summed, copied = ph.sems("staged turned matched paid summed copied")
        gathered, scattered = ([ph.sem(f"{n}{s}") for s in (0, 1)] for n in ("gathered", "scattered"))
        key_t, sums = bank[0:2], bank[2:4]
        block = ph.ctx.enter_context(nc.Block())

        @block.gpsimd
        def _(pool):
            def rows_of(s):
                gather_rows(nc, [(xs[s][:, q, :], q) for q in range(G)], table, src_i[s], gathered[s], ph.passed)

            def step(n, i, s, first, last):
                if not last:
                    pool.wait_ge(staged, n + 3)
                pool.wait_ge(copied, n + 1)
                if not (first and s == 0):
                    pool.wait_ge(scattered[1 - s], 64 * last_use(i, s))
                hold(pool, ph.passed)
                for q in range(G):
                    nc.gpsimd.indirect_dma_start(
                        table, bass.IndirectOffsetOnAxis(ap=put_i[s][:, q:q + 1], axis=0),
                        sums_sb[s][:, q * W:(q + 1) * W], None, compute_op=ALU.add).then_inc(scattered[s], 16)
                if not last:
                    rows_of(s)

            for s in (0, 1):
                pool.wait_ge(staged, s + 1)
                rows_of(s)
            over_pairs(pool, BLOCKS, step)
            for s in (0, 1):
                pool.wait_ge(scattered[s], 64 * (BLOCKS // 2))

        @block.vector
        def _(dve):
            def stage(n, s):
                bl.stage(n, s, ((src_i[s], st["src_g2"]),)).then_inc(staged, 1)

            def step(n, i, s, first, last):
                w = st["w_exp"][:, bass.ds(n * G, G)]
                dve.wait_ge(turned, n + 1)
                if not first:
                    dve.wait_ge(summed, n - 1)
                bl.make_match(key_t[s], s).then_inc(matched, 1)
                dve.wait_ge(gathered[s], 64 * (i + 1))
                nc.vector.tensor_copy(bl.payload[s][:, :, D], w)
                nc.vector.tensor_tensor(bl.payload[s][:, :, 0:D], xs[s][:, :, 0:D], bcast(w, D), ALU.mult
                                        ).then_inc(paid, 1)
                if not last:
                    dve.wait_ge(matched, n + 1)
                    dve.wait_ge(paid, n + 1)
                    stage(n + 2, s)

            for s in (0, 1):
                stage(s, s)
            over_pairs(dve, BLOCKS, step)

        @block.scalar
        def _(act):
            def step(n, i, s, first, last):
                act.wait_ge(summed, n + 1)
                if not first:
                    act.wait_ge(scattered[s], 64 * i)
                nc.scalar.activation(put_i[s][:], st["dst_put2"][:, bass.ds(n * G, G)], ACT.Copy)
                nc.scalar.activation(sums_sb[s][:], sums[s][:, 0:G * W], ACT.Copy).then_inc(copied, 1)

            over_pairs(act, BLOCKS, step)

        @block.tensor
        def _(pe):
            def turn(n, s):
                pe.wait_ge(staged, n + 1)
                bl.turn_keys(key_t[s], s).then_inc(turned, 1)

            def step(n, i, s, first, last):
                if not (last and s == 1):
                    turn(n + 1, 1 - s)
                pe.wait_ge(matched, n + 1)
                pe.wait_ge(paid, n + 1)
                if not first:
                    pe.wait_ge(copied, n - 1)
                bl.segment_sums(sums[s], s).then_inc(summed, 1)

            turn(0, 0)
            over_pairs(pe, BLOCKS, step)


def first_node(st, n):
    return min(n * CHUNK, st["N"] - CHUNK) if isinstance(n, int) else n * CHUNK


def load_and_store(sp, st, load, store, outs_ready, used, stored):
    CHUNKS = st["CHUNKS"]

    def step(n, i, s, first, last):
        if not last:
            for sem in used:
                sp.wait_ge(sem, n + 1)
            load(s, first_node(st, n + 2))
        sp.wait_ge(outs_ready, n + 1)
        if last and s == 1:
            sp.wait_ge(stored[0], 16 * (i + 1))
        store(s, first_node(st, n)).then_inc(stored[s], 16)

    for s in (0, 1):
        load(s, first_node(st, s))
    over_pairs(sp, CHUNKS, step)
    for s in (0, 1):
        sp.wait_ge(stored[s], 16 * (CHUNKS // 2))


def table_rows(tab, row, per=1):
    return tab[bass.ds(row * per, CHUNK * per)].rearrange("(p r) w -> p (r w)", p=P)


def x_of(tab, row):
    return tab[bass.ds(row * 2, CHUNK * 2)].rearrange("(p r two) w -> p r two w", p=P, two=2)[:, :, 0, 0:D]


def over_rows(ap):
    return ap.unsqueeze(1).broadcast_to([P, R, ap.shape[1]])


class Norm:

    def __init__(self, nc, ph, st, tag, centre, by_log=False):
        self.nc, self.centre, self.by_log, self.eps = nc, centre, by_log, st["eps"]
        self.sum, self.mean, self.var, self.root, self.rstd = (
            ph.sb(f"{tag}_{n}", [P, R]) for n in ("sum", "mean", "var", "root", "rstd"))
        self.square = ph.sb(f"{tag}_square", [P, R, D])
        self.centred, self.squared, self.summed, self.rooted, self.act_chain = ph.sems(
            f"{tag}_centred {tag}_squared {tag}_summed {tag}_rooted {tag}_act_chain")

    def steps(self):
        return (2 if self.centre else 0) + (0 if self.by_log else 1)

    def take_mean(self, steps, v):
        steps.then(self.nc.vector.reduce_sum(self.sum[:], v, AX_X))
        steps.then(self.nc.vector.tensor_scalar(self.mean[:], self.sum[:], -1.0 / D, None, ALU.mult))
        self.nc.vector.tensor_tensor(v, v, bcast(self.mean[:], D), ALU.add).then_inc(self.centred, 1)

    def squares(self, act, n, v, ready=None):
        act.wait_ge(ready or self.centred, n + 1)
        self.nc.scalar.activation(self.square[:], v, ACT.Square).then_inc(self.squared, 1)

    def take_root(self, act, n):
        nc = self.nc
        act.wait_ge(self.summed, n + 1)
        if self.by_log:
            nc.scalar.activation(self.root[:], self.var[:], ACT.Ln, scale=1.0 / D, bias=self.eps[:]
                                 ).then_inc(self.act_chain, 1)
            act.wait_ge(self.act_chain, n + 1)
            nc.scalar.activation(self.rstd[:], self.root[:], ACT.Exp, scale=-0.5).then_inc(self.rooted, 1)
        else:
            nc.scalar.activation(self.root[:], self.var[:], ACT.Sqrt, scale=1.0 / D, bias=self.eps[:]
                                 ).then_inc(self.rooted, 1)

    def sum_squares(self, dve, n):
        dve.wait_ge(self.squared, n + 1)
        self.nc.vector.reduce_sum(self.var[:], self.square[:], AX_X).then_inc(self.summed, 1)

    def scale(self, dve, steps, n, v, out):
        dve.wait_ge(self.rooted, n + 1)
        if not self.by_log:
            steps.then(self.nc.vector.reciprocal(self.rstd[:], self.root[:]))
        return self.nc.vector.tensor_tensor(out, v, bcast(self.rstd[:], D), ALU.mult)


class Product:

    def __init__(self, nc, ph, st, tag, width, turn_banks, out_banks):
        self.nc, self.st, self.width, self.passed = nc, st, width, ph.passed
        self.turn_banks, self.out_banks = turn_banks, out_banks
        self.rows_t = [[ph.sb(f"{tag}_t{s}{h}", [width, R // 2 * P]) for h in (0, 1)] for s in (0, 1)]
        self.turned, self.copied, self.done = ph.sems(f"{tag}_turned {tag}_copied {tag}_done")

    def turn(self, pe, n, s, rows, ready, first):
        pe.wait_ge(ready[0], ready[1])
        one = len(self.turn_banks) == 2
        if one:
            if not n_is(n, 0, first):
                pe.wait_ge(self.copied, n * 2)
        elif not first:
            pe.wait_ge(self.copied, n * 2 - 2)
        hold(pe, self.passed)
        for h in (0, 1):
            b = self.turn_banks[h if one else 2 * s + h]
            for r in range(R // 2):
                ins = self.nc.tensor.transpose(b[0:self.width, r * P:(r + 1) * P], rows[:, h * (R // 2) + r, :],
                                               self.st["ident"][:])
            ins.then_inc(self.turned, 1)

    def copy(self, act, n, s, first):
        for h in (0, 1):
            b = self.turn_banks[h if len(self.turn_banks) == 2 else 2 * s + h]
            act.wait_ge(self.turned, n * 2 + h + 1)
            if not first:
                act.wait_ge(self.done, n - 1)
            self.nc.scalar.activation(self.rows_t[s][h][:], b[0:self.width, :], ACT.Copy).then_inc(self.copied, 1)

    def multiply(self, pe, n, s, weight, read, first):
        b = self.out_banks[s if len(self.out_banks) == 2 else 0]
        if len(self.out_banks) == 2:
            if not first:
                pe.wait_ge(read, n - 1)
        elif not n_is(n, 0, first):
            pe.wait_ge(read, n)
        for h in (0, 1):
            pe.wait_ge(self.copied, n * 2 + h + 1)
            for r in range(R // 2):
                q = h * (R // 2) + r
                ins = self.nc.tensor.matmul(b[:, q * D:(q + 1) * D], self.rows_t[s][h][:, r * P:(r + 1) * P], weight,
                                            start=True, stop=True)
        ins.then_inc(self.done, 1)

    def result(self, s):
        b = self.out_banks[s if len(self.out_banks) == 2 else 0]
        return b[:].rearrange("p (r d) -> p r d", d=D)


def dense_mean(nc, a, st):
    CHUNKS, BLOCKS, NT, bank = st["CHUNKS"], st["BLOCKS"], st["NT"], st["bank"]
    assert CHUNKS == BLOCKS
    with Phase(nc, "d0") as ph:
        x, agg = ([ph.sb(f"{n}{s}", [P, R, w]) for s in (0, 1)] for n, w in (("x", D), ("agg", 66)))
        both = [ph.sb(f"both{s}", [P, R, P]) for s in (0, 1)]
        out = [ph.sb(f"out{s}", [P, R, P]) for s in (0, 1)]
        v = [ph.sb(f"v{s}", [P, R, D]) for s in (0, 1)]
        recip = ph.sb("recip", [P, R])
        max_of = [ph.sb(f"max_of{s}", [P, G]) for s in (0, 1)]
        max_i = [ph.sb(f"max_i{s}", [P, G], I32) for s in (0, 1)]
        pr = Product(nc, ph, st, "p", P, bank[0:4], bank[4:6])
        ln = Norm(nc, ph, st, "n", False)
        x_put, scaled, added, normed, chain_a, chain_b, max_staged, max_used, self_arg = ph.sems(
            "x_put scaled added normed chain_a chain_b max_staged max_used self_arg")
        loaded, stored, max_in = ([ph.sem(f"{n}{s}") for s in (0, 1)] for n in ("loaded", "stored", "max_in"))
        block = ph.ctx.enter_context(nc.Block())

        @block.sync
        def _(sp):
            def load(s, row):
                sp.dma_start(x[s][:].rearrange("p r d -> p (r d)"), table_rows(a["x"], row)).then_inc(loaded[s], 16)
                sp.dma_start(agg[s][:].rearrange("p r d -> p (r d)"), table_rows(st["mean_tab"], row)
                             ).then_inc(loaded[s], 16)

            def store(s, row):
                return sp.dma_start(table_rows(st["gate1_tab"], row, 2), out[s][:].rearrange("p r d -> p (r d)"))

            load_and_store(sp, st, load, store, normed, (scaled, x_put), stored)

        @block.gpsimd
        def _(pool):
            maxima = st["mean_tab"].rearrange("n (w o) -> (n w) o", o=1)

            def step(n, i, s, first, last):
                pool.wait_ge(max_staged, n + 1)
                gather_rows(nc, [(max_of[s][:, q:q + 1], q) for q in range(G)], maxima, max_i[s], max_in[s], ph.passed)

            over_pairs(pool, BLOCKS, step)

        @block.vector
        def _(dve):
            steps_a, steps_b = Steps(dve, chain_a, 2), Steps(dve, chain_b, ln.steps())

            def stage_max(n, s):
                nc.vector.tensor_scalar(max_i[s][:], st["dst_g"][:, bass.ds(n * G, G)], 66.0, 65.0, ALU.mult, ALU.add
                                        ).then_inc(max_staged, 1)

            def scale(n, i, s, first):
                steps_a.turn(n)
                dve.wait_ge(loaded[s], 32 * (i + 1))
                if not first:
                    dve.wait_ge(pr.turned, n * 2 - 2)
                cols = bass.ds(n * R, R)
                nc.vector.tensor_copy(st["degree"][:, cols], agg[s][:, :, 64])
                nc.vector.tensor_copy(st["self_exp"][:, cols], agg[s][:, :, 65])
                steps_a.then(nc.vector.tensor_scalar(recip[:], agg[s][:, :, 64], 1.0, None, ALU.max))
                steps_a.then(nc.vector.reciprocal(recip[:], recip[:]))
                nc.vector.tensor_tensor(both[s][:, :, D:P], agg[s][:, :, 0:D], bcast(recip[:], D), ALU.mult
                                        ).then_inc(scaled, 1)
                steps_a.end()

            def step(n, i, s, first, last):
                steps_b.turn(n)
                dve.wait_ge(pr.done, n + 1)
                if not first:
                    dve.wait_ge(normed, n - 1)
                nc.vector.tensor_tensor(v[s][:], pr.result(s), over_rows(st["rows"][:, st["B_MEAN"], :]), ALU.add
                                        ).then_inc(added, 1)
                if not last:
                    dve.wait_ge(scaled, n + 2)
                    scale(n + 2, i + 1, s, False)
                dve.wait_ge(max_in[s], 64 * (i + 1))
                cols = bass.ds(n * G, G)
                nc.vector.tensor_tensor(st["w_exp"][:, cols], st["w_edge"][:, cols], max_of[s][:], ALU.subtract
                                        ).then_inc(max_used, 1)
                if not last:
                    dve.wait_ge(max_used, n + 1)
                    stage_max(n + 2, s)
                ln.sum_squares(dve, n)
                if not first:
                    dve.wait_ge(stored[s], 16 * i)
                ln.scale(dve, steps_b, n, v[s][:], out[s][:, :, 0:D]).then_inc(normed, 1)
                steps_b.end()

            for s in (0, 1):
                nc.vector.memset(out[s][:, :, D:P], 0.0)
            for s in (0, 1):
                stage_max(s, s)
                if s == 1:
                    dve.wait_ge(scaled, 1)
                scale(s, 0, s, True)
            over_pairs(dve, CHUNKS, step)
            nc.vector.tensor_scalar(st["self_exp"][:], st["self_exp"][:], -1.0, 1.0, ALU.mult, ALU.add
                                    ).then_inc(self_arg, 1)

        @block.scalar
        def _(act):
            act.preload_act_table_set("sqrt_and_others")

            def put_x(n, i, s, first):
                act.wait_ge(loaded[s], 32 * (i + 1))
                if not first:
                    act.wait_ge(pr.turned, n * 2 - 2)
                nc.scalar.activation(both[s][:, :, 0:D], x[s][:], ACT.Copy).then_inc(x_put, 1)

            def step(n, i, s, first, last):
                pr.copy(act, n, s, first)
                if not last:
                    put_x(n + 2, i + 1, s, False)
                if not n_is(n, 0, first):
                    act.wait_ge(normed, n)
                ln.squares(act, n, v[s][:], added)
                ln.take_root(act, n)

            for s in (0, 1):
                put_x(s, 0, s, True)
            over_pairs(act, CHUNKS, step)
            act.wait_ge(self_arg, 1)
            nc.scalar.activation(st["self_exp"][:], st["self_exp"][:], ACT.Exp)
            nc.scalar.activation(st["w_exp"][:], st["w_exp"][:], ACT.Exp)

        @block.tensor
        def _(pe):
            def turn(n, s, first):
                pe.wait_ge(scaled, n + 1)
                pr.turn(pe, n, s, both[s], (x_put, n + 1), first)

            def step(n, i, s, first, last):
                if not (last and s == 1):
                    turn(n + 1, 1 - s, n_is(n, 0, first))
                pr.multiply(pe, n, s, st["w_self"][:], added, first)

            turn(0, 0, True)
            over_pairs(pe, CHUNKS, step)


def dense_gate(nc, st, tag, table, which, residual, dest):
    CHUNKS, bank = st["CHUNKS"], st["bank"]
    final = residual is not None
    W = D if final else P
    with Phase(nc, tag) as ph:
        both = [ph.sb(f"both{s}", [P, R, P]) for s in (0, 1)]
        out = [ph.sb(f"out{s}", [P, R, W]) for s in (0, 1)]
        v = [ph.sb(f"v{s}", [P, R, D]) for s in (0, 1)]
        res = [ph.sb(f"res{s}", [P, R, D]) for s in (0, 1)]
        pr = Product(nc, ph, st, "p", P, bank[0:4], bank[4:6])
        ln = Norm(nc, ph, st, "n", True)
        added, finished, chain = ph.sems("added finished chain")
        loaded, stored, res_in = ([ph.sem(f"{n}{s}") for s in (0, 1)] for n in ("loaded", "stored", "res_in"))
        bias = over_rows(st["rows"][:, st["B_MIX1"] + which, :])
        block = ph.ctx.enter_context(nc.Block())

        @block.sync
        def _(sp):
            def load(s, row):
                sp.dma_start(both[s][:].rearrange("p r d -> p (r d)"), table_rows(table, row, 2)
                             ).then_inc(loaded[s], 16)
                if final:
                    sp.dma_start(res[s][:], x_of(residual, row)).then_inc(res_in[s], 16)

            def store(s, row):
                return sp.dma_start(table_rows(dest, row, W // D), out[s][:].rearrange("p r d -> p (r d)"))

            load_and_store(sp, st, load, store, finished, (added, finished) if final else (added,), stored)

        @block.vector
        def _(dve):
            steps = Steps(dve, chain, 1 + ln.steps())

            def step(n, i, s, first, last):
                dve.wait_ge(pr.done, n + 1)
                if not first:
                    dve.wait_ge(finished, n - 1)
                ins = nc.vector.tensor_tensor(v[s][:], pr.result(s), bias, ALU.add).then_inc(added, 1)
                if final:
                    steps.turn(n)
                    dve.wait_ge(added, n + 1)
                    dve.wait_ge(res_in[s], 16 * (i + 1))
                    steps.then(nc.vector.scalar_tensor_tensor(out=v[s][:], in0=v[s][:], scalar=0.0, in1=res[s][:],
                                                              op0=ALU.max, op1=ALU.add))
                    ln.take_mean(steps, v[s][:])
                    ln.sum_squares(dve, n)
                    if not first:
                        dve.wait_ge(stored[s], 16 * i)
                    ln.scale(dve, steps, n, v[s][:], out[s][:]).then_inc(finished, 1)
                    steps.end()

            if not final:
                for s in (0, 1):
                    nc.vector.memset(out[s][:, :, D:P], 0.0)
            over_pairs(dve, CHUNKS, step)

        @block.scalar
        def _(act):
            act.preload_act_table_set("sqrt_and_others")

            def step(n, i, s, first, last):
                pr.copy(act, n, s, first)
                if final:
                    if not n_is(n, 0, first):
                        act.wait_ge(finished, n)
                    ln.squares(act, n, v[s][:])
                    ln.take_root(act, n)
                else:
                    act.wait_ge(added, n + 1)
                    if not first:
                        act.wait_ge(stored[s], 16 * i)
                    nc.scalar.activation(out[s][:, :, 0:D], v[s][:], ACT.Relu).then_inc(finished, 1)

            over_pairs(act, CHUNKS, step)

        @block.tensor
        def _(pe):
            def turn(n, i, s, first):
                pr.turn(pe, n, s, both[s], (loaded[s], 16 * (i + 1)), first)

            def step(n, i, s, first, last):
                if not (last and s == 1):
                    turn(n + 1, i + s, 1 - s, n_is(n, 0, first))
                pr.multiply(pe, n, s, st["w_mix"][which][:], added, first)

            turn(0, 0, 0, True)
            over_pairs(pe, CHUNKS, step)


def attention_sums(nc, st):
    BLOCKS, bank, ident = st["BLOCKS"], st["bank"], st["ident"]
    HW = DH + 1
    W = H * HW
    QW = 3 * D + H
    with Phase(nc, "att") as ph:
        bl = Blocks(nc, ph, st, st["src_key"], W)
        ends = [ph.sb(f"ends{s}", [P, G, P]) for s in (0, 1)]
        ends_t = ph.sb("ends_t", [P, G * P])
        qkv = ph.sb("qkv", [P, G, QW])
        state, new = ([ph.sb(f"{n}{s}", [P, G, W + H]) for s in (0, 1)] for n in ("state", "new"))
        src_i, dst_i, put_i = ([ph.sb(f"{n}{s}", [P, G], I32) for s in (0, 1)] for n in ("src_i", "dst_i", "put_i"))
        away = ph.sb("away", [P, G, G * P])
        junk = ph.sb("junk", [P, G, G * P])
        prod, vals = ph.sb("prod", [P, G, D]), ph.sb("vals", [P, G, D])
        logit, top, ex_arg, ex = (ph.sb(n, [P, G, H]) for n in ("logit", "top", "ex_arg", "ex"))
        diff, factor = ph.sb("diff", [P, 2, G, H]), ph.sb("factor", [P, 2, G, H])
        old_part, new_part = ph.sb("old_part", [P, G, W]), ph.sb("new_part", [P, G, W])
        (staged, turned, matched, away_done, ends_turned, ends_copied, produced, qkv_copied, logits, qkv_used,
         logit_turned, head_max, ex_ready, ex_done, paid, summed, differences, factors, updated, chain_f, chain_b,
         chain_u) = ph.sems(
            "staged turned matched away_done ends_turned ends_copied produced qkv_copied logits qkv_used "
            "logit_turned head_max ex_ready ex_done paid summed differences factors updated chain_f chain_b chain_u")
        gathered, state_in, scattered = ([ph.sem(f"{n}{s}") for s in (0, 1)] for n in
                                         ("gathered", "state_in", "scattered"))
        key_t, ends_b, qkv_b, logit_t, sums = bank[0], bank[1], bank[2:4], bank[4:6], bank[6:8]
        block = ph.ctx.enter_context(nc.Block())

        @block.gpsimd
        def _(pool):
            def dst_rows(s):
                gather_rows(nc, [(ends[s][:, q, 0:D], q) for q in range(G)], st["attn_x"], dst_i[s], gathered[s], ph.passed)

            def src_rows(s):
                gather_rows(nc, [(ends[s][:, q, D:P], q) for q in range(G)], st["attn_x"], src_i[s], gathered[s], ph.passed)

            def step(n, i, s, first, last):
                more = not (last and s == 1)
                if more:
                    pool.wait_ge(staged, n + 2)
                    if not n_is(n, 0, first):
                        pool.wait_ge(ends_turned, n)
                    dst_rows(1 - s)
                if not (first and s == 0):
                    pool.wait_ge(scattered[1 - s], 64 * last_use(i, s))
                gather_rows(nc, [(state[s][:, q, :], q) for q in range(G)], st["attn_tab"], src_i[s], state_in[s], ph.passed)
                if more:
                    src_rows(1 - s)
                pool.wait_ge(updated, n + 1)
                hold(pool, ph.passed)
                for q in range(G):
                    nc.gpsimd.indirect_dma_start(
                        st["attn_tab"], bass.IndirectOffsetOnAxis(ap=put_i[s][:, q:q + 1], axis=0),
                        new[s][:, q, :], None).then_inc(scattered[s], 16)

            pool.wait_ge(staged, 1)
            dst_rows(0)
            src_rows(0)
            over_pairs(pool, BLOCKS, step)
            for s in (0, 1):
                pool.wait_ge(scattered[s], 64 * (BLOCKS // 2))

        @block.vector
        def _(dve):
            steps_f, steps_b, steps_u = Steps(dve, chain_f, 3), Steps(dve, chain_b, 1), Steps(dve, chain_u, 2)

            def stage(n, s):
                bl.stage(n, s, ((src_i[s], st["src_g"]), (dst_i[s], st["dst_g"]))).then_inc(staged, 1)

            def heads(ap):
                return ap.rearrange("p t (h c) -> p t h c", h=H)

            def over_heads(ap):
                return ap.unsqueeze(2).broadcast_to([P, G, H, EF])

            def per_head(ap, w):
                return ap.unsqueeze(3).broadcast_to([P, G, H, w])

            def front(n, s, first):
                steps_f.turn(n)
                kv = st["edge_kv"][:, bass.ds(n * G, G), :]
                dve.wait_ge(turned, n + 1)
                if not first:
                    dve.wait_ge(summed, n - 1)
                bl.make_match(key_t, s).then_inc(matched, 1)
                dve.wait_ge(qkv_copied, n + 1)
                steps_f.then(nc.vector.tensor_tensor(heads(prod[:]), heads(qkv[:, :, D + H:2 * D + H]),
                                                     over_heads(kv[:, :, 0:EF]), ALU.mult))
                steps_f.then(nc.vector.tensor_tensor(prod[:], prod[:], qkv[:, :, 0:D], ALU.mult))
                steps_f.then(nc.vector.reduce_sum(logit[:], heads(prod[:]), AX_X))
                nc.vector.tensor_tensor(logit[:], logit[:], qkv[:, :, D:D + H], ALU.add).then_inc(logits, 1)
                nc.vector.tensor_tensor(heads(vals[:]), heads(qkv[:, :, 2 * D + H:QW]),
                                        over_heads(kv[:, :, EF:2 * EF]), ALU.mult).then_inc(qkv_used, 1)
                steps_f.end()

            def pay(n, s):
                steps_b.turn(n)
                dve.wait_ge(away_done, n + 1)
                for h in range(H):
                    dve.wait_ge(logit_turned, n * H + h + 1)
                    hold(dve, ph.passed)
                    for q in range(G):
                        ins = nc.vector.tensor_tensor_reduce(junk[:, q, :], away[:, q, :], logit_t[h % 2][:], 1.0,
                                                             -2.0 * BIG, ALU.add, ALU.max, top[:, q, h:h + 1])
                    ins.then_inc(head_max, 1)
                    dve.wait_ge(head_max, n * H + h + 1)
                nc.vector.tensor_tensor(ex_arg[:], logit[:], top[:], ALU.subtract).then_inc(ex_ready, 1)
                dve.wait_ge(ex_done, n + 1)
                dve.wait_ge(qkv_used, n + 1)
                out = heads(bl.payload[s][:])
                steps_b.then(nc.vector.tensor_copy(out[:, :, :, DH], ex[:]))
                nc.vector.tensor_tensor(out[:, :, :, 0:DH], heads(vals[:]), per_head(ex[:], DH), ALU.mult
                                        ).then_inc(paid, 1)
                steps_b.end()

            def update(n, i, s, first):
                steps_u.turn(n)
                dve.wait_ge(state_in[s], 64 * (i + 1))
                if not first:
                    dve.wait_ge(scattered[s], 64 * i)
                old, row = state[s], new[s]
                steps_u.then(nc.vector.tensor_tensor(row[:, :, W:W + H], old[:, :, W:W + H], top[:], ALU.max))
                nc.vector.tensor_tensor(diff[:, 0], old[:, :, W:W + H], row[:, :, W:W + H], ALU.subtract)
                nc.vector.tensor_tensor(diff[:, 1], top[:], row[:, :, W:W + H], ALU.subtract
                                        ).then_inc(differences, 1)
                nc.vector.tensor_copy(put_i[s][:], st["src_put"][:, bass.ds(n * G, G)])
                dve.wait_ge(factors, n + 1)
                nc.vector.tensor_tensor(heads(old_part[:]), heads(old[:, :, 0:W]), per_head(factor[:, 0], HW), ALU.mult)
                dve.wait_ge(summed, n + 1)
                steps_u.then(nc.vector.tensor_tensor(
                    heads(new_part[:]), heads(sums[s][:, 0:G * W].rearrange("p (t w) -> p t w", w=W)),
                    per_head(factor[:, 1], HW), ALU.mult))
                nc.vector.tensor_tensor(row[:, :, 0:W], old_part[:], new_part[:], ALU.add).then_inc(updated, 1)
                steps_u.end()

            def step(n, i, s, first, last):
                pay(n, s)
                if not (last and s == 1):
                    front(n + 1, 1 - s, n_is(n, 0, first))
                update(n, i, s, first)
                if not last:
                    stage(n + 2, s)

            for s in (0, 1):
                stage(s, s)
            front(0, 0, True)
            over_pairs(dve, BLOCKS, step)

        @block.scalar
        def _(act):
            act.preload_act_table_set("natural_log_exp_and_others")

            def front(n, i, s, first):
                act.wait_ge(ends_turned, n + 1)
                if not first:
                    act.wait_ge(produced, n)
                nc.scalar.activation(ends_t[:], ends_b[:], ACT.Copy).then_inc(ends_copied, 1)
                act.wait_ge(produced, n + 1)
                if not first:
                    act.wait_ge(qkv_used, n)
                for k in (0, 1):
                    ins = nc.scalar.activation(qkv[:, 2 * k:2 * k + 2, :],
                                               qkv_b[k][:, 0:2 * QW].rearrange("p (t w) -> p t w", w=QW), ACT.Copy)
                ins.then_inc(qkv_copied, 1)
                act.wait_ge(matched, n + 1)
                if not first:
                    act.wait_ge(head_max, n * H)
                for q in range(G):
                    ins = nc.scalar.activation(away[:, q, :], bl.match[s][:, q, :], ACT.Identity, scale=BIG,
                                               bias=st["minus_big"][:])
                ins.then_inc(away_done, 1)

            def step(n, i, s, first, last):
                act.wait_ge(ex_ready, n + 1)
                if not n_is(n, 0, first):
                    act.wait_ge(paid, n)
                nc.scalar.activation(ex[:], ex_arg[:], ACT.Exp).then_inc(ex_done, 1)
                if not (last and s == 1):
                    front(n + 1, i + s, 1 - s, False)
                act.wait_ge(differences, n + 1)
                if not n_is(n, 0, first):
                    act.wait_ge(updated, n)
                nc.scalar.activation(factor[:], diff[:], ACT.Exp).then_inc(factors, 1)

            front(0, 0, 0, True)
            over_pairs(act, BLOCKS, step)

        @block.tensor
        def _(pe):
            def front(n, i, s, first):
                pe.wait_ge(gathered[s], 128 * (i + 1))
                if not first:
                    pe.wait_ge(ends_copied, n)
                for q in range(G):
                    ins = nc.tensor.transpose(ends_b[:, q * P:(q + 1) * P], ends[s][:, q, :], ident[:])
                ins.then_inc(ends_turned, 1)
                pe.wait_ge(staged, n + 1)
                if not first:
                    pe.wait_ge(matched, n)
                bl.turn_keys(key_t, s).then_inc(turned, 1)
                pe.wait_ge(ends_copied, n + 1)
                if not first:
                    pe.wait_ge(qkv_copied, n)
                for q in range(G):
                    ins = nc.tensor.matmul(qkv_b[q // 2][:, q % 2 * QW:(q % 2 + 1) * QW], ends_t[:, q * P:(q + 1) * P],
                                           st["w_att"][:], start=True, stop=True)
                ins.then_inc(produced, 1)

            def turn_logits(n, first):
                pe.wait_ge(logits, n + 1)
                for h in range(H):
                    if not (first and h < 2):
                        pe.wait_ge(head_max, n * H + h - 1)
                    for q in range(G):
                        ins = nc.tensor.transpose(logit_t[h % 2][:, q * P:(q + 1) * P],
                                                  logit[:, q, h:h + 1].broadcast_to([P, P]), ident[:])
                    ins.then_inc(logit_turned, 1)

            def step(n, i, s, first, last):
                if not (last and s == 1):
                    front(n + 1, i + s, 1 - s, False)
                pe.wait_ge(matched, n + 1)
                pe.wait_ge(paid, n + 1)
                if not first:
                    pe.wait_ge(updated, n - 1)
                bl.segment_sums(sums[s], s).then_inc(summed, 1)
                if not (last and s == 1):
                    turn_logits(n + 1, False)

            front(0, 0, 0, True)
            turn_logits(0, True)
            over_pairs(pe, BLOCKS, step)


def dense_attention(nc, st):
    CHUNKS, bank, rows = st["CHUNKS"], st["bank"], st["rows"]
    HW = DH + 1
    with Phase(nc, "da") as ph:
        x, agg, res = ([ph.sb(f"{n}{s}", [P, R, w]) for s in (0, 1)] for n, w in (("x", D), ("agg", 72), ("res", D)))
        both = [ph.sb(f"both{s}", [P, R, P]) for s in (0, 1)]
        out = [ph.sb(f"out{s}", [P, R, 130]) for s in (0, 1)]
        v = [ph.sb(f"v{s}", [P, R, D]) for s in (0, 1)]
        part = [ph.sb(f"part{s}", [P, R, H]) for s in (0, 1)]
        recip = ph.sb("recip", [P, R, H])
        z, e, soft, vb = (ph.sb(n, [P, R, D]) for n in ("z", "e", "soft", "vb"))
        p1 = Product(nc, ph, st, "p1", P, bank[0:2], bank[4:5])
        p2 = Product(nc, ph, st, "p2", D, bank[2:4], bank[5:7])
        ln1 = Norm(nc, ph, st, "n1", False, by_log=True)
        ln2 = Norm(nc, ph, st, "n2", True, by_log=True)
        (x_put, scaled, added1, added2, logged, softened, finished, chain_a, chain_b, chain_c, chain_l) = ph.sems(
            "x_put scaled added1 added2 logged softened finished chain_a chain_b chain_c chain_l")
        loaded, stored, res_in = ([ph.sem(f"{n}{s}") for s in (0, 1)] for n in ("loaded", "stored", "res_in"))
        block = ph.ctx.enter_context(nc.Block())

        @block.sync
        def _(sp):
            def load(s, row):
                sp.dma_start(x[s][:].rearrange("p r d -> p (r d)"), table_rows(st["attn_x"], row)
                             ).then_inc(loaded[s], 16)
                sp.dma_start(agg[s][:].rearrange("p r d -> p (r d)"), table_rows(st["attn_tab"], row)
                             ).then_inc(loaded[s], 16)

            def step(n, i, s, first, last):
                if not last:
                    sp.wait_ge(scaled, n + 1)
                    sp.wait_ge(x_put, n + 1)
                    load(s, first_node(st, n + 2))
                sp.wait_ge(finished, n + 1)
                if last and s == 1:
                    sp.wait_ge(stored[0], 16 * (i + 1))
                sp.dma_start(table_rows(st["sage1_tab"], first_node(st, n), 2),
                             out[s][:].rearrange("p r d -> p (r d)")).then_inc(stored[s], 16)
                if not last:
                    sp.dma_start(res[s][:].rearrange("p r d -> p (r d)"),
                                 table_rows(st["attn_x"], first_node(st, n + 2))).then_inc(res_in[s], 16)

            for s in (0, 1):
                load(s, first_node(st, s))
                sp.dma_start(res[s][:].rearrange("p r d -> p (r d)"), table_rows(st["attn_x"], first_node(st, s))
                             ).then_inc(res_in[s], 16)
            over_pairs(sp, CHUNKS, step)
            for s in (0, 1):
                sp.wait_ge(stored[s], 16 * (CHUNKS // 2))

        @block.vector
        def _(dve):
            steps_a, steps_b = Steps(dve, chain_a, 2), Steps(dve, chain_b, 2)
            steps_c = Steps(dve, chain_c, 4 + ln1.steps() + ln2.steps())

            def heads(ap):
                return ap.rearrange("p r (h c) -> p r h c", h=H)

            def per_head(ap):
                return ap.unsqueeze(3).broadcast_to([P, R, H, DH])

            def scale(n, i, s, first):
                steps_a.turn(n)
                dve.wait_ge(loaded[s], 32 * (i + 1))
                if not first:
                    dve.wait_ge(p1.turned, n * 2 - 2)
                hd = agg[s][:, :, 0:H * HW].rearrange("p r (h c) -> p r h c", c=HW)
                steps_a.then(nc.vector.tensor_scalar(recip[:], hd[:, :, :, DH], 1e-16, None, ALU.add))
                steps_a.then(nc.vector.reciprocal(recip[:], recip[:]))
                nc.vector.tensor_tensor(part[s][:], hd[:, :, :, DH], recip[:], ALU.mult)
                nc.vector.tensor_tensor(heads(both[s][:, :, D:P]), hd[:, :, :, 0:DH], per_head(recip[:]), ALU.mult
                                        ).then_inc(scaled, 1)
                steps_a.end()

            def first_half(n, s):
                steps_b.turn(n)
                dve.wait_ge(scaled, n + 1)
                steps_b.then(nc.vector.tensor_tensor(heads(vb[:]), per_head(part[s][:]),
                                                     heads(over_rows(rows[:, st["B_VL"], :])), ALU.mult))
                steps_b.then(nc.vector.tensor_tensor(vb[:], vb[:], over_rows(rows[:, st["B_CEN"], :]), ALU.add))
                dve.wait_ge(p1.done, n + 1)
                nc.vector.tensor_tensor(z[:], p1.result(s), vb[:], ALU.add).then_inc(added1, 1)
                steps_b.end()

            def soften(n, first):
                dve.wait_ge(logged, n + 1)
                if not first:
                    dve.wait_ge(p2.turned, n * 2)
                nc.vector.scalar_tensor_tensor(out=soft[:], in0=z[:], scalar=0.0, in1=e[:], op0=ALU.max, op1=ALU.add
                                               ).then_inc(softened, 1)

            def step(n, i, s, first, last):
                steps_c.turn(n)
                more = not (last and s == 1)
                dve.wait_ge(p2.done, n + 1)
                nc.vector.tensor_tensor(v[s][:], p2.result(s), over_rows(rows[:, st["B_OUT"], :]), ALU.add
                                        ).then_inc(added2, 1)
                if not last:
                    scale(n + 2, i + 1, s, False)
                if more:
                    first_half(n + 1, 1 - s)
                ln1.sum_squares(dve, n)
                if more:
                    soften(n + 1, False)
                steps_c.then(ln1.scale(dve, steps_c, n, v[s][:], v[s][:]))
                steps_c.then(nc.vector.tensor_tensor(v[s][:], v[s][:], over_rows(rows[:, st["B_LNG"], :]), ALU.mult))
                steps_c.then(nc.vector.tensor_tensor(v[s][:], v[s][:], over_rows(rows[:, st["B_LNB"], :]), ALU.add))
                dve.wait_ge(res_in[s], 16 * (i + 1))
                steps_c.then(nc.vector.tensor_tensor(v[s][:], v[s][:], res[s][:], ALU.add))
                ln2.take_mean(steps_c, v[s][:])
                ln2.sum_squares(dve, n)
                if not first:
                    dve.wait_ge(stored[s], 16 * i)
                ln2.scale(dve, steps_c, n, v[s][:], out[s][:, :, 0:D]).then_inc(finished, 1)
                steps_c.end()

            for s in (0, 1):
                nc.vector.memset(out[s][:, :, D:130], 0.0)
            for s in (0, 1):
                if s:
                    dve.wait_ge(scaled, 1)
                scale(s, 0, s, True)
            first_half(0, 0)
            soften(0, True)
            over_pairs(dve, CHUNKS, step)

        @block.scalar
        def _(act):
            act.preload_act_table_set("natural_log_exp_and_others")

            def put_x(n, i, s, first):
                act.wait_ge(loaded[s], 32 * (i + 1))
                if not first:
                    act.wait_ge(p1.turned, n * 2 - 2)
                nc.scalar.activation(both[s][:, :, 0:D], x[s][:], ACT.Copy).then_inc(x_put, 1)

            def log_part(n, first):
                act.wait_ge(added1, n + 1)
                if not first:
                    act.wait_ge(softened, n)
                nc.scalar.activation(e[:], z[:], ACT.Abs).then_inc(chain_l, 1)
                act.wait_ge(chain_l, n * 2 + 1)
                nc.scalar.activation(e[:], e[:], ACT.Exp, scale=-1.0).then_inc(chain_l, 1)
                act.wait_ge(chain_l, n * 2 + 2)
                nc.scalar.activation(e[:], e[:], ACT.Ln, bias=st["half"][:], scale=0.5).then_inc(logged, 1)

            def step(n, i, s, first, last):
                more = not (last and s == 1)
                ln1.squares(act, n, v[s][:], added2)
                if not last:
                    put_x(n + 2, i + 1, s, False)
                    p1.copy(act, n + 2, s, False)
                if more:
                    log_part(n + 1, False)
                ln1.take_root(act, n)
                if more:
                    p2.copy(act, n + 1, 1 - s, n_is(n, 0, first))
                ln2.squares(act, n, v[s][:])
                ln2.take_root(act, n)

            for s in (0, 1):
                put_x(s, 0, s, True)
                p1.copy(act, s, s, True)
            log_part(0, True)
            p2.copy(act, 0, 0, True)
            over_pairs(act, CHUNKS, step)

        @block.tensor
        def _(pe):
            def product1(n, s, first):
                pe.wait_ge(scaled, n + 1)
                p1.turn(pe, n, s, both[s], (x_put, n + 1), first)
                p1.multiply(pe, n, s, st["w_att_out"][:], added1, first)

            def product2(n, s, first):
                p2.turn(pe, n, s, soft, (softened, n + 1), first)
                p2.multiply(pe, n, s, st["w_out"][:], added2, first)

            def step(n, i, s, first, last):
                if not last:
                    product1(n + 2, s, False)
                if not (last and s == 1):
                    product2(n + 1, 1 - s, n_is(n, 0, first))

            for s in (0, 1):
                product1(s, s, True)
            product2(0, 0, True)
            over_pairs(pe, CHUNKS, step)


def dense_sage(nc, st, tag, table, which, residual, dest):
    CHUNKS, bank = st["CHUNKS"], st["bank"]
    final = residual is not None
    W = D if final else 130
    K = D + 1
    with Phase(nc, tag) as ph:
        both = [ph.sb(f"both{s}", [P, R, 2 * K]) for s in (0, 1)]
        mix = [ph.sb(f"mix{s}", [P, R, K]) for s in (0, 1)]
        rho = [ph.sb(f"rho{s}", [P, R]) for s in (0, 1)]
        own = ph.sb("own", [P, R, D])
        out = [ph.sb(f"out{s}", [P, R, W]) for s in (0, 1)]
        v = [ph.sb(f"v{s}", [P, R, D]) for s in (0, 1)]
        res = [ph.sb(f"res{s}", [P, R, D]) for s in (0, 1)]
        deg1 = ph.sb("deg1", [P, R])
        pr = Product(nc, ph, st, "p", K, bank[0:4], bank[4:6])
        ln = Norm(nc, ph, st, "n", True)
        mixed, added, finished, chain, chain_m = ph.sems("mixed added finished chain chain_m")
        loaded, stored, res_in = ([ph.sem(f"{n}{s}") for s in (0, 1)] for n in ("loaded", "stored", "res_in"))
        block = ph.ctx.enter_context(nc.Block())

        @block.sync
        def _(sp):
            def step(n, i, s, first, last):
                if not last:
                    sp.wait_ge(mixed, n + 1)
                    load(s, first_node(st, n + 2))
                sp.wait_ge(finished, n + 1)
                if last and s == 1:
                    sp.wait_ge(stored[0], 16 * (i + 1))
                row = first_node(st, n)
                sp.dma_start(table_rows(dest, row, 1 if final else 2), out[s][:].rearrange("p r d -> p (r d)")
                             ).then_inc(stored[s], 16)
                if final and not last:
                    load_res(s, first_node(st, n + 2))

            def load(s, row):
                sp.dma_start(both[s][:].rearrange("p r d -> p (r d)"), table_rows(table, row, 2)
                             ).then_inc(loaded[s], 16)

            def load_res(s, row):
                sp.dma_start(res[s][:], x_of(residual, row)).then_inc(res_in[s], 16)

            for s in (0, 1):
                load(s, first_node(st, s))
                if final:
                    load_res(s, first_node(st, s))
            over_pairs(sp, CHUNKS, step)
            for s in (0, 1):
                sp.wait_ge(stored[s], 16 * (CHUNKS // 2))

        @block.vector
        def _(dve):
            steps = Steps(dve, chain, 1 + ln.steps())
            steps_m = Steps(dve, chain_m, 4)

            def mix_rows(n, i, s, first):
                steps_m.turn(n)
                dve.wait_ge(loaded[s], 16 * (i + 1))
                if not first:
                    dve.wait_ge(pr.turned, n * 2 - 2)
                cols = bass.ds(n * R, R)
                self_exp = st["self_exp"][:, cols]
                steps_m.then(nc.vector.tensor_tensor(own[:], both[s][:, :, 0:D], bcast(self_exp, D), ALU.mult))
                nc.vector.tensor_tensor(mix[s][:, :, 0:D], own[:], both[s][:, :, K:K + D], ALU.add)
                steps_m.then(nc.vector.tensor_tensor(mix[s][:, :, D], both[s][:, :, 2 * K - 1], self_exp, ALU.add))
                nc.vector.tensor_scalar(deg1[:], st["degree"][:, cols], 1.0, None, ALU.add)
                steps_m.then(nc.vector.tensor_scalar(rho[s][:], mix[s][:, :, D], 1e-16, None, ALU.add))
                steps_m.then(nc.vector.tensor_tensor(rho[s][:], rho[s][:], deg1[:], ALU.mult))
                nc.vector.reciprocal(rho[s][:], rho[s][:]).then_inc(mixed, 1)
                steps_m.end()

            def step(n, i, s, first, last):
                dve.wait_ge(pr.done, n + 1)
                if not first:
                    dve.wait_ge(finished, n - 1)
                nc.vector.tensor_tensor(v[s][:], pr.result(s), bcast(rho[s][:], D), ALU.mult).then_inc(added, 1)
                if not last:
                    dve.wait_ge(added, n + 1)
                    mix_rows(n + 2, i + 1, s, False)
                if final:
                    steps.turn(n)
                    dve.wait_ge(added, n + 1)
                    dve.wait_ge(res_in[s], 16 * (i + 1))
                    steps.then(nc.vector.tensor_tensor(v[s][:], v[s][:], res[s][:], ALU.add))
                    ln.take_mean(steps, v[s][:])
                    ln.sum_squares(dve, n)
                    if not first:
                        dve.wait_ge(stored[s], 16 * i)
                    ln.scale(dve, steps, n, v[s][:], out[s][:]).then_inc(finished, 1)
                    steps.end()

            if not final:
                for s in (0, 1):
                    nc.vector.memset(out[s][:, :, D:W], 0.0)
            for s in (0, 1):
                if s:
                    dve.wait_ge(mixed, 1)
                mix_rows(s, 0, s, True)
            over_pairs(dve, CHUNKS, step)

        @block.scalar
        def _(act):
            act.preload_act_table_set("sqrt_and_others")

            def step(n, i, s, first, last):
                pr.copy(act, n, s, first)
                if final:
                    if not n_is(n, 0, first):
                        act.wait_ge(finished, n)
                    ln.squares(act, n, v[s][:])
                    ln.take_root(act, n)
                else:
                    act.wait_ge(added, n + 1)
                    if not first:
                        act.wait_ge(stored[s], 16 * i)
                    nc.scalar.activation(out[s][:, :, 0:D], v[s][:], ACT.Relu).then_inc(finished, 1)

            over_pairs(act, CHUNKS, step)

        @block.tensor
        def _(pe):
            def turn(n, s, first):
                pr.turn(pe, n, s, mix[s], (mixed, n + 1), first)

            def step(n, i, s, first, last):
                if not (last and s == 1):
                    turn(n + 1, 1 - s, n_is(n, 0, first))
                pr.multiply(pe, n, s, st["w_sage"][which][:], added, first)

            turn(0, 0, True)
            over_pairs(pe, CHUNKS, step)


INPUTS = ["x", "src", "dst", "edge_attr_16", "edge_weight", "edge_weight1"] + [f"L0_gnn_{n}" for n in (
    "W_self", "b_self", "W_neigh", "b_neigh")] + [f"L1_gnn_{n}" for n in (
        "Wk1", "Wq1", "Wv1", "Ws1", "b1", "Wl1", "bl1", "Wk2", "Wq2", "Wv2", "Ws2", "b2", "Wl2", "bl2")] + [
            f"L2_gnn_{n}" for n in (
                "Wk", "Wq", "Wv", "wk1_w", "wk1_b", "wk2_w", "wk2_b", "wkl_w", "wkl_b", "wv1_w", "wv1_b", "wv2_w",
                "wv2_b", "wvl_w", "wvl_b", "cen_w", "cen_b", "out_w", "out_b", "ln_g", "ln_b")] + [
                    f"L3_gnn_{n}" for n in ("lin1_w", "lin1_b", "W1", "lin2_w", "lin2_b", "W2")]


def kernel(**inputs):
    import numpy as np
    import concourse.bacc as bacc
    from concourse.bass_utils import run_bass_kernel_spmd

    nc = bacc.Bacc("TRN2", target_bir_lowering=False, num_devices=1)
    arrays, aps = {}, {}
    for name in INPUTS:
        arr = np.ascontiguousarray(inputs[name])
        arrays[f"in_{name}"] = arr
        aps[name] = nc.dram_tensor(f"in_{name}", arr.shape, mybir.dt.from_np(arr.dtype), kind="ExternalInput").ap()
    shape = arrays["in_x"].shape
    out = nc.dram_tensor("out_0", shape, F32, kind="ExternalOutput").ap()
    gnn_program(nc, aps, out)
    got = run_bass_kernel_spmd(nc, [arrays], core_ids=[0])
    return got.results[0]["out_0"]
```

```python
from contextlib import ExitStack

import concourse.bass as bass
from concourse import mybir

P = 128
D = 64
G = 4
R = 8
CHUNK = P * R
H = 4
DH = D // H
EF = 16
SCRAP = 5 * P
BIG = float(2 ** 100)
LN_EPS = 1e-5
GT = 8

F32 = mybir.dt.float32
I32 = mybir.dt.int32
ALU = mybir.AluOpType
ACT = mybir.ActivationFunctionType
AX_X = mybir.AxisListType.X


def over_pairs(eng, count, body, tail=4):
    assert count % 2 == 0 and count >= tail + 2
    for n in (0, 1):
        body(n, 0, n, True, False)
    with eng.Fori(1, (count - tail) // 2) as i:
        for s in (0, 1):
            body(i * 2 + s, i, s, False, False)
    for n in range(count - tail, count):
        body(n, n // 2, n % 2, False, n >= count - 2)


def hold(eng, passed):
    eng.sem_inc(passed, 1)


def ahead(n, i, s, k):
    return n + k, i + (s + k) // 2, (s + k) % 2


def fresh(n, slots=2):
    return isinstance(n, int) and n < slots


def there(n, count):
    return not isinstance(n, int) or n < count


def last_use(i, s):
    return i + s


class Steps:

    def __init__(self, eng, sem, steps):
        self.eng, self.sem, self.steps = eng, sem, steps

    def turn(self, n):
        self.base, self.k = n * self.steps, 0

    def then(self, ins):
        self.k += 1
        ins.then_inc(self.sem, 1)
        self.eng.wait_ge(self.sem, self.base + self.k)

    def end(self):
        assert self.k == self.steps, (self.k, self.steps)


def bcast(ap, n):
    return ap.unsqueeze(2).broadcast_to([ap.shape[0], ap.shape[1], n])


def gnn_program(nc, a, out):
    N = a["x"].shape[0]
    E = a["src"].shape[0]
    TILES = -(-(-(-E // P)) // GT) * GT
    BLOCKS = TILES // G
    FULL, REST = E // TILES, E % TILES
    CHUNKS = -(-N // CHUNK)
    NT = N + SCRAP
    assert N >= CHUNK and NT * 2 < 2 ** 24

    def dram(name, shape):
        return nc.dram_tensor(name, shape, F32).ap()

    mean_tab = dram("mean_tab", [NT, 66])
    gate1_tab = dram("gate1_tab", [2 * NT, D])
    gate2_tab = dram("gate2_tab", [2 * NT, D])
    attn_x = dram("attn_x", [N, D])
    attn_tab = dram("attn_tab", [NT, 72])
    sage1_tab = dram("sage1_tab", [2 * NT, 65])
    sage2_tab = dram("sage2_tab", [2 * NT, 65])

    ctx = ExitStack()
    with ctx:
        def sb(name, shape, dt=F32):
            return ctx.enter_context(nc.sbuf_tensor(name, shape, dt))

        bank = [ctx.enter_context(nc.psum_tensor(f"bank{i}", [P, 512], F32)) for i in range(8)]

        ident = sb("ident", [P, P])
        earlier = sb("earlier", [P, G, G * P])
        scrap_row = sb("scrap_row", [P, G])
        src_g, dst_g = sb("src_g", [P, TILES], I32), sb("dst_g", [P, TILES], I32)
        src_g2, dst_g2 = sb("src_g2", [P, TILES], I32), sb("dst_g2", [P, TILES], I32)
        src_key, dst_key = sb("src_key", [P, TILES]), sb("dst_key", [P, TILES])
        src_put, dst_put = sb("src_put", [P, TILES], I32), sb("dst_put", [P, TILES], I32)
        dst_put2 = sb("dst_put2", [P, TILES], I32)
        w_mean, w_edge, w_exp = sb("w_mean", [P, TILES]), sb("w_edge", [P, TILES]), sb("w_exp", [P, TILES])
        w_one = sb("w_one", [P, TILES])
        edge_kv = sb("edge_kv", [P, TILES, 2 * EF])
        degree = sb("degree", [P, CHUNKS * R])
        self_exp = sb("self_exp", [P, CHUNKS * R])
        rho = sb("rho", [P, CHUNKS * R])
        w_self = sb("w_self", [P, D])
        w_gate = [sb(f"w_gate{i}", [P, P]) for i in (1, 2)]
        w_mix = [sb(f"w_mix{i}", [P, D]) for i in (1, 2)]
        w_att = sb("w_att", [P, 196])
        w_att_out = sb("w_att_out", [P, D])
        w_out = sb("w_out", [P, P])
        w_sage = [sb(f"w_sage{i}", [D + 1, D]) for i in (1, 2)]
        rows = sb("rows", [P, 10, D])
        B_MEAN, B_MIX1, B_MIX2, B_CEN, B_VL, B_OUT, B_LNG, B_LNB, B_TMP, B_TMP2 = range(10)
        half, eps, minus_big = sb("half", [P, 1]), sb("eps", [P, 1]), sb("minus_big", [P, 1])
        st = dict(locals())

        prepare_weights(nc, a, st)
        prepare_edges(nc, a, st)

        mean_and_weight_max(nc, a, st)
        dense_mean(nc, a, st)
        gated_sums(nc, st, "g1", gate1_tab, w_gate[0])
        dense_gate(nc, st, "dg1", gate1_tab, 0, None, gate2_tab)
        gated_sums(nc, st, "g2", gate2_tab, w_gate[1])
        dense_gate(nc, st, "dg2", gate2_tab, 1, gate1_tab, attn_x)
        attention_sums(nc, st)
        dense_attention(nc, st)
        sage_sums(nc, st, "s1", sage1_tab)
        dense_sage(nc, st, "ds1", sage1_tab, 0, None, sage2_tab)
        sage_sums(nc, st, "s2", sage2_tab)
        dense_sage(nc, st, "ds2", sage2_tab, 1, sage1_tab, out)


class Phase:

    def __init__(self, nc, tag):
        self.nc, self.tag, self.ctx, self.all_sems = nc, tag, ExitStack(), []
        self.passed = self.sem("passed")

    def __enter__(self):
        return self

    def __exit__(self, *e):
        self.ctx.__exit__(*e)
        self.nc.clear_and_free_semaphores(self.all_sems)
        self.nc.all_engine_barrier()

    def sb(self, name, shape, dt=F32):
        return self.ctx.enter_context(self.nc.sbuf_tensor(f"{self.tag}_{name}", shape, dt))

    def sem(self, name):
        self.all_sems.append(self.nc.alloc_semaphore(f"{self.tag}_{name}"))
        return self.all_sems[-1]

    def sems(self, names):
        return [self.sem(n) for n in names.split()]


def prepare_weights(nc, a, st):
    ident, rows, bank = st["ident"], st["rows"], st["bank"]
    R_ = {k: st[k] for k in st if k.startswith("B_")}
    with Phase(nc, "pw") as ph:
        sem = ph.sem
        names = ["self", "neigh", "ws1", "wl1", "ws2", "wl2", "lin1", "w1", "lin2", "w2"]
        drams = ["L0_gnn_W_self", "L0_gnn_W_neigh", "L1_gnn_Ws1", "L1_gnn_Wl1", "L1_gnn_Ws2", "L1_gnn_Wl2",
                 "L3_gnn_lin1_w", "L3_gnn_W1", "L3_gnn_lin2_w", "L3_gnn_W2"]
        W = {n: ph.sb(n, [D, D]) for n in names}
        BQ, BK, BV, BWL, BVL = (ph.sb(n, [D, D]) for n in ("bq", "bk", "bv", "bwl", "bvl"))
        CR, OW = ph.sb("cr", [D, D]), ph.sb("ow", [D, D])
        SA = ph.sb("sa", [D, D])
        cols = ph.sb("cols", [D, 8])
        headc = ph.sb("headc", [D, H])
        loaded, zeroed, made, mm, ev, idz = (sem(n) for n in ("loaded", "zeroed", "made", "mm", "ev", "idz"))
        block = ph.ctx.enter_context(nc.Block())
        col_names = ["L1_gnn_b1", "L1_gnn_b2", "L3_gnn_lin1_b", "L3_gnn_lin2_b", "L2_gnn_out_b"]
        row_names = [("L0_gnn_b_self", R_["B_TMP"]), ("L0_gnn_b_neigh", R_["B_TMP2"]), ("L1_gnn_bl1", R_["B_MIX1"]),
                     ("L1_gnn_bl2", R_["B_MIX2"]), ("L2_gnn_cen_b", R_["B_CEN"]),
                     ("L2_gnn_ln_g", R_["B_LNG"]), ("L2_gnn_ln_b", R_["B_LNB"])]
        n_loads = [0]

        @block.sync
        def _(sp):
            def load(dst, src):
                sp.dma_start(dst, src).then_inc(loaded, 16)
                n_loads[0] += 16

            for n, d in zip(names, drams):
                load(W[n][:], a[d])
            for k, n in enumerate(col_names):
                load(cols[:, k:k + 1], a[n].unsqueeze(1))
            for n, k in row_names:
                load(rows[:, k, :], a[n].unsqueeze(0).broadcast_to([P, D]))
            for i in (1, 2):
                wg = st["w_gate"][i - 1]
                load(wg[0:D, 0:D], a[f"L1_gnn_Wk{i}"])
                load(wg[D:P, 0:D], a[f"L1_gnn_Wq{i}"])
                load(wg[D:P, D:P], a[f"L1_gnn_Wv{i}"])
            load(st["w_att_out"][0:D, :], a["L2_gnn_cen_w"])
            load(OW[:], a["L2_gnn_out_w"])
            sp.wait_ge(zeroed, 1)
            for h in range(H):
                o = slice(h * DH, (h + 1) * DH)
                load(BQ[o, o], a["L2_gnn_Wq"][h])
                load(BK[o, o], a["L2_gnn_Wk"][h])
                load(BV[o, o], a["L2_gnn_Wv"][h])
                load(BWL[o, o], a["L2_gnn_wkl_w"])
                load(BVL[o, o], a["L2_gnn_wvl_w"])
                load(headc[o, h:h + 1], a["L2_gnn_wkl_b"].unsqueeze(1))
                load(rows[:, R_["B_VL"], o], a["L2_gnn_wvl_b"].unsqueeze(0).broadcast_to([P, DH]))

        @block.gpsimd
        def _(pool):
            nc.gpsimd.memset(ident[:], 0.0).then_inc(idz, 1)
            pool.wait_ge(idz, 1)
            nc.gpsimd.affine_select(out=ident[:], in_=ident[:], compare_op=ALU.not_equal, fill=1.0, base=0,
                                    pattern=[[-1, P]], channel_multiplier=1).then_inc(idz, 1)

        evac = [0]

        @block.vector
        def _(dve):
            for t in (BQ[:], BK[:], BV[:], BWL[:], BVL[:], headc[:], st["w_gate"][0][0:D, D:P],
                      st["w_gate"][1][0:D, D:P], st["w_att"][:], st["w_out"][:]):
                ins = nc.vector.memset(t, 0.0)
            nc.vector.memset(st["half"][:], 0.5)
            nc.vector.memset(st["eps"][:], LN_EPS)
            nc.vector.memset(st["minus_big"][:], -BIG)
            ins = nc.vector.memset(CR[:], -1.0 / D)
            ins.then_inc(zeroed, 1)
            dve.wait_ge(zeroed, 1)
            dve.wait_ge(idz, 2)
            dve.wait_ge(loaded, n_loads[0])
            nc.vector.tensor_tensor(CR[:], CR[:], ident[0:D, 0:D], ALU.add).then_inc(made, 1)
            nc.vector.tensor_tensor(rows[:, R_["B_TMP"], :], rows[:, R_["B_TMP"], :], rows[:, R_["B_TMP2"], :],
                                    ALU.add).then_inc(made, 1)
            dve.wait_ge(made, 2)
            nc.vector.reduce_sum(rows[:, R_["B_TMP2"], 0:1], rows[:, R_["B_TMP"], :], AX_X).then_inc(made, 1)
            dve.wait_ge(made, 3)
            nc.vector.tensor_scalar(rows[:, R_["B_TMP2"], 1:2], rows[:, R_["B_TMP2"], 0:1], -1.0 / D, None,
                                    ALU.mult).then_inc(made, 1)
            dve.wait_ge(made, 4)
            nc.vector.tensor_scalar(rows[:, R_["B_MEAN"], :], rows[:, R_["B_TMP"], :],
                                    rows[:, R_["B_TMP2"], 1:2], None, ALU.add).then_inc(made, 1)

            def take(dst, src, add=None, scale=None):
                evac[0] += 1
                dve.wait_ge(mm, evac[0])
                if add is not None:
                    ins = nc.vector.tensor_tensor(dst, src, add, ALU.add)
                elif scale is not None:
                    ins = nc.vector.tensor_scalar(dst, src, scale, None, ALU.mult)
                else:
                    ins = nc.vector.tensor_copy(dst, src)
                ins.then_inc(ev, 1)

            b = bank[0]
            take(SA[:], b[0:D, 0:D], add=ident[0:D, 0:D])
            take(st["w_self"][0:D, :], b[0:D, 0:D])
            take(st["w_self"][D:P, :], b[0:D, 0:D])
            for i in (0, 1):
                take(SA[:], b[0:D, 0:D])
                take(st["w_mix"][i][0:D, :], b[0:D, 0:D])
                take(st["w_mix"][i][D:P, :], b[0:D, 0:D])
                bi = R_["B_MIX1"] + i
                take(rows[:, bi, :], b[:, 0:D], add=rows[:, bi, :])
            for i in (0, 1):
                take(st["w_sage"][i][0:D, :], b[0:D, 0:D])
                take(st["w_sage"][i][D:D + 1, :], b[0:1, 0:D])
            take(SA[:], b[0:D, 0:D])
            take(st["w_att"][D:P, 0:D], b[0:D, 0:D], scale=0.25)
            take(st["w_att"][D:P, D:D + H], b[0:D, 0:H], scale=0.25)
            take(st["w_att"][0:D, D + H:2 * D + H], b[0:D, 0:D])
            take(st["w_att"][0:D, 2 * D + H:3 * D + H], b[0:D, 0:D])
            take(st["w_att_out"][D:P, :], b[0:D, 0:D])
            take(SA[:], b[0:D, 0:D])
            take(st["w_out"][0:D, 0:D], b[0:D, 0:D])
            take(st["w_out"][D:P, D:P], b[0:D, 0:D])
            take(rows[:, R_["B_OUT"], :], b[:, 0:D])

        @block.tensor
        def _(pe):
            n = [0]
            b = bank[0]
            pe.wait_ge(made, 5)

            def mul(out, lhsT, rhs):
                if n[0]:
                    pe.wait_ge(ev, n[0])
                nc.tensor.matmul(out, lhsT, rhs, start=True, stop=True).then_inc(mm, 1)
                n[0] += 1

            idn = ident[0:D, 0:D]
            mul(b[0:D, 0:D], idn, W["self"][:])
            mul(b[0:D, 0:D], SA[:], CR[:])
            mul(b[0:D, 0:D], W["neigh"][:], CR[:])
            for i in (1, 2):
                mul(b[0:D, 0:D], W[f"ws{i}"][:], idn)
                mul(b[0:D, 0:D], SA[:], W[f"wl{i}"][:])
                mul(b[0:D, 0:D], idn, W[f"wl{i}"][:])
                mul(b[:, 0:D], cols[:, i - 1:i].broadcast_to([D, P]), W[f"wl{i}"][:])
            for i in (1, 2):
                mul(b[0:D, 0:D], W[f"lin{i}"][:], W[f"w{i}"][:])
                mul(b[:, 0:D], cols[:, i + 1:i + 2].broadcast_to([D, P]), W[f"w{i}"][:])
            mul(b[0:D, 0:D], BWL[:], idn)
            mul(b[0:D, 0:D], BQ[:], SA[:])
            mul(b[0:D, 0:H], BQ[:], headc[:])
            mul(b[0:D, 0:D], BK[:], idn)
            mul(b[0:D, 0:D], BV[:], idn)
            mul(b[0:D, 0:D], idn, BVL[:])
            mul(b[0:D, 0:D], OW[:], idn)
            mul(b[0:D, 0:D], SA[:], CR[:])
            mul(b[0:D, 0:D], SA[:], CR[:])
            mul(b[:, 0:D], cols[:, 4:5].broadcast_to([D, P]), CR[:])


def prepare_edges(nc, a, st):
    FULL, REST, BLOCKS, TILES, N, NT = (st[k] for k in ("FULL", "REST", "BLOCKS", "TILES", "N", "NT"))
    bank, ident, earlier = st["bank"], st["ident"], st["earlier"]
    with Phase(nc, "pe") as ph:
        sem = ph.sem
        src_i, dst_i = ph.sb("src_i", [P, TILES], I32), ph.sb("dst_i", [P, TILES], I32)
        iota_i = ph.sb("iota_i", [P, G], I32)
        ZR = 32
        init = ph.sb("init", [P, ZR, 72])
        init_m = ph.sb("init_m", [P, ZR, 66])
        cleared, loaded, masks, inited, stored = ph.sems("cleared loaded masks inited stored")
        block = ph.ctx.enter_context(nc.Block())
        n_loads = [0]

        @block.sync
        def _(sp):
            sp.wait_ge(cleared, 1)
            for dst, name in ((src_i, "src"), (st["src_g"], "src"), (dst_i, "dst"), (st["dst_g"], "dst"),
                              (st["w_mean"], "edge_weight1"), (st["w_edge"], "edge_weight")):
                v = a[name] if len(a[name].shape) == 1 else a[name].rearrange("e o -> (e o)")
                sp.dma_start(dst[0:FULL, :], v[0:FULL * TILES].rearrange("(p t) -> p t", t=TILES)).then_inc(loaded, 16)
                n_loads[0] += 16
                if REST:
                    sp.dma_start(dst[FULL:FULL + 1, 0:REST], v[FULL * TILES:E_of(a)].unsqueeze(0)).then_inc(loaded, 16)
                    n_loads[0] += 16

            sp.wait_ge(inited, 1)
            n = [0]

            def fill(tab, src, width, rows):
                per = rows // P
                body = tab[0:per * P].rearrange("(p r) w -> p (r w)", p=P)
                for r in range(0, per, ZR):
                    k = min(ZR, per - r)
                    sp.dma_start(body[:, r * width:(r + k) * width],
                                 src[:, 0:k, :].rearrange("p r w -> p (r w)")).then_inc(stored, 16)
                    n[0] += 16
                if rows > per * P:
                    sp.dma_start(tab[per * P:rows], src[0:rows - per * P, 0, :]).then_inc(stored, 16)
                    n[0] += 16

            fill(st["mean_tab"], init_m, 66, NT)
            fill(st["attn_tab"], init, 72, NT)
            for tab, width in ((st["gate1_tab"], D), (st["gate2_tab"], D), (st["sage1_tab"], 65),
                               (st["sage2_tab"], 65)):
                v = tab[2 * N:2 * NT].rearrange("(p r) w -> p r w", p=P)
                sp.dma_start(v, init[:, 0:2 * SCRAP // P, 0:width]).then_inc(stored, 16)
                n[0] += 16
            sp.wait_ge(stored, n[0])

        @block.gpsimd
        def _(pool):
            nc.gpsimd.memset(earlier[:], 1.0).then_inc(masks, 1)
            nc.gpsimd.iota(iota_i[:], pattern=[[P, G]], base=N, channel_multiplier=1).then_inc(masks, 1)
            pool.wait_ge(masks, 1)
            for q in range(G):
                nc.gpsimd.affine_select(out=earlier[:, q, :], in_=earlier[:, q, :], compare_op=ALU.is_gt,
                                        fill=0.0, base=q * P, pattern=[[-1, G * P]],
                                        channel_multiplier=1).then_inc(masks, 1)

        @block.vector
        def _(dve):
            for t, v in ((src_i, N + G * P), (dst_i, N + G * P), (st["src_g"], 0), (st["dst_g"], 0),
                         (st["w_mean"], 0.0), (st["w_edge"], 0.0)):
                ins = nc.vector.memset(t[:], v)
            nc.vector.memset(st["w_one"][:], 1.0)
            ins = nc.vector.memset(init[:], 0.0)
            ins.then_inc(cleared, 1)
            dve.wait_ge(cleared, 1)
            nc.vector.memset(init[:, :, 68:72], -BIG)
            nc.vector.memset(init_m[:, :, 0:65], 0.0)
            nc.vector.memset(init_m[:, :, 65:66], 1.0).then_inc(inited, 1)
            dve.wait_ge(loaded, n_loads[0])
            dve.wait_ge(masks, 2)
            nc.vector.tensor_copy(st["scrap_row"][:], iota_i[:])
            nc.vector.tensor_copy(st["src_key"][:], src_i[:])
            nc.vector.tensor_copy(st["dst_key"][:], dst_i[:])
            nc.vector.tensor_scalar(st["src_g2"][:], st["src_g"][:], 2.0, None, ALU.mult)
            nc.vector.tensor_scalar(st["dst_g2"][:], st["dst_g"][:], 2.0, None, ALU.mult)


def E_of(a):
    return a["src"].shape[0]


class Blocks:

    def __init__(self, nc, ph, st, key, width):
        self.nc, self.st, self.key, self.width = nc, st, key, width
        self.keys = [ph.sb(f"keys{s}", [P, G]) for s in (0, 1)]
        self.match = [ph.sb(f"match{s}", [P, G, G * P]) for s in (0, 1)]
        self.payload = [ph.sb(f"payload{s}", [P, G, width]) for s in (0, 1)]

    def turn_keys(self, bank, s):
        for q in range(G):
            ins = self.nc.tensor.transpose(bank[:, q * P:(q + 1) * P],
                                           self.keys[s][:, q:q + 1].broadcast_to([P, P]), self.st["ident"][:])
        return ins

    def make_match(self, bank, s):
        for q in range(G):
            ins = self.nc.vector.tensor_scalar(self.match[s][:, q, :], bank[:], self.keys[s][:, q:q + 1], None,
                                               ALU.is_equal)
        return ins

    def segment_sums(self, bank, s):
        w = self.width
        for u in range(G):
            for t in range(G):
                ins = self.nc.tensor.matmul(bank[:, u * w:(u + 1) * w], self.match[s][:, t, u * P:(u + 1) * P],
                                            self.payload[s][:, t, :], start=(t == 0), stop=(t == G - 1))
        return ins

    def stage(self, n, s, copies):
        cols = bass.ds(n * G, G)
        ins = self.nc.vector.tensor_copy(self.keys[s][:], self.key[:, cols])
        for dst, src in copies:
            ins = self.nc.vector.tensor_copy(dst[:], src[:, cols])
        return ins


class Leaders:

    def __init__(self, nc, ph, st, tag):
        self.nc, self.st = nc, st
        self.before, self.lead, self.diff = (ph.sb(f"{tag}_{n}", [P, G]) for n in ("before", "lead", "diff"))
        self.junk = ph.sb(f"{tag}_junk", [P, G, G * P])

    STEPS = 4

    def find(self, steps, match, keys, outs):
        nc, scrap = self.nc, self.st["scrap_row"]
        for q in range(G):
            w = (q + 1) * P
            ins = nc.vector.tensor_tensor_reduce(self.junk[:, q, 0:w], match[:, q, 0:w], self.st["earlier"][:, q, 0:w],
                                                 1.0, 0.0, ALU.mult, ALU.add, self.before[:, q:q + 1])
        steps.then(ins)
        steps.then(nc.vector.tensor_scalar(self.lead[:], self.before[:], 0.0, None, ALU.is_equal))
        steps.then(nc.vector.tensor_tensor(self.diff[:], keys[:], scrap[:], ALU.subtract))
        steps.then(nc.vector.tensor_tensor(self.diff[:], self.diff[:], self.lead[:], ALU.mult))
        for dst in outs:
            ins = nc.vector.tensor_tensor(dst, self.diff[:], scrap[:], ALU.add)
        return ins


def gather_rows(nc, out_cols, table, index, sem, passed):
    hold(nc.gpsimd, passed)
    for dst, q in out_cols:
        nc.gpsimd.indirect_dma_start(dst, None, table, bass.IndirectOffsetOnAxis(ap=index[:, q:q + 1], axis=0)
                                     ).then_inc(sem, 16)


def mean_and_weight_max(nc, a, st):
    BLOCKS, bank, x = st["BLOCKS"], st["bank"], a["x"]
    with Phase(nc, "mean") as ph:
        bl = Blocks(nc, ph, st, st["dst_key"], 65)
        ld = Leaders(nc, ph, st, "dst")
        xs = [ph.sb(f"xs{s}", [P, G, D]) for s in (0, 1)]
        state, new = ([ph.sb(f"{n}{s}", [P, G, 66]) for s in (0, 1)] for n in ("state", "new"))
        weight = [ph.sb(f"weight{s}", [P, G]) for s in (0, 1)]
        src_i, dst_i, put_i = ([ph.sb(f"{n}{s}", [P, G], I32) for s in (0, 1)] for n in ("src_i", "dst_i", "put_i"))
        top, junk = ph.sb("top", [P, G]), ph.sb("junk", [P, G, G * P])
        staged, turned, matched, paid, summed, topped, updated, chain = ph.sems(
            "staged turned matched paid summed topped updated chain")
        gathered, state_in, scattered = ([ph.sem(f"{n}{s}") for s in (0, 1)] for n in
                                         ("gathered", "state_in", "scattered"))
        mlp = EdgeMlp(nc, a, ph, st)
        block = ph.ctx.enter_context(nc.Block())
        key_t, weight_t, sums = bank[0:2], bank[2:4], bank[4:6]

        @block.sync
        def _(sp):
            mlp.load(sp)

        @block.gpsimd
        def _(pool):
            def x_rows(i, s, part):
                gather_rows(nc, [(xs[s][:, q, :], q) for q in part], x, src_i[s], gathered[s], ph.passed)

            def step(n, i, s, first, last):
                more = not (last and s == 1)
                if more:
                    pool.wait_ge(staged, n + 2)
                    if not n_is(n, 0, first):
                        pool.wait_ge(paid, n)
                    x_rows(i, 1 - s, (0, 1))
                if not (first and s == 0):
                    pool.wait_ge(scattered[1 - s], 64 * last_use(i, s))
                gather_rows(nc, [(state[s][:, q, :], q) for q in range(G)], st["mean_tab"], dst_i[s], state_in[s], ph.passed)
                if more:
                    x_rows(i, 1 - s, (2, 3))
                pool.wait_ge(updated, n + 1)
                hold(pool, ph.passed)
                for q in range(G):
                    nc.gpsimd.indirect_dma_start(
                        st["mean_tab"], bass.IndirectOffsetOnAxis(ap=put_i[s][:, q:q + 1], axis=0),
                        new[s][:, q, :], None).then_inc(scattered[s], 16)

            pool.wait_ge(staged, 1)
            x_rows(0, 0, range(G))
            over_pairs(pool, BLOCKS, step)
            for s in (0, 1):
                pool.wait_ge(scattered[s], 64 * (BLOCKS // 2))

        @block.vector
        def _(dve):
            steps = Steps(dve, chain, Leaders.STEPS)

            def stage(n, s):
                bl.stage(n, s, ((weight[s], st["w_edge"]), (src_i[s], st["src_g"]), (dst_i[s], st["dst_g"]))
                         ).then_inc(staged, 1)

            def step(n, i, s, first, last):
                steps.turn(n)
                dve.wait_ge(turned, n + 1)
                if not first:
                    dve.wait_ge(summed, n - 1)
                bl.make_match(key_t[s], s).then_inc(matched, 1)
                dve.wait_ge(gathered[s], 64 * (i + 1))
                nc.vector.tensor_tensor(bl.payload[s][:, :, 0:D], xs[s][:],
                                        bcast(st["w_mean"][:, bass.ds(n * G, G)], D), ALU.mult).then_inc(paid, 1)
                dve.wait_ge(matched, n + 1)
                hold(dve, ph.passed)
                for q in range(G):
                    ins = nc.vector.tensor_tensor_reduce(junk[:, q, :], bl.match[s][:, q, :], weight_t[s][:], 1.0, 1.0,
                                                         ALU.mult, ALU.max, top[:, q:q + 1])
                ins.then_inc(topped, 1)
                if not first:
                    dve.wait_ge(scattered[s], 64 * i)
                ld.find(steps, bl.match[s], bl.keys[s], (
                    put_i[s][:], st["dst_put"][:, bass.ds(n * G, G)]))
                steps.end()
                mlp.vector(dve, i, s, first)
                dve.wait_ge(summed, n + 1)
                dve.wait_ge(state_in[s], 64 * (i + 1))
                dve.wait_ge(topped, n + 1)
                nc.vector.tensor_tensor(new[s][:, :, 0:65], sums[s][:, 0:G * 65].rearrange("p (t w) -> p t w", w=65),
                                        state[s][:, :, 0:65], ALU.add)
                nc.vector.tensor_tensor(new[s][:, :, 65], state[s][:, :, 65], top[:], ALU.max).then_inc(updated, 1)
                if not last:
                    stage(n + 2, s)

            mlp.clear(dve)
            for s in (0, 1):
                nc.vector.memset(bl.payload[s][:], 1.0)
                stage(s, s)
            over_pairs(dve, BLOCKS, step)
            mlp.last_keep(dve)
            nc.vector.tensor_scalar(st["dst_put2"][:], st["dst_put"][:], 2.0, 1.0, ALU.mult, ALU.add)

        @block.scalar
        def _(act):
            act.preload_act_table_set("natural_log_exp_and_others")

            def step(n, i, s, first, last):
                mlp.scalar(act, i, s, first)

            over_pairs(act, BLOCKS, step)

        @block.tensor
        def _(pe):
            def turn(n, s):
                pe.wait_ge(staged, n + 1)
                bl.turn_keys(key_t[s], s)
                for q in range(G):
                    ins = nc.tensor.transpose(weight_t[s][:, q * P:(q + 1) * P],
                                              weight[s][:, q:q + 1].broadcast_to([P, P]), st["ident"][:])
                ins.then_inc(turned, 1)

            def step(n, i, s, first, last):
                if not (last and s == 1):
                    turn(n + 1, 1 - s)
                mlp.tensor_before(pe, i, s, first)
                pe.wait_ge(matched, n + 1)
                pe.wait_ge(paid, n + 1)
                if not first:
                    pe.wait_ge(updated, n - 1)
                bl.segment_sums(sums[s], s).then_inc(summed, 1)
                mlp.tensor_after(pe, i, s, first)

            turn(0, 0)
            over_pairs(pe, BLOCKS, step)


def n_is(n, value, first):
    return first and n == value


class EdgeMlp:

    def __init__(self, nc, a, ph, st):
        self.nc, self.a, self.st = nc, a, st
        assert GT == 2 * G
        self.attr = ph.sb("attr", [P, st["TILES"] * EF])
        self.w1, self.w2 = ph.sb("mlp_w1", [P, 2, P]), ph.sb("mlp_w2", [P, 2, P])
        self.b1, self.b2 = ph.sb("mlp_b1", [P, 2]), ph.sb("mlp_b2", [P, GT, 2, EF])
        self.stage_t, self.attr_t = ph.sb("mlp_stage", [P, P]), ph.sb("mlp_attr_t", [P, P])
        self.z, self.e, self.soft = (ph.sb(f"mlp_{n}", [P, 2, P]) for n in ("z", "e", "soft"))
        (self.cleared, self.loaded, self.staged, self.turned, self.copied, self.first_mm, self.z_done, self.ln_done,
         self.soft_done, self.second_mm, self.kept, self.chain) = ph.sems(
            "mcleared mloaded mstaged mturned mcopied mfirst_mm mz_done mln_done msoft_done msecond_mm mkept mchain")
        self.loads = 0

    def load(self, sp):
        st, a = self.st, self.a
        FULL, REST, TILES = st["FULL"], st["REST"], st["TILES"]

        def load(dst, src):
            sp.dma_start(dst, src).then_inc(self.loaded, 16)
            self.loads += 16

        sp.wait_ge(self.cleared, 1)
        v = a["edge_attr_16"]
        load(self.attr[0:FULL, :], v[0:FULL * TILES].rearrange("(p t) f -> p (t f)", t=TILES))
        if REST:
            load(self.attr[FULL:FULL + 1, 0:REST * EF], v[FULL * TILES:E_of(a)].rearrange("(o t) f -> o (t f)", o=1))
        for t in range(GT):
            o = slice(t * EF, (t + 1) * EF)
            for k, n in ((0, "k"), (1, "v")):
                load(self.w1[o, k, o], a[f"L2_gnn_w{n}1_w"])
                load(self.w2[o, k, o], a[f"L2_gnn_w{n}2_w"])
                load(self.b1[o, k:k + 1], a[f"L2_gnn_w{n}1_b"].unsqueeze(1))
                load(self.b2[:, t, k, :], a[f"L2_gnn_w{n}2_b"].unsqueeze(0).broadcast_to([P, EF]))

    def clear(self, dve):
        nc = self.nc
        nc.vector.memset(self.w1[:], 0.0)
        nc.vector.memset(self.w2[:], 0.0)
        nc.vector.memset(self.attr[:], 0.0).then_inc(self.cleared, 1)

    def vector(self, dve, g, s, first):
        nc, bank = self.nc, self.st["bank"]
        if s == 0:
            if first:
                dve.wait_ge(self.loaded, self.loads)
            else:
                dve.wait_ge(self.turned, g)
            nc.vector.tensor_copy(self.stage_t[:], self.attr[:, bass.ds(g * P, P)]).then_inc(self.staged, 1)
            if not first:
                dve.wait_ge(self.second_mm, g)
                self.keep(g - 1)
        else:
            dve.wait_ge(self.ln_done, g + 1)
            nc.vector.scalar_tensor_tensor(out=self.soft[:], in0=self.z[:], scalar=0.0, in1=self.e[:], op0=ALU.max,
                                           op1=ALU.add).then_inc(self.soft_done, 1)

    def keep(self, g):
        bank = self.st["bank"][6]
        for k in (0, 1):
            ins = self.nc.vector.tensor_tensor(
                self.st["edge_kv"][:, bass.ds(g * GT, GT), k * EF:(k + 1) * EF],
                bank[:, k * P:(k + 1) * P].rearrange("p (t f) -> p t f", f=EF), self.b2[:, :, k, :], ALU.add)
        ins.then_inc(self.kept, 1)

    def scalar(self, act, g, s, first):
        nc, bank = self.nc, self.st["bank"]
        if s == 0:
            act.wait_ge(self.turned, g + 1)
            nc.scalar.activation(self.attr_t[:], bank[7][:, 2 * P:3 * P], ACT.Copy).then_inc(self.copied, 1)
        else:
            act.wait_ge(self.first_mm, g + 1)
            if not first:
                act.wait_ge(self.soft_done, g)
            for k in (0, 1):
                ins = nc.scalar.activation(self.z[:, k, :], bank[7][:, k * P:(k + 1) * P], ACT.Identity,
                                           bias=self.b1[:, k:k + 1])
            ins.then_inc(self.z_done, 1)
            act.wait_ge(self.z_done, g + 1)
            nc.scalar.activation(self.e[:], self.z[:], ACT.Abs).then_inc(self.chain, 1)
            act.wait_ge(self.chain, g * 2 + 1)
            nc.scalar.activation(self.e[:], self.e[:], ACT.Exp, scale=-1.0).then_inc(self.chain, 1)
            act.wait_ge(self.chain, g * 2 + 2)
            nc.scalar.activation(self.e[:], self.e[:], ACT.Ln, bias=self.st["half"][:], scale=0.5
                                 ).then_inc(self.ln_done, 1)

    def tensor_before(self, pe, g, s, first):
        nc, bank = self.nc, self.st["bank"]
        if s == 0:
            pe.wait_ge(self.staged, g + 1)
            if not first:
                pe.wait_ge(self.z_done, g)
            nc.tensor.transpose(bank[7][:, 2 * P:3 * P], self.stage_t[:], self.st["ident"][:]).then_inc(self.turned, 1)

    def tensor_after(self, pe, g, s, first):
        nc, bank = self.nc, self.st["bank"]
        if s == 0:
            pe.wait_ge(self.copied, g + 1)
            for k in (0, 1):
                ins = nc.tensor.matmul(bank[7][:, k * P:(k + 1) * P], self.w1[:, k, :], self.attr_t[:], start=True,
                                       stop=True)
            ins.then_inc(self.first_mm, 1)
        else:
            pe.wait_ge(self.soft_done, g + 1)
            if not first:
                pe.wait_ge(self.kept, g)
            for k in (0, 1):
                ins = nc.tensor.matmul(bank[6][:, k * P:(k + 1) * P], self.soft[:, k, :], self.w2[:, k, :], start=True,
                                       stop=True)
            ins.then_inc(self.second_mm, 1)

    def last_keep(self, dve):
        dve.wait_ge(self.second_mm, self.st["BLOCKS"] // 2)
        self.keep(self.st["BLOCKS"] // 2 - 1)


def gated_sums(nc, st, tag, table, weight):
    BLOCKS, bank, ident = st["BLOCKS"], st["bank"], st["ident"]
    lead = tag == "g1"
    with Phase(nc, tag) as ph:
        bl = Blocks(nc, ph, st, st["dst_key"], D)
        ends = [ph.sb(f"ends{s}", [P, G, P]) for s in (0, 1)]
        ends_t = [ph.sb(f"ends_t{s}", [P, G * P]) for s in (0, 1)]
        gate = [ph.sb(f"gate{s}", [P, G, D]) for s in (0, 1)]
        sums_sb = [ph.sb(f"sums_sb{s}", [P, G * D]) for s in (0, 1)]
        src_i, dst_i, put_i = ([ph.sb(f"{n}{s}", [P, G], I32) for s in (0, 1)] for n in ("src_i", "dst_i", "put_i"))
        (staged, turned, matched, ends_turned, ends_copied, produced, gated, paid, summed, copied) = ph.sems(
            "staged turned matched ends_turned ends_copied produced gated paid summed copied")
        gathered, scattered = ([ph.sem(f"{n}{s}") for s in (0, 1)] for n in ("gathered", "scattered"))
        key_t, ends_b, kqv_b, sums = bank[0:2], bank[2], bank[3:5], bank[5:7]
        if lead:
            src_keys = ph.sb("src_keys", [P, G])
            src_match = ph.sb("src_match", [P, G, G * P])
            ld = Leaders(nc, ph, st, "src")
            src_staged, src_turned, chain = ph.sems("src_staged src_turned chain")
        block = ph.ctx.enter_context(nc.Block())

        @block.gpsimd
        def _(pool):
            def rows_of(s):
                gather_rows(nc, [(ends[s][:, q, 0:D], q) for q in range(G)], table, dst_i[s], gathered[s], ph.passed)
                gather_rows(nc, [(ends[s][:, q, D:P], q) for q in range(G)], table, src_i[s], gathered[s], ph.passed)

            def step(n, i, s, first, last):
                if not (last and s == 1):
                    pool.wait_ge(staged, n + 2)
                    if not n_is(n, 0, first):
                        pool.wait_ge(ends_turned, n)
                    rows_of(1 - s)
                pool.wait_ge(copied, n + 1)
                if not (first and s == 0):
                    pool.wait_ge(scattered[1 - s], 64 * last_use(i, s))
                hold(pool, ph.passed)
                for q in range(G):
                    nc.gpsimd.indirect_dma_start(
                        table, bass.IndirectOffsetOnAxis(ap=put_i[s][:, q:q + 1], axis=0),
                        sums_sb[s][:, q * D:(q + 1) * D], None, compute_op=ALU.add).then_inc(scattered[s], 16)

            pool.wait_ge(staged, 1)
            rows_of(0)
            over_pairs(pool, BLOCKS, step)
            for s in (0, 1):
                pool.wait_ge(scattered[s], 64 * (BLOCKS // 2))

        @block.vector
        def _(dve):
            if lead:
                steps = Steps(dve, chain, Leaders.STEPS + 1)

            def stage(n, s):
                bl.stage(n, s, ((src_i[s], st["src_g2"]), (dst_i[s], st["dst_g2"]))).then_inc(staged, 1)

            def step(n, i, s, first, last):
                dve.wait_ge(turned, n + 1)
                if not first:
                    dve.wait_ge(summed, n - 1)
                bl.make_match(key_t[s], s).then_inc(matched, 1)
                dve.wait_ge(gated, n + 1)
                nc.vector.tensor_tensor(bl.payload[s][:], gate[s][:],
                                        kqv_b[s][:].rearrange("p (t w) -> p t w", w=P)[:, :, D:P], ALU.mult
                                        ).then_inc(paid, 1)
                if lead:
                    steps.turn(n)
                    dve.wait_ge(src_turned, n + 1)
                    for q in range(G):
                        w = (q + 1) * P
                        ins = nc.vector.tensor_scalar(src_match[:, q, 0:w], bank[7][:, 0:w], src_keys[:, q:q + 1],
                                                      None, ALU.is_equal)
                    steps.then(ins)
                    ld.find(steps, src_match, src_keys, (st["src_put"][:, bass.ds(n * G, G)],))
                    steps.end()
                    if not (last and s == 1):
                        nc.vector.tensor_copy(src_keys[:], st["src_key"][:, bass.ds(n * G + G, G)]
                                              ).then_inc(src_staged, 1)
                if not last:
                    dve.wait_ge(matched, n + 1)
                    stage(n + 2, s)

            if lead:
                nc.vector.tensor_copy(src_keys[:], st["src_key"][:, 0:G]).then_inc(src_staged, 1)
            for s in (0, 1):
                stage(s, s)
            over_pairs(dve, BLOCKS, step)

        @block.scalar
        def _(act):
            def step(n, i, s, first, last):
                act.wait_ge(ends_turned, n + 1)
                if not first:
                    act.wait_ge(produced, n - 1)
                nc.scalar.activation(ends_t[s][:], ends_b[:], ACT.Copy).then_inc(ends_copied, 1)
                act.wait_ge(produced, n + 1)
                if not first:
                    act.wait_ge(paid, n - 1)
                nc.scalar.activation(gate[s][:], kqv_b[s][:].rearrange("p (t w) -> p t w", w=P)[:, :, 0:D],
                                     ACT.Sigmoid).then_inc(gated, 1)
                act.wait_ge(summed, n + 1)
                if not first:
                    act.wait_ge(scattered[s], 64 * i)
                nc.scalar.activation(put_i[s][:], st["dst_put2"][:, bass.ds(n * G, G)], ACT.Copy)
                nc.scalar.activation(sums_sb[s][:], sums[s][:, 0:G * D], ACT.Copy).then_inc(copied, 1)

            over_pairs(act, BLOCKS, step)

        @block.tensor
        def _(pe):
            def turn(n, s):
                pe.wait_ge(staged, n + 1)
                bl.turn_keys(key_t[s], s).then_inc(turned, 1)

            def step(n, i, s, first, last):
                if not (last and s == 1):
                    turn(n + 1, 1 - s)
                pe.wait_ge(gathered[s], 128 * (i + 1))
                if not n_is(n, 0, first):
                    pe.wait_ge(ends_copied, n)
                for q in range(G):
                    ins = nc.tensor.transpose(ends_b[:, q * P:(q + 1) * P], ends[s][:, q, :], ident[:])
                ins.then_inc(ends_turned, 1)
                pe.wait_ge(ends_copied, n + 1)
                if not first:
                    pe.wait_ge(paid, n - 1)
                for q in range(G):
                    ins = nc.tensor.matmul(kqv_b[s][:, q * P:(q + 1) * P], ends_t[s][:, q * P:(q + 1) * P], weight[:],
                                           start=True, stop=True)
                ins.then_inc(produced, 1)
                if lead:
                    pe.wait_ge(src_staged, n + 1)
                    for q in range(G):
                        ins = nc.tensor.transpose(bank[7][:, q * P:(q + 1) * P],
                                                  src_keys[:, q:q + 1].broadcast_to([P, P]), ident[:])
                    ins.then_inc(src_turned, 1)
                pe.wait_ge(matched, n + 1)
                pe.wait_ge(paid, n + 1)
                if not first:
                    pe.wait_ge(copied, n - 1)
                bl.segment_sums(sums[s], s).then_inc(summed, 1)

            turn(0, 0)
            over_pairs(pe, BLOCKS, step)


def sage_sums(nc, st, tag, table):
    BLOCKS, bank = st["BLOCKS"], st["bank"]
    W = D + 1
    with Phase(nc, tag) as ph:
        bl = Blocks(nc, ph, st, st["dst_key"], W)
        xs = [ph.sb(f"xs{s}", [P, G, W]) for s in (0, 1)]
        sums_sb = [ph.sb(f"sums_sb{s}", [P, G * W]) for s in (0, 1)]
        src_i, put_i = ([ph.sb(f"{n}{s}", [P, G], I32) for s in (0, 1)] for n in ("src_i", "put_i"))
        staged, turned, matched, paid, summed, copied = ph.sems("staged turned matched paid summed copied")
        gathered, scattered = ([ph.sem(f"{n}{s}") for s in (0, 1)] for n in ("gathered", "scattered"))
        key_t, sums = bank[0:2], bank[2:4]
        block = ph.ctx.enter_context(nc.Block())

        @block.gpsimd
        def _(pool):
            def rows_of(s):
                gather_rows(nc, [(xs[s][:, q, :], q) for q in range(G)], table, src_i[s], gathered[s], ph.passed)

            def step(n, i, s, first, last):
                if not last:
                    pool.wait_ge(staged, n + 3)
                pool.wait_ge(copied, n + 1)
                if not (first and s == 0):
                    pool.wait_ge(scattered[1 - s], 64 * last_use(i, s))
                hold(pool, ph.passed)
                for q in range(G):
                    nc.gpsimd.indirect_dma_start(
                        table, bass.IndirectOffsetOnAxis(ap=put_i[s][:, q:q + 1], axis=0),
                        sums_sb[s][:, q * W:(q + 1) * W], None, compute_op=ALU.add).then_inc(scattered[s], 16)
                if not last:
                    rows_of(s)

            for s in (0, 1):
                pool.wait_ge(staged, s + 1)
                rows_of(s)
            over_pairs(pool, BLOCKS, step)
            for s in (0, 1):
                pool.wait_ge(scattered[s], 64 * (BLOCKS // 2))

        @block.vector
        def _(dve):
            def stage(n, s):
                bl.stage(n, s, ((src_i[s], st["src_g2"]),)).then_inc(staged, 1)

            def step(n, i, s, first, last):
                w = st["w_exp"][:, bass.ds(n * G, G)]
                dve.wait_ge(turned, n + 1)
                if not first:
                    dve.wait_ge(summed, n - 1)
                bl.make_match(key_t[s], s).then_inc(matched, 1)
                dve.wait_ge(gathered[s], 64 * (i + 1))
                nc.vector.tensor_copy(bl.payload[s][:, :, D], w)
                nc.vector.tensor_tensor(bl.payload[s][:, :, 0:D], xs[s][:, :, 0:D], bcast(w, D), ALU.mult
                                        ).then_inc(paid, 1)
                if not last:
                    dve.wait_ge(matched, n + 1)
                    dve.wait_ge(paid, n + 1)
                    stage(n + 2, s)

            for s in (0, 1):
                stage(s, s)
            over_pairs(dve, BLOCKS, step)

        @block.scalar
        def _(act):
            def step(n, i, s, first, last):
                act.wait_ge(summed, n + 1)
                if not first:
                    act.wait_ge(scattered[s], 64 * i)
                nc.scalar.activation(put_i[s][:], st["dst_put2"][:, bass.ds(n * G, G)], ACT.Copy)
                nc.scalar.activation(sums_sb[s][:], sums[s][:, 0:G * W], ACT.Copy).then_inc(copied, 1)

            over_pairs(act, BLOCKS, step)

        @block.tensor
        def _(pe):
            def turn(n, s):
                pe.wait_ge(staged, n + 1)
                bl.turn_keys(key_t[s], s).then_inc(turned, 1)

            def step(n, i, s, first, last):
                if not (last and s == 1):
                    turn(n + 1, 1 - s)
                pe.wait_ge(matched, n + 1)
                pe.wait_ge(paid, n + 1)
                if not first:
                    pe.wait_ge(copied, n - 1)
                bl.segment_sums(sums[s], s).then_inc(summed, 1)

            turn(0, 0)
            over_pairs(pe, BLOCKS, step)


def first_node(st, n):
    return min(n * CHUNK, st["N"] - CHUNK) if isinstance(n, int) else n * CHUNK


def loads(sp, ph, st, load, used):
    CHUNKS = st["CHUNKS"]

    def step(n, i, s, first, last):
        if there(n + 2, CHUNKS):
            for sem, per in used:
                sp.wait_ge(sem, n * per + per)
                hold(sp, ph.passed)
            load(s, first_node(st, n + 2))

    for s in (0, 1):
        load(s, first_node(st, s))
    over_pairs(sp, CHUNKS, step)


def stores(pool, ph, st, store, ready, stored, beside=None):
    CHUNKS = st["CHUNKS"]

    def step(n, i, s, first, last):
        if beside:
            beside(n, i, s)
        pool.wait_ge(ready, n + 1)
        if not there(n + 1, CHUNKS):
            pool.wait_ge(stored[0], 16 * (i + 1))
        hold(pool, ph.passed)
        store(s, first_node(st, n)).then_inc(stored[s], 16)

    over_pairs(pool, CHUNKS, step)
    for s in (0, 1):
        pool.wait_ge(stored[s], 16 * (CHUNKS // 2))


def table_rows(tab, row, per=1):
    return tab[bass.ds(row * per, CHUNK * per)].rearrange("(p r) w -> p (r w)", p=P)


def x_of(tab, row):
    return tab[bass.ds(row * 2, CHUNK * 2)].rearrange("(p r two) w -> p r two w", p=P, two=2)[:, :, 0, 0:D]


def over_rows(ap):
    return ap.unsqueeze(1).broadcast_to([P, R, ap.shape[1]])


class Norm:

    def __init__(self, nc, ph, st, tag, by_log=False):
        self.nc, self.by_log, self.eps = nc, by_log, st["eps"]
        self.sum, self.mean, self.var, self.root, self.rstd = (
            ph.sb(f"{tag}_{n}", [P, R]) for n in ("sum", "mean", "var", "root", "rstd"))
        self.square = ph.sb(f"{tag}_square", [P, R, D])
        self.centred, self.squared, self.summed, self.rooted, self.act_chain = ph.sems(
            f"{tag}_centred {tag}_squared {tag}_summed {tag}_rooted {tag}_act_chain")

    def steps(self):
        return 0 if self.by_log else 1

    def take_mean(self, steps, v):
        steps.then(self.nc.vector.reduce_sum(self.sum[:], v, AX_X))
        steps.then(self.nc.vector.tensor_scalar(self.mean[:], self.sum[:], -1.0 / D, None, ALU.mult))
        self.nc.vector.tensor_tensor(v, v, bcast(self.mean[:], D), ALU.add).then_inc(self.centred, 1)

    def squares(self, act, n, v, ready=None):
        act.wait_ge(ready or self.centred, n + 1)
        self.nc.scalar.activation(self.square[:], v, ACT.Square).then_inc(self.squared, 1)

    def take_root(self, act, n):
        nc = self.nc
        act.wait_ge(self.summed, n + 1)
        if self.by_log:
            nc.scalar.activation(self.root[:], self.var[:], ACT.Ln, scale=1.0 / D, bias=self.eps[:]
                                 ).then_inc(self.act_chain, 1)
            act.wait_ge(self.act_chain, n + 1)
            nc.scalar.activation(self.rstd[:], self.root[:], ACT.Exp, scale=-0.5).then_inc(self.rooted, 1)
        else:
            nc.scalar.activation(self.root[:], self.var[:], ACT.Sqrt, scale=1.0 / D, bias=self.eps[:]
                                 ).then_inc(self.rooted, 1)

    def sum_squares(self, dve, n):
        dve.wait_ge(self.squared, n + 1)
        self.nc.vector.reduce_sum(self.var[:], self.square[:], AX_X).then_inc(self.summed, 1)

    def scale(self, dve, steps, n, v, out):
        dve.wait_ge(self.rooted, n + 1)
        if not self.by_log:
            steps.then(self.nc.vector.reciprocal(self.rstd[:], self.root[:]))
        return self.nc.vector.tensor_tensor(out, v, bcast(self.rstd[:], D), ALU.mult)


class Product:

    def __init__(self, nc, ph, st, tag, width, turn_banks, out_banks):
        self.nc, self.st, self.passed = nc, st, ph.passed
        self.pair = P // width
        self.turns = R // self.pair * P // 512
        self.width = width * self.pair
        self.turn_banks, self.out_banks = turn_banks, out_banks
        self.rows_t = [[ph.sb(f"{tag}_t{s}{h}", [self.width, 512]) for h in range(self.turns)] for s in (0, 1)]
        self.turned, self.copied, self.done = ph.sems(f"{tag}_turned {tag}_copied {tag}_done")
        self.slots = len(turn_banks) // self.turns

    def turn_bank(self, s, h):
        return self.turn_banks[(s * self.turns if self.slots == 2 else 0) + h]

    def turn(self, pe, n, s, rows, ready):
        pe.wait_ge(ready[0], ready[1])
        if not fresh(n, self.slots):
            pe.wait_ge(self.copied, (n + 1 - self.slots) * self.turns)
        hold(pe, self.passed)
        for h in range(self.turns):
            for r in range(512 // P):
                q = (h * (512 // P) + r) * self.pair
                block = rows[:, q, :] if self.pair == 1 else flat(rows[:, q:q + self.pair, :])
                ins = self.nc.tensor.transpose(self.turn_bank(s, h)[0:self.width, r * P:(r + 1) * P], block,
                                               self.st["ident"][:])
            ins.then_inc(self.turned, 1)

    def copy(self, act, n, s):
        for h in range(self.turns):
            act.wait_ge(self.turned, n * self.turns + h + 1)
            if not fresh(n):
                act.wait_ge(self.done, n - 1)
            self.nc.scalar.activation(self.rows_t[s][h][:], self.turn_bank(s, h)[0:self.width, :], ACT.Copy
                                      ).then_inc(self.copied, 1)

    def multiply(self, pe, n, s, weight, read):
        k, w = len(self.out_banks), D * self.pair
        b = self.out_banks[s if k == 2 else 0]
        if not fresh(n, k):
            pe.wait_ge(read, n + 1 - k)
        for h in range(self.turns):
            pe.wait_ge(self.copied, n * self.turns + h + 1)
            for r in range(512 // P):
                q = h * (512 // P) + r
                ins = self.nc.tensor.matmul(b[:, q * w:(q + 1) * w], self.rows_t[s][h][:, r * P:(r + 1) * P], weight,
                                            start=True, stop=True)
        ins.then_inc(self.done, 1)

    def result(self, s):
        b = self.out_banks[s if len(self.out_banks) == 2 else 0]
        return b[:].rearrange("p (r d) -> p r d", d=D)


def product_program(pe, st, pr, rows, ready, weight, read):
    def turn(n, i, s):
        for sem, value in ready(n, i, s)[:-1]:
            pe.wait_ge(sem, value)
        pr.turn(pe, n, s, rows[s], ready(n, i, s)[-1])

    def step(n, i, s, first, last):
        if there(n + 1, st["CHUNKS"]):
            turn(*ahead(n, i, s, 1))
        pr.multiply(pe, n, s, weight, read)

    turn(0, 0, 0)
    over_pairs(pe, st["CHUNKS"], step)


def flat(ap):
    return ap.rearrange("p r d -> p (r d)")


def dense_mean(nc, a, st):
    CHUNKS, BLOCKS, NT, bank = st["CHUNKS"], st["BLOCKS"], st["NT"], st["bank"]
    assert CHUNKS == BLOCKS
    with Phase(nc, "d0") as ph:
        x, agg = ([ph.sb(f"{n}{s}", [P, R, w]) for s in (0, 1)] for n, w in (("x", D), ("agg", 66)))
        both = [ph.sb(f"both{s}", [P, R, P]) for s in (0, 1)]
        out = [ph.sb(f"out{s}", [P, R, P]) for s in (0, 1)]
        v = [ph.sb(f"v{s}", [P, R, D]) for s in (0, 1)]
        recip = ph.sb("recip", [P, R])
        max_of = [ph.sb(f"max_of{s}", [P, G]) for s in (0, 1)]
        max_i = [ph.sb(f"max_i{s}", [P, G], I32) for s in (0, 1)]
        pr = Product(nc, ph, st, "p", P, bank[0:4], bank[4:6])
        ln = Norm(nc, ph, st, "n")
        x_put, scaled, added, normed, chain_a, chain_b, max_staged, max_used, self_arg = ph.sems(
            "x_put scaled added normed chain_a chain_b max_staged max_used self_arg")
        loaded, stored, max_in = ([ph.sem(f"{n}{s}") for s in (0, 1)] for n in ("loaded", "stored", "max_in"))
        block = ph.ctx.enter_context(nc.Block())

        @block.sync
        def _(sp):
            def load(s, row):
                sp.dma_start(flat(x[s][:]), table_rows(a["x"], row)).then_inc(loaded[s], 16)
                sp.dma_start(flat(agg[s][:]), table_rows(st["mean_tab"], row)).then_inc(loaded[s], 16)

            loads(sp, ph, st, load, ((scaled, 1), (x_put, 1)))

        @block.gpsimd
        def _(pool):
            maxima = st["mean_tab"].rearrange("n (w o) -> (n w) o", o=1)

            def gather(n, i, s):
                pool.wait_ge(max_staged, n + 1)
                gather_rows(nc, [(max_of[s][:, q:q + 1], q) for q in range(G)], maxima, max_i[s], max_in[s], ph.passed)

            def store(s, row):
                return pool.dma_start(table_rows(st["gate1_tab"], row, 2), flat(out[s][:]))

            stores(pool, ph, st, store, normed, stored, beside=gather)

        @block.vector
        def _(dve):
            steps_a, steps_b = Steps(dve, chain_a, 2), Steps(dve, chain_b, ln.steps())

            def stage_max(n, s):
                nc.vector.tensor_scalar(max_i[s][:], st["dst_g"][:, bass.ds(n * G, G)], 66.0, 65.0, ALU.mult, ALU.add
                                        ).then_inc(max_staged, 1)

            def scale(n, i, s):
                steps_a.turn(n)
                dve.wait_ge(loaded[s], 32 * (i + 1))
                if not fresh(n):
                    dve.wait_ge(pr.turned, n * 2 - 2)
                if not fresh(n, 1):
                    dve.wait_ge(scaled, n)
                cols = bass.ds(n * R, R)
                nc.vector.tensor_copy(st["degree"][:, cols], agg[s][:, :, 64])
                nc.vector.tensor_copy(st["self_exp"][:, cols], agg[s][:, :, 65])
                steps_a.then(nc.vector.tensor_scalar(recip[:], agg[s][:, :, 64], 1.0, None, ALU.max))
                steps_a.then(nc.vector.reciprocal(recip[:], recip[:]))
                nc.vector.tensor_tensor(both[s][:, :, D:P], agg[s][:, :, 0:D], bcast(recip[:], D), ALU.mult
                                        ).then_inc(scaled, 1)
                steps_a.end()

            def add(n, i, s):
                dve.wait_ge(pr.done, n + 1)
                if not fresh(n):
                    dve.wait_ge(normed, n - 1)
                nc.vector.tensor_tensor(v[s][:], pr.result(s), over_rows(st["rows"][:, st["B_MEAN"], :]), ALU.add
                                        ).then_inc(added, 1)

            def step(n, i, s, first, last):
                steps_b.turn(n)
                if there(n + 1, CHUNKS):
                    add(*ahead(n, i, s, 1))
                ln.sum_squares(dve, n)
                if there(n + 3, CHUNKS):
                    scale(*ahead(n, i, s, 3))
                dve.wait_ge(max_in[s], 64 * (i + 1))
                cols = bass.ds(n * G, G)
                nc.vector.tensor_tensor(st["w_exp"][:, cols], st["w_edge"][:, cols], max_of[s][:], ALU.subtract
                                        ).then_inc(max_used, 1)
                if there(n + 2, CHUNKS):
                    dve.wait_ge(max_used, n + 1)
                    stage_max(n + 2, s)
                if not fresh(n):
                    dve.wait_ge(stored[s], 16 * i)
                ln.scale(dve, steps_b, n, v[s][:], out[s][:, :, 0:D]).then_inc(normed, 1)
                steps_b.end()

            for s in (0, 1):
                nc.vector.memset(out[s][:, :, D:P], 0.0)
                stage_max(s, s)
            for n in (0, 1, 2):
                scale(n, n // 2, n % 2)
            add(0, 0, 0)
            over_pairs(dve, CHUNKS, step)
            nc.vector.tensor_scalar(st["self_exp"][:], st["self_exp"][:], -1.0, 1.0, ALU.mult, ALU.add
                                    ).then_inc(self_arg, 1)

        @block.scalar
        def _(act):
            act.preload_act_table_set("sqrt_and_others")

            def put_x(n, i, s):
                act.wait_ge(loaded[s], 32 * (i + 1))
                if not fresh(n):
                    act.wait_ge(pr.turned, n * 2 - 2)
                nc.scalar.activation(both[s][:, :, 0:D], x[s][:], ACT.Copy).then_inc(x_put, 1)

            def step(n, i, s, first, last):
                if not fresh(n, 1):
                    act.wait_ge(ln.summed, n)
                ln.squares(act, n, v[s][:], added)
                if there(n + 2, CHUNKS):
                    pr.copy(act, n + 2, s)
                ln.take_root(act, n)
                if there(n + 3, CHUNKS):
                    put_x(*ahead(n, i, s, 3))

            put_x(0, 0, 0)
            put_x(1, 0, 1)
            pr.copy(act, 0, 0)
            put_x(2, 1, 0)
            pr.copy(act, 1, 1)
            over_pairs(act, CHUNKS, step)
            act.wait_ge(self_arg, 1)
            nc.scalar.activation(st["self_exp"][:], st["self_exp"][:], ACT.Exp)
            nc.scalar.activation(st["w_exp"][:], st["w_exp"][:], ACT.Exp)

        @block.tensor
        def _(pe):
            product_program(pe, st, pr, both, lambda n, i, s: ((scaled, n + 1), (x_put, n + 1)), st["w_self"][:],
                            added)


def dense_gate(nc, st, tag, table, which, residual, dest):
    CHUNKS, bank = st["CHUNKS"], st["bank"]
    final = residual is not None
    W = D if final else P
    with Phase(nc, tag) as ph:
        both = [ph.sb(f"both{s}", [P, R, P]) for s in (0, 1)]
        out = [ph.sb(f"out{s}", [P, R, W]) for s in (0, 1)]
        v = [ph.sb(f"v{s}", [P, R, D]) for s in (0, 1)]
        res = [ph.sb(f"res{s}", [P, R, D]) for s in (0, 1)]
        pr = Product(nc, ph, st, "p", P, bank[0:4], bank[4:6])
        ln = Norm(nc, ph, st, "n")
        added, mixed, finished, chain, chain_m = ph.sems("added mixed finished chain chain_m")
        loaded, stored, res_in = ([ph.sem(f"{n}{s}") for s in (0, 1)] for n in ("loaded", "stored", "res_in"))
        bias = over_rows(st["rows"][:, st["B_MIX1"] + which, :])
        block = ph.ctx.enter_context(nc.Block())

        @block.sync
        def _(sp):
            def load(s, row):
                sp.dma_start(flat(both[s][:]), table_rows(table, row, 2)).then_inc(loaded[s], 16)
                if final:
                    sp.dma_start(res[s][:], x_of(residual, row)).then_inc(res_in[s], 16)

            loads(sp, ph, st, load, ((pr.turned, 2), (mixed, 1)) if final else ((pr.turned, 2),))

        @block.gpsimd
        def _(pool):
            def store(s, row):
                return pool.dma_start(table_rows(dest, row, W // D), flat(out[s][:]))

            stores(pool, ph, st, store, finished, stored)

        @block.vector
        def _(dve):
            steps, steps_m = Steps(dve, chain, ln.steps()), Steps(dve, chain_m, 2)

            def add(n, i, s):
                dve.wait_ge(pr.done, n + 1)
                if not fresh(n):
                    dve.wait_ge(finished, n - 1)
                nc.vector.tensor_tensor(v[s][:], pr.result(s), bias, ALU.add).then_inc(added, 1)
                if final:
                    dve.wait_ge(added, n + 1)
                    dve.wait_ge(res_in[s], 16 * (i + 1))
                    nc.vector.scalar_tensor_tensor(out=v[s][:], in0=v[s][:], scalar=0.0, in1=res[s][:], op0=ALU.max,
                                                   op1=ALU.add).then_inc(mixed, 1)

            def centre(n, s):
                steps_m.turn(n)
                dve.wait_ge(mixed, n + 1)
                ln.take_mean(steps_m, v[s][:])
                steps_m.end()

            def step(n, i, s, first, last):
                if not final:
                    add(n, i, s)
                    return
                more = there(n + 1, CHUNKS)
                if more:
                    add(*ahead(n, i, s, 1))
                ln.sum_squares(dve, n)
                if more:
                    centre(n + 1, 1 - s)
                else:
                    dve.wait_ge(finished, n)
                steps.turn(n)
                if not fresh(n):
                    dve.wait_ge(stored[s], 16 * i)
                ln.scale(dve, steps, n, v[s][:], out[s][:]).then_inc(finished, 1)
                steps.end()

            if final:
                add(0, 0, 0)
                centre(0, 0)
            else:
                for s in (0, 1):
                    nc.vector.memset(out[s][:, :, D:P], 0.0)
            over_pairs(dve, CHUNKS, step)

        @block.scalar
        def _(act):
            act.preload_act_table_set("sqrt_and_others")

            def step(n, i, s, first, last):
                if final:
                    if not fresh(n, 1):
                        act.wait_ge(ln.summed, n)
                    ln.squares(act, n, v[s][:])
                else:
                    act.wait_ge(added, n + 1)
                    if not fresh(n):
                        act.wait_ge(stored[s], 16 * i)
                    nc.scalar.activation(out[s][:, :, 0:D], v[s][:], ACT.Relu).then_inc(finished, 1)
                if there(n + 2, CHUNKS):
                    pr.copy(act, n + 2, s)
                if final:
                    ln.take_root(act, n)

            pr.copy(act, 0, 0)
            pr.copy(act, 1, 1)
            over_pairs(act, CHUNKS, step)

        @block.tensor
        def _(pe):
            product_program(pe, st, pr, both, lambda n, i, s: ((loaded[s], 16 * (i + 1)),), st["w_mix"][which][:],
                            added)


def attention_sums(nc, st):
    BLOCKS, bank, ident = st["BLOCKS"], st["bank"], st["ident"]
    HW = DH + 1
    W = H * HW
    QW = 3 * D + H
    with Phase(nc, "att") as ph:
        bl = Blocks(nc, ph, st, st["src_key"], W)
        ends = [ph.sb(f"ends{s}", [P, G, P]) for s in (0, 1)]
        ends_t = ph.sb("ends_t", [P, G * P])
        qkv = ph.sb("qkv", [P, G, QW])
        state, new = ([ph.sb(f"{n}{s}", [P, G, W + H]) for s in (0, 1)] for n in ("state", "new"))
        src_i, dst_i, put_i = ([ph.sb(f"{n}{s}", [P, G], I32) for s in (0, 1)] for n in ("src_i", "dst_i", "put_i"))
        away = ph.sb("away", [P, G, G * P])
        junk = ph.sb("junk", [P, G, G * P])
        prod, vals = ph.sb("prod", [P, G, D]), ph.sb("vals", [P, G, D])
        logit, top, ex_arg, ex = (ph.sb(n, [P, G, H]) for n in ("logit", "top", "ex_arg", "ex"))
        diff, factor = ph.sb("diff", [P, 2, G, H]), ph.sb("factor", [P, 2, G, H])
        old_part, new_part = ph.sb("old_part", [P, G, W]), ph.sb("new_part", [P, G, W])
        (staged, turned, matched, away_done, ends_turned, ends_copied, produced, qkv_copied, logits, qkv_used,
         logit_turned, head_max, ex_ready, ex_done, paid, summed, differences, factors, updated, chain_f, chain_b,
         chain_u) = ph.sems(
            "staged turned matched away_done ends_turned ends_copied produced qkv_copied logits qkv_used "
            "logit_turned head_max ex_ready ex_done paid summed differences factors updated chain_f chain_b chain_u")
        gathered, state_in, scattered = ([ph.sem(f"{n}{s}") for s in (0, 1)] for n in
                                         ("gathered", "state_in", "scattered"))
        key_t, ends_b, qkv_b, logit_t, sums = bank[0], bank[1], bank[2:4], bank[4:6], bank[6:8]
        block = ph.ctx.enter_context(nc.Block())

        @block.gpsimd
        def _(pool):
            def dst_rows(s):
                gather_rows(nc, [(ends[s][:, q, 0:D], q) for q in range(G)], st["attn_x"], dst_i[s], gathered[s], ph.passed)

            def src_rows(s):
                gather_rows(nc, [(ends[s][:, q, D:P], q) for q in range(G)], st["attn_x"], src_i[s], gathered[s], ph.passed)

            def step(n, i, s, first, last):
                more = not (last and s == 1)
                if more:
                    pool.wait_ge(staged, n + 2)
                    if not n_is(n, 0, first):
                        pool.wait_ge(ends_turned, n)
                    dst_rows(1 - s)
                if not (first and s == 0):
                    pool.wait_ge(scattered[1 - s], 64 * last_use(i, s))
                gather_rows(nc, [(state[s][:, q, :], q) for q in range(G)], st["attn_tab"], src_i[s], state_in[s], ph.passed)
                if more:
                    src_rows(1 - s)
                pool.wait_ge(updated, n + 1)
                hold(pool, ph.passed)
                for q in range(G):
                    nc.gpsimd.indirect_dma_start(
                        st["attn_tab"], bass.IndirectOffsetOnAxis(ap=put_i[s][:, q:q + 1], axis=0),
                        new[s][:, q, :], None).then_inc(scattered[s], 16)

            pool.wait_ge(staged, 1)
            dst_rows(0)
            src_rows(0)
            over_pairs(pool, BLOCKS, step)
            for s in (0, 1):
                pool.wait_ge(scattered[s], 64 * (BLOCKS // 2))

        @block.vector
        def _(dve):
            steps_f, steps_b, steps_u = Steps(dve, chain_f, 3), Steps(dve, chain_b, 1), Steps(dve, chain_u, 2)

            def stage(n, s):
                bl.stage(n, s, ((src_i[s], st["src_g"]), (dst_i[s], st["dst_g"]))).then_inc(staged, 1)

            def heads(ap):
                return ap.rearrange("p t (h c) -> p t h c", h=H)

            def over_heads(ap):
                return ap.unsqueeze(2).broadcast_to([P, G, H, EF])

            def per_head(ap, w):
                return ap.unsqueeze(3).broadcast_to([P, G, H, w])

            def front(n, s, first):
                steps_f.turn(n)
                kv = st["edge_kv"][:, bass.ds(n * G, G), :]
                dve.wait_ge(turned, n + 1)
                if not first:
                    dve.wait_ge(summed, n - 1)
                bl.make_match(key_t, s).then_inc(matched, 1)
                dve.wait_ge(qkv_copied, n + 1)
                steps_f.then(nc.vector.tensor_tensor(heads(prod[:]), heads(qkv[:, :, D + H:2 * D + H]),
                                                     over_heads(kv[:, :, 0:EF]), ALU.mult))
                steps_f.then(nc.vector.tensor_tensor(prod[:], prod[:], qkv[:, :, 0:D], ALU.mult))
                steps_f.then(nc.vector.reduce_sum(logit[:], heads(prod[:]), AX_X))
                nc.vector.tensor_tensor(logit[:], logit[:], qkv[:, :, D:D + H], ALU.add).then_inc(logits, 1)
                nc.vector.tensor_tensor(heads(vals[:]), heads(qkv[:, :, 2 * D + H:QW]),
                                        over_heads(kv[:, :, EF:2 * EF]), ALU.mult).then_inc(qkv_used, 1)
                steps_f.end()

            def pay(n, s):
                steps_b.turn(n)
                dve.wait_ge(away_done, n + 1)
                for h in range(H):
                    dve.wait_ge(logit_turned, n * H + h + 1)
                    hold(dve, ph.passed)
                    for q in range(G):
                        ins = nc.vector.tensor_tensor_reduce(junk[:, q, :], away[:, q, :], logit_t[h % 2][:], 1.0,
                                                             -2.0 * BIG, ALU.add, ALU.max, top[:, q, h:h + 1])
                    ins.then_inc(head_max, 1)
                    dve.wait_ge(head_max, n * H + h + 1)
                nc.vector.tensor_tensor(ex_arg[:], logit[:], top[:], ALU.subtract).then_inc(ex_ready, 1)
                dve.wait_ge(ex_done, n + 1)
                dve.wait_ge(qkv_used, n + 1)
                out = heads(bl.payload[s][:])
                steps_b.then(nc.vector.tensor_copy(out[:, :, :, DH], ex[:]))
                nc.vector.tensor_tensor(out[:, :, :, 0:DH], heads(vals[:]), per_head(ex[:], DH), ALU.mult
                                        ).then_inc(paid, 1)
                steps_b.end()

            def update(n, i, s, first):
                steps_u.turn(n)
                dve.wait_ge(state_in[s], 64 * (i + 1))
                if not first:
                    dve.wait_ge(scattered[s], 64 * i)
                old, row = state[s], new[s]
                steps_u.then(nc.vector.tensor_tensor(row[:, :, W:W + H], old[:, :, W:W + H], top[:], ALU.max))
                nc.vector.tensor_tensor(diff[:, 0], old[:, :, W:W + H], row[:, :, W:W + H], ALU.subtract)
                nc.vector.tensor_tensor(diff[:, 1], top[:], row[:, :, W:W + H], ALU.subtract
                                        ).then_inc(differences, 1)
                nc.vector.tensor_copy(put_i[s][:], st["src_put"][:, bass.ds(n * G, G)])
                dve.wait_ge(factors, n + 1)
                nc.vector.tensor_tensor(heads(old_part[:]), heads(old[:, :, 0:W]), per_head(factor[:, 0], HW), ALU.mult)
                dve.wait_ge(summed, n + 1)
                steps_u.then(nc.vector.tensor_tensor(
                    heads(new_part[:]), heads(sums[s][:, 0:G * W].rearrange("p (t w) -> p t w", w=W)),
                    per_head(factor[:, 1], HW), ALU.mult))
                nc.vector.tensor_tensor(row[:, :, 0:W], old_part[:], new_part[:], ALU.add).then_inc(updated, 1)
                steps_u.end()

            def step(n, i, s, first, last):
                pay(n, s)
                if not (last and s == 1):
                    front(n + 1, 1 - s, n_is(n, 0, first))
                update(n, i, s, first)
                if not last:
                    stage(n + 2, s)

            for s in (0, 1):
                stage(s, s)
            front(0, 0, True)
            over_pairs(dve, BLOCKS, step)

        @block.scalar
        def _(act):
            act.preload_act_table_set("natural_log_exp_and_others")

            def front(n, i, s, first):
                act.wait_ge(ends_turned, n + 1)
                if not first:
                    act.wait_ge(produced, n)
                nc.scalar.activation(ends_t[:], ends_b[:], ACT.Copy).then_inc(ends_copied, 1)
                act.wait_ge(produced, n + 1)
                if not first:
                    act.wait_ge(qkv_used, n)
                for k in (0, 1):
                    ins = nc.scalar.activation(qkv[:, 2 * k:2 * k + 2, :],
                                               qkv_b[k][:, 0:2 * QW].rearrange("p (t w) -> p t w", w=QW), ACT.Copy)
                ins.then_inc(qkv_copied, 1)
                act.wait_ge(matched, n + 1)
                if not first:
                    act.wait_ge(head_max, n * H)
                for q in range(G):
                    ins = nc.scalar.activation(away[:, q, :], bl.match[s][:, q, :], ACT.Identity, scale=BIG,
                                               bias=st["minus_big"][:])
                ins.then_inc(away_done, 1)

            def step(n, i, s, first, last):
                act.wait_ge(ex_ready, n + 1)
                if not n_is(n, 0, first):
                    act.wait_ge(paid, n)
                nc.scalar.activation(ex[:], ex_arg[:], ACT.Exp).then_inc(ex_done, 1)
                if not (last and s == 1):
                    front(n + 1, i + s, 1 - s, False)
                act.wait_ge(differences, n + 1)
                if not n_is(n, 0, first):
                    act.wait_ge(updated, n)
                nc.scalar.activation(factor[:], diff[:], ACT.Exp).then_inc(factors, 1)

            front(0, 0, 0, True)
            over_pairs(act, BLOCKS, step)

        @block.tensor
        def _(pe):
            def front(n, i, s, first):
                pe.wait_ge(gathered[s], 128 * (i + 1))
                if not first:
                    pe.wait_ge(ends_copied, n)
                for q in range(G):
                    ins = nc.tensor.transpose(ends_b[:, q * P:(q + 1) * P], ends[s][:, q, :], ident[:])
                ins.then_inc(ends_turned, 1)
                pe.wait_ge(staged, n + 1)
                if not first:
                    pe.wait_ge(matched, n)
                bl.turn_keys(key_t, s).then_inc(turned, 1)
                pe.wait_ge(ends_copied, n + 1)
                if not first:
                    pe.wait_ge(qkv_copied, n)
                for q in range(G):
                    ins = nc.tensor.matmul(qkv_b[q // 2][:, q % 2 * QW:(q % 2 + 1) * QW], ends_t[:, q * P:(q + 1) * P],
                                           st["w_att"][:], start=True, stop=True)
                ins.then_inc(produced, 1)

            def turn_logits(n, first):
                pe.wait_ge(logits, n + 1)
                for h in range(H):
                    if not (first and h < 2):
                        pe.wait_ge(head_max, n * H + h - 1)
                    for q in range(G):
                        ins = nc.tensor.transpose(logit_t[h % 2][:, q * P:(q + 1) * P],
                                                  logit[:, q, h:h + 1].broadcast_to([P, P]), ident[:])
                    ins.then_inc(logit_turned, 1)

            def step(n, i, s, first, last):
                if not (last and s == 1):
                    front(n + 1, i + s, 1 - s, False)
                pe.wait_ge(matched, n + 1)
                pe.wait_ge(paid, n + 1)
                if not first:
                    pe.wait_ge(updated, n - 1)
                bl.segment_sums(sums[s], s).then_inc(summed, 1)
                if not (last and s == 1):
                    turn_logits(n + 1, False)

            front(0, 0, 0, True)
            turn_logits(0, True)
            over_pairs(pe, BLOCKS, step)


def dense_attention(nc, st):
    CHUNKS, bank, rows = st["CHUNKS"], st["bank"], st["rows"]
    HW = DH + 1
    with Phase(nc, "da") as ph:
        x, agg, res = ([ph.sb(f"{n}{s}", [P, R, w]) for s in (0, 1)] for n, w in (("x", D), ("agg", 72), ("res", D)))
        both = [ph.sb(f"both{s}", [P, R, P]) for s in (0, 1)]
        out = [ph.sb(f"out{s}", [P, R, 130]) for s in (0, 1)]
        v = [ph.sb(f"v{s}", [P, R, D]) for s in (0, 1)]
        part = [ph.sb(f"part{s}", [P, R, H]) for s in (0, 1)]
        recip = ph.sb("recip", [P, R, H])
        z, e, soft, bias = (ph.sb(n, [P, R, D]) for n in ("z", "e", "soft", "bias"))
        p1 = Product(nc, ph, st, "p1", P, bank[0:2], bank[4:6])
        p2 = Product(nc, ph, st, "p2", D, bank[2:4], bank[6:8])
        ln1 = Norm(nc, ph, st, "n1", by_log=True)
        ln2 = Norm(nc, ph, st, "n2", by_log=True)
        (x_put, scaled, biased, added1, added2, logged, softened, res_moved, res_used, finished, chain_a, chain_b,
         chain_c, chain_m, chain_l) = ph.sems(
             "x_put scaled biased added1 added2 logged softened res_moved res_used finished chain_a chain_b "
             "chain_c chain_m chain_l")
        loaded, stored, res_in = ([ph.sem(f"{n}{s}") for s in (0, 1)] for n in ("loaded", "stored", "res_in"))
        block = ph.ctx.enter_context(nc.Block())

        def heads(ap):
            return ap.rearrange("p r (h c) -> p r h c", h=H)

        def per_head(ap):
            return ap.unsqueeze(3).broadcast_to([P, R, H, DH])

        @block.sync
        def _(sp):
            def load(n, s):
                if not fresh(n):
                    sp.wait_ge(scaled, n - 1)
                    sp.wait_ge(x_put, n - 1)
                row = first_node(st, n)
                sp.dma_start(flat(x[s][:]), table_rows(st["attn_x"], row)).then_inc(loaded[s], 16)
                sp.dma_start(flat(agg[s][:]), table_rows(st["attn_tab"], row)).then_inc(loaded[s], 16)

            def load_res(n, s):
                sp.dma_start(flat(res[s][:]), table_rows(st["attn_x"], first_node(st, n))).then_inc(res_in[s], 16)

            def step(n, i, s, first, last):
                if there(n + 6, CHUNKS):
                    load(n + 6, s)
                if there(n + 2, CHUNKS):
                    sp.wait_ge(res_used, n + 1)
                    load_res(n + 2, s)
                sp.wait_ge(finished, n + 1)
                if not there(n + 1, CHUNKS):
                    sp.wait_ge(stored[0], 16 * (i + 1))
                sp.dma_start(table_rows(st["sage1_tab"], first_node(st, n), 2), flat(out[s][:])
                             ).then_inc(stored[s], 16)

            for n in (0, 1):
                load(n, n)
                load_res(n, n)
            for n in (2, 3, 4, 5):
                load(n, n % 2)
            over_pairs(sp, CHUNKS, step, tail=8)
            for s in (0, 1):
                sp.wait_ge(stored[s], 16 * (CHUNKS // 2))

        @block.gpsimd
        def _(pool):
            steps_b = Steps(pool, chain_b, 1)

            def put_x(n, i, s):
                pool.wait_ge(loaded[s], 32 * (i + 1))
                if not fresh(n):
                    pool.wait_ge(p1.turned, n * 2 - 2)
                hold(pool, ph.passed)
                nc.gpsimd.tensor_copy(both[s][:, :, 0:D], x[s][:]).then_inc(x_put, 1)

            def make_bias(n, i, s):
                steps_b.turn(n)
                pool.wait_ge(scaled, n + 1)
                if not fresh(n, 1):
                    pool.wait_ge(added1, n)
                steps_b.then(nc.gpsimd.tensor_tensor(heads(bias[:]), per_head(part[s][:]),
                                                     heads(over_rows(rows[:, st["B_VL"], :])), ALU.mult))
                nc.gpsimd.tensor_tensor(bias[:], bias[:], over_rows(rows[:, st["B_CEN"], :]), ALU.add
                                        ).then_inc(biased, 1)
                steps_b.end()

            def move_res(n, i, s):
                pool.wait_ge(res_in[s], 16 * (i + 1))
                nc.gpsimd.tensor_tensor(res[s][:], res[s][:], over_rows(rows[:, st["B_LNB"], :]), ALU.add
                                        ).then_inc(res_moved, 1)

            def step(n, i, s, first, last):
                if there(n + 3, CHUNKS):
                    make_bias(*ahead(n, i, s, 3))
                if there(n + 4, CHUNKS):
                    put_x(*ahead(n, i, s, 4))
                if there(n + 1, CHUNKS):
                    move_res(*ahead(n, i, s, 1))

            put_x(0, 0, 0)
            make_bias(0, 0, 0)
            put_x(1, 0, 1)
            put_x(2, 1, 0)
            make_bias(1, 0, 1)
            put_x(3, 1, 1)
            make_bias(2, 1, 0)
            move_res(0, 0, 0)
            over_pairs(pool, CHUNKS, step)

        @block.vector
        def _(dve):
            steps_a, steps_c, steps_m = Steps(dve, chain_a, 2), Steps(dve, chain_c, 2), Steps(dve, chain_m, 2)

            def scale(n, i, s):
                steps_a.turn(n)
                dve.wait_ge(loaded[s], 32 * (i + 1))
                if not fresh(n):
                    dve.wait_ge(p1.turned, n * 2 - 2)
                    dve.wait_ge(biased, n - 1)
                if not fresh(n, 1):
                    dve.wait_ge(scaled, n)
                hd = agg[s][:, :, 0:H * HW].rearrange("p r (h c) -> p r h c", c=HW)
                steps_a.then(nc.vector.tensor_scalar(recip[:], hd[:, :, :, DH], 1e-16, None, ALU.add))
                steps_a.then(nc.vector.reciprocal(recip[:], recip[:]))
                nc.vector.tensor_tensor(part[s][:], hd[:, :, :, DH], recip[:], ALU.mult)
                nc.vector.tensor_tensor(heads(both[s][:, :, D:P]), hd[:, :, :, 0:DH], per_head(recip[:]), ALU.mult
                                        ).then_inc(scaled, 1)
                steps_a.end()

            def add1(n, i, s):
                dve.wait_ge(biased, n + 1)
                dve.wait_ge(p1.done, n + 1)
                if not fresh(n, 1):
                    dve.wait_ge(softened, n)
                nc.vector.tensor_tensor(z[:], p1.result(s), bias[:], ALU.add).then_inc(added1, 1)

            def soften(n, i, s):
                dve.wait_ge(logged, n + 1)
                if not fresh(n, 1):
                    dve.wait_ge(p2.turned, n)
                nc.vector.scalar_tensor_tensor(out=soft[:], in0=z[:], scalar=0.0, in1=e[:], op0=ALU.max, op1=ALU.add
                                               ).then_inc(softened, 1)

            def add2(n, i, s):
                dve.wait_ge(p2.done, n + 1)
                if not fresh(n):
                    dve.wait_ge(finished, n - 1)
                nc.vector.tensor_tensor(v[s][:], p2.result(s), over_rows(rows[:, st["B_OUT"], :]), ALU.add
                                        ).then_inc(added2, 1)

            def norm1(n, i, s):
                steps_c.turn(n)
                steps_m.turn(n)
                steps_c.then(ln1.scale(dve, steps_c, n, v[s][:], v[s][:]))
                steps_c.then(nc.vector.tensor_tensor(v[s][:], v[s][:], over_rows(rows[:, st["B_LNG"], :]), ALU.mult))
                dve.wait_ge(res_moved, n + 1)
                nc.vector.tensor_tensor(v[s][:], v[s][:], res[s][:], ALU.add).then_inc(res_used, 1)
                dve.wait_ge(res_used, n + 1)
                ln2.take_mean(steps_m, v[s][:])
                steps_c.end()
                steps_m.end()

            def finish(n, i, s):
                if not fresh(n):
                    dve.wait_ge(stored[s], 16 * i)
                ln2.scale(dve, None, n, v[s][:], out[s][:, :, 0:D]).then_inc(finished, 1)

            def step(n, i, s, first, last):
                if there(n + 2, CHUNKS):
                    add1(*ahead(n, i, s, 2))
                if not fresh(n, 1):
                    finish(n - 1, i + s - 1, 1 - s)
                ln1.sum_squares(dve, n)
                if there(n + 4, CHUNKS):
                    scale(*ahead(n, i, s, 4))
                if there(n + 2, CHUNKS):
                    soften(*ahead(n, i, s, 2))
                norm1(n, i, s)
                if there(n + 1, CHUNKS):
                    add2(*ahead(n, i, s, 1))
                ln2.sum_squares(dve, n)

            for s in (0, 1):
                nc.vector.memset(out[s][:, :, D:130], 0.0)
            scale(0, 0, 0)
            scale(1, 0, 1)
            add1(0, 0, 0)
            scale(2, 1, 0)
            soften(0, 0, 0)
            add1(1, 0, 1)
            scale(3, 1, 1)
            soften(1, 0, 1)
            add2(0, 0, 0)
            over_pairs(dve, CHUNKS, step)
            finish(CHUNKS - 1, CHUNKS // 2 - 1, 1)

        @block.scalar
        def _(act):
            act.preload_act_table_set("natural_log_exp_and_others")

            def log_part(n):
                act.wait_ge(added1, n + 1)
                if not fresh(n, 1):
                    act.wait_ge(softened, n)
                nc.scalar.activation(e[:], z[:], ACT.Abs).then_inc(chain_l, 1)
                act.wait_ge(chain_l, n * 2 + 1)
                nc.scalar.activation(e[:], e[:], ACT.Exp, scale=-1.0).then_inc(chain_l, 1)
                act.wait_ge(chain_l, n * 2 + 2)
                nc.scalar.activation(e[:], e[:], ACT.Ln, bias=st["half"][:], scale=0.5).then_inc(logged, 1)

            def step(n, i, s, first, last):
                ln1.squares(act, n, v[s][:], added2)
                if there(n + 2, CHUNKS):
                    log_part(n + 2)
                ln1.take_root(act, n)
                if there(n + 3, CHUNKS):
                    p1.copy(act, n + 3, 1 - s)
                ln2.squares(act, n, v[s][:])
                if there(n + 2, CHUNKS):
                    p2.copy(act, n + 2, s)
                ln2.take_root(act, n)

            p1.copy(act, 0, 0)
            log_part(0)
            p1.copy(act, 1, 1)
            p2.copy(act, 0, 0)
            log_part(1)
            p1.copy(act, 2, 0)
            p2.copy(act, 1, 1)
            over_pairs(act, CHUNKS, step)

        @block.tensor
        def _(pe):
            def turn1(n, s):
                pe.wait_ge(scaled, n + 1)
                p1.turn(pe, n, s, both[s], (x_put, n + 1))

            def multiply1(n, s):
                p1.multiply(pe, n, s, st["w_att_out"][:], added1)

            def turn2(n, s):
                p2.turn(pe, n, s, soft, (softened, n + 1))

            def multiply2(n, s):
                p2.multiply(pe, n, s, st["w_out"][:], added2)

            def step(n, i, s, first, last):
                if there(n + 3, CHUNKS):
                    turn1(n + 3, 1 - s)
                if there(n + 1, CHUNKS):
                    multiply2(n + 1, 1 - s)
                if there(n + 2, CHUNKS):
                    turn2(n + 2, s)
                if there(n + 3, CHUNKS):
                    multiply1(n + 3, 1 - s)

            turn1(0, 0)
            multiply1(0, 0)
            turn1(1, 1)
            turn2(0, 0)
            multiply1(1, 1)
            turn1(2, 0)
            multiply2(0, 0)
            turn2(1, 1)
            multiply1(2, 0)
            over_pairs(pe, CHUNKS, step)


def dense_sage(nc, st, tag, table, which, residual, dest):
    CHUNKS, bank = st["CHUNKS"], st["bank"]
    final = residual is not None
    W = D if final else 130
    K = D + 1
    with Phase(nc, tag) as ph:
        both = [ph.sb(f"both{s}", [P, R, 2 * K]) for s in (0, 1)]
        mix = [ph.sb(f"mix{s}", [P, R, K]) for s in (0, 1)]
        own = ph.sb("own", [P, R, D])
        out = [ph.sb(f"out{s}", [P, R, W]) for s in (0, 1)]
        v = [ph.sb(f"v{s}", [P, R, D]) for s in (0, 1)]
        res = [ph.sb(f"res{s}", [P, R, D]) for s in (0, 1)]
        deg1 = ph.sb("deg1", [P, R])
        pr = Product(nc, ph, st, "p", K, bank[0:4], bank[4:6])
        ln = Norm(nc, ph, st, "n")
        mixed, added, res_used, finished, chain, chain_n, chain_m = ph.sems(
            "mixed added res_used finished chain chain_n chain_m")
        loaded, stored, res_in = ([ph.sem(f"{n}{s}") for s in (0, 1)] for n in ("loaded", "stored", "res_in"))
        block = ph.ctx.enter_context(nc.Block())

        @block.sync
        def _(sp):
            def load(s, row):
                sp.dma_start(flat(both[s][:]), table_rows(table, row, 2)).then_inc(loaded[s], 16)

            loads(sp, ph, st, load, ((mixed, 1),))

        @block.gpsimd
        def _(pool):
            def load_res(n, i, s):
                if there(n + 1, CHUNKS):
                    if not fresh(n, 1):
                        pool.wait_ge(res_used, n)
                    hold(pool, ph.passed)
                    pool.dma_start(res[1 - s][:], x_of(residual, first_node(st, n + 1))).then_inc(res_in[1 - s], 16)

            def store(s, row):
                return pool.dma_start(table_rows(dest, row, 1 if final else 2), flat(out[s][:]))

            if final:
                pool.dma_start(res[0][:], x_of(residual, first_node(st, 0))).then_inc(res_in[0], 16)
            stores(pool, ph, st, store, finished, stored, beside=load_res if final else None)

        @block.vector
        def _(dve):
            steps, steps_n, steps_m = (
                Steps(dve, chain, ln.steps()), Steps(dve, chain_n, 2), Steps(dve, chain_m, 1 if final else 4))

            def mix_rows(n, i, s):
                steps_m.turn(n)
                dve.wait_ge(loaded[s], 16 * (i + 1))
                if not fresh(n):
                    dve.wait_ge(pr.turned, n * 2 - 2)
                if not fresh(n, 1):
                    dve.wait_ge(mixed, n)
                cols = bass.ds(n * R, R)
                self_exp = st["self_exp"][:, cols]
                rho = st["rho"][:, cols]
                if final:
                    nc.vector.tensor_tensor(mix[s][:, :, D], both[s][:, :, 2 * K - 1], self_exp, ALU.add)
                else:
                    nc.vector.tensor_scalar(deg1[:], st["degree"][:, cols], 1.0, None, ALU.add)
                    steps_m.then(nc.vector.tensor_tensor(mix[s][:, :, D], both[s][:, :, 2 * K - 1], self_exp, ALU.add))
                    steps_m.then(nc.vector.tensor_scalar(rho, mix[s][:, :, D], 1e-16, None, ALU.add))
                    steps_m.then(nc.vector.tensor_tensor(rho, rho, deg1[:], ALU.mult))
                    hold(dve, ph.passed)
                    nc.vector.reciprocal(rho, rho)
                steps_m.then(nc.vector.tensor_tensor(own[:], both[s][:, :, 0:D], bcast(self_exp, D), ALU.mult))
                nc.vector.tensor_tensor(mix[s][:, :, 0:D], own[:], both[s][:, :, K:K + D], ALU.add
                                        ).then_inc(mixed, 1)
                steps_m.end()

            def add(n, i, s):
                dve.wait_ge(pr.done, n + 1)
                if not fresh(n):
                    dve.wait_ge(finished, n - 1)
                nc.vector.tensor_tensor(v[s][:], pr.result(s),
                                        bcast(st["rho"][:, bass.ds(n * R, R)], D), ALU.mult).then_inc(added, 1)
                if final:
                    dve.wait_ge(added, n + 1)
                    dve.wait_ge(res_in[s], 16 * (i + 1))
                    nc.vector.tensor_tensor(v[s][:], v[s][:], res[s][:], ALU.add).then_inc(res_used, 1)

            def centre(n, s):
                steps_n.turn(n)
                dve.wait_ge(res_used, n + 1)
                ln.take_mean(steps_n, v[s][:])
                steps_n.end()

            def step(n, i, s, first, last):
                more = there(n + 1, CHUNKS)
                if not final:
                    add(n, i, s)
                elif more:
                    add(*ahead(n, i, s, 1))
                if final:
                    ln.sum_squares(dve, n)
                    if more:
                        centre(n + 1, 1 - s)
                    else:
                        dve.wait_ge(finished, n)
                if there(n + 3, CHUNKS):
                    mix_rows(*ahead(n, i, s, 3))
                if final:
                    steps.turn(n)
                    if not fresh(n):
                        dve.wait_ge(stored[s], 16 * i)
                    ln.scale(dve, steps, n, v[s][:], out[s][:]).then_inc(finished, 1)
                    steps.end()

            if not final:
                for s in (0, 1):
                    nc.vector.memset(out[s][:, :, D:W], 0.0)
            mix_rows(0, 0, 0)
            mix_rows(1, 0, 1)
            mix_rows(2, 1, 0)
            if final:
                add(0, 0, 0)
                centre(0, 0)
            over_pairs(dve, CHUNKS, step)

        @block.scalar
        def _(act):
            act.preload_act_table_set("sqrt_and_others")

            def step(n, i, s, first, last):
                if final:
                    ln.squares(act, n, v[s][:])
                else:
                    act.wait_ge(added, n + 1)
                    if not fresh(n):
                        act.wait_ge(stored[s], 16 * i)
                    nc.scalar.activation(out[s][:, :, 0:D], v[s][:], ACT.Relu).then_inc(finished, 1)
                if there(n + 2, CHUNKS):
                    pr.copy(act, n + 2, s)
                if final:
                    ln.take_root(act, n)

            pr.copy(act, 0, 0)
            pr.copy(act, 1, 1)
            over_pairs(act, CHUNKS, step)

        @block.tensor
        def _(pe):
            product_program(pe, st, pr, mix, lambda n, i, s: ((mixed, n + 1),), st["w_sage"][which][:], added)


INPUTS = ["x", "src", "dst", "edge_attr_16", "edge_weight", "edge_weight1"] + [f"L0_gnn_{n}" for n in (
    "W_self", "b_self", "W_neigh", "b_neigh")] + [f"L1_gnn_{n}" for n in (
        "Wk1", "Wq1", "Wv1", "Ws1", "b1", "Wl1", "bl1", "Wk2", "Wq2", "Wv2", "Ws2", "b2", "Wl2", "bl2")] + [
            f"L2_gnn_{n}" for n in (
                "Wk", "Wq", "Wv", "wk1_w", "wk1_b", "wk2_w", "wk2_b", "wkl_w", "wkl_b", "wv1_w", "wv1_b", "wv2_w",
                "wv2_b", "wvl_w", "wvl_b", "cen_w", "cen_b", "out_w", "out_b", "ln_g", "ln_b")] + [
                    f"L3_gnn_{n}" for n in ("lin1_w", "lin1_b", "W1", "lin2_w", "lin2_b", "W2")]


def kernel(**inputs):
    import numpy as np
    import concourse.bacc as bacc
    from concourse.bass_utils import run_bass_kernel_spmd

    nc = bacc.Bacc("TRN2", target_bir_lowering=False, num_devices=1)
    arrays, aps = {}, {}
    for name in INPUTS:
        arr = np.ascontiguousarray(inputs[name])
        arrays[f"in_{name}"] = arr
        aps[name] = nc.dram_tensor(f"in_{name}", arr.shape, mybir.dt.from_np(arr.dtype), kind="ExternalInput").ap()
    shape = arrays["in_x"].shape
    out = nc.dram_tensor("out_0", shape, F32, kind="ExternalOutput").ap()
    gnn_program(nc, aps, out)
    got = run_bass_kernel_spmd(nc, [arrays], core_ids=[0])
    return got.results[0]["out_0"]
```

```python
from contextlib import ExitStack

import concourse.bass as bass
from concourse import mybir

P = 128
D = 64
G = 4
R = 8
CHUNK = P * R
H = 4
DH = D // H
EF = 16
SCRAP = 5 * P
BIG = float(2 ** 100)
LN_EPS = 1e-5
FILL = 32
GT = 8

F32 = mybir.dt.float32
I32 = mybir.dt.int32
ALU = mybir.AluOpType
ACT = mybir.ActivationFunctionType
AX_X = mybir.AxisListType.X


def over_pairs(eng, count, body, tail=4):
    assert count % 2 == 0 and count >= tail + 2
    for n in (0, 1):
        body(n, 0, n, True, False)
    with eng.Fori(1, (count - tail) // 2) as i:
        for s in (0, 1):
            body(i * 2 + s, i, s, False, False)
    for n in range(count - tail, count):
        body(n, n // 2, n % 2, False, n >= count - 2)


def hold(eng, passed):
    eng.sem_inc(passed, 1)


def ahead(n, i, s, k):
    return n + k, i + (s + k) // 2, (s + k) % 2


def fresh(n, slots=2):
    return isinstance(n, int) and n < slots


def there(n, count):
    return not isinstance(n, int) or n < count


def last_use(i, s):
    return i + s


class Steps:

    def __init__(self, eng, sem, steps):
        self.eng, self.sem, self.steps = eng, sem, steps

    def turn(self, n):
        self.base, self.k = n * self.steps, 0

    def then(self, ins):
        self.k += 1
        ins.then_inc(self.sem, 1)
        self.eng.wait_ge(self.sem, self.base + self.k)

    def end(self):
        assert self.k == self.steps, (self.k, self.steps)


def bcast(ap, n):
    return ap.unsqueeze(2).broadcast_to([ap.shape[0], ap.shape[1], n])


def gnn_program(nc, a, out):
    N = a["x"].shape[0]
    E = a["src"].shape[0]
    TILES = -(-(-(-E // P)) // GT) * GT
    BLOCKS = TILES // G
    FULL, REST = E // TILES, E % TILES
    CHUNKS = -(-N // CHUNK)
    NT = N + SCRAP
    assert N >= CHUNK and NT * 2 < 2 ** 24

    def dram(name, shape):
        return nc.dram_tensor(name, shape, F32).ap()

    mean_tab = dram("mean_tab", [NT, 66])
    gate1_tab = dram("gate1_tab", [2 * NT, D])
    gate2_tab = dram("gate2_tab", [2 * NT, D])
    attn_x = dram("attn_x", [N, D])
    attn_tab = dram("attn_tab", [NT, 72])
    sage1_tab = dram("sage1_tab", [2 * NT, 65])
    sage2_tab = dram("sage2_tab", [2 * NT, 65])

    ctx = ExitStack()
    with ctx:
        def sb(name, shape, dt=F32):
            return ctx.enter_context(nc.sbuf_tensor(name, shape, dt))

        bank = [ctx.enter_context(nc.psum_tensor(f"bank{i}", [P, 512], F32)) for i in range(8)]

        ident = sb("ident", [P, P])
        earlier = sb("earlier", [P, G, G * P])
        scrap_row = sb("scrap_row", [P, G])
        src_g, dst_g = sb("src_g", [P, TILES], I32), sb("dst_g", [P, TILES], I32)
        src_g2, dst_g2 = sb("src_g2", [P, TILES], I32), sb("dst_g2", [P, TILES], I32)
        src_key, dst_key = sb("src_key", [P, TILES]), sb("dst_key", [P, TILES])
        src_put, dst_put = sb("src_put", [P, TILES], I32), sb("dst_put", [P, TILES], I32)
        dst_put2 = sb("dst_put2", [P, TILES], I32)
        w_mean, w_edge, w_exp = sb("w_mean", [P, TILES]), sb("w_edge", [P, TILES]), sb("w_exp", [P, TILES])
        mean_start = sb("mean_start", [P, FILL, 66])
        mean_filled = ctx.enter_context(nc.semaphore("mean_tab_filled"))
        edge_kv = sb("edge_kv", [P, TILES, 2 * EF])
        degree = sb("degree", [P, CHUNKS * R])
        self_exp = sb("self_exp", [P, CHUNKS * R])
        rho, share = sb("rho", [P, CHUNKS * R]), sb("share", [P, CHUNKS * R])
        w_self = sb("w_self", [P, D])
        w_gate = [sb(f"w_gate{i}", [P, P]) for i in (1, 2)]
        w_mix = [sb(f"w_mix{i}", [P, D]) for i in (1, 2)]
        w_att = sb("w_att", [P, 196])
        w_att_out = sb("w_att_out", [P, D])
        w_out = sb("w_out", [P, P])
        w_sage = [sb(f"w_sage{i}", [P, P]) for i in (1, 2)]
        rows = sb("rows", [P, 12, D])
        (B_MEAN, B_MIX1, B_MIX2, B_CEN, B_VL, B_OUT, B_LNG, B_LNB, B_SAGE1, B_SAGE2, B_TMP, B_TMP2) = range(12)
        half, eps, one = sb("half", [P, 1]), sb("eps", [P, 1]), sb("one", [P, 1])
        st = dict(locals())

        prepare_edges(nc, a, st)
        prepare_weights(nc, a, st)
        mean_and_weight_max(nc, a, st)
        dense_mean(nc, a, st)
        gated_sums(nc, st, "g1", gate1_tab, w_gate[0])
        dense_gate(nc, st, "dg1", gate1_tab, 0, None, gate2_tab)
        gated_sums(nc, st, "g2", gate2_tab, w_gate[1])
        dense_gate(nc, st, "dg2", gate2_tab, 1, gate1_tab, attn_x)
        attention_sums(nc, st)
        dense_attention(nc, st)
        sage_sums(nc, st, "s1", sage1_tab)
        dense_sage(nc, st, "ds1", sage1_tab, 0, None, sage2_tab)
        sage_sums(nc, st, "s2", sage2_tab)
        dense_sage(nc, st, "ds2", sage2_tab, 1, sage1_tab, out)


class Phase:

    def __init__(self, nc, tag):
        self.nc, self.tag, self.ctx, self.all_sems = nc, tag, ExitStack(), []
        self.passed = self.sem("passed")

    def __enter__(self):
        return self

    def __exit__(self, *e):
        self.ctx.__exit__(*e)
        self.nc.clear_and_free_semaphores(self.all_sems)
        self.nc.all_engine_barrier()

    def sb(self, name, shape, dt=F32):
        return self.ctx.enter_context(self.nc.sbuf_tensor(f"{self.tag}_{name}", shape, dt))

    def sem(self, name):
        self.all_sems.append(self.nc.alloc_semaphore(f"{self.tag}_{name}"))
        return self.all_sems[-1]

    def sems(self, names):
        return [self.sem(n) for n in names.split()]


def prepare_weights(nc, a, st):
    ident, rows, bank = st["ident"], st["rows"], st["bank"]
    R_ = {k: st[k] for k in st if k.startswith("B_")}
    with Phase(nc, "pw") as ph:
        sem = ph.sem
        names = ["self", "neigh", "ws1", "wl1", "ws2", "wl2", "lin1", "w1", "lin2", "w2"]
        drams = ["L0_gnn_W_self", "L0_gnn_W_neigh", "L1_gnn_Ws1", "L1_gnn_Wl1", "L1_gnn_Ws2", "L1_gnn_Wl2",
                 "L3_gnn_lin1_w", "L3_gnn_W1", "L3_gnn_lin2_w", "L3_gnn_W2"]
        W = {n: ph.sb(n, [D, D]) for n in names}
        BQ, BK, BV, BWL, BVL = (ph.sb(n, [D, D]) for n in ("bq", "bk", "bv", "bwl", "bvl"))
        CR, OW = ph.sb("cr", [D, D]), ph.sb("ow", [D, D])
        SA = ph.sb("sa", [D, D])
        cols = ph.sb("cols", [D, 8])
        headc = ph.sb("headc", [D, H])
        loaded, zeroed, made, mm, ev, idz, started = (
            sem(n) for n in ("loaded", "zeroed", "made", "mm", "ev", "idz", "started"))
        block = ph.ctx.enter_context(nc.Block())
        col_names = ["L1_gnn_b1", "L1_gnn_b2", "L3_gnn_lin1_b", "L3_gnn_lin2_b", "L2_gnn_out_b"]
        row_names = [("L0_gnn_b_self", R_["B_TMP"]), ("L0_gnn_b_neigh", R_["B_TMP2"]), ("L1_gnn_bl1", R_["B_MIX1"]),
                     ("L1_gnn_bl2", R_["B_MIX2"]), ("L2_gnn_cen_b", R_["B_CEN"]),
                     ("L2_gnn_ln_g", R_["B_LNG"]), ("L2_gnn_ln_b", R_["B_LNB"])]
        n_loads = [0]

        @block.sync
        def _(sp):
            def load(dst, src):
                sp.dma_start(dst, src).then_inc(loaded, 16)
                n_loads[0] += 16

            for n, d in zip(names, drams):
                load(W[n][:], a[d])
            for k, n in enumerate(col_names):
                load(cols[:, k:k + 1], a[n].unsqueeze(1))
            for n, k in row_names:
                load(rows[:, k, :], a[n].unsqueeze(0).broadcast_to([P, D]))
            for i in (1, 2):
                wg = st["w_gate"][i - 1]
                load(wg[0:D, 0:D], a[f"L1_gnn_Wk{i}"])
                load(wg[D:P, 0:D], a[f"L1_gnn_Wq{i}"])
                load(wg[D:P, D:P], a[f"L1_gnn_Wv{i}"])
            load(st["w_att_out"][0:D, :], a["L2_gnn_cen_w"])
            load(OW[:], a["L2_gnn_out_w"])
            sp.wait_ge(zeroed, 1)
            for h in range(H):
                o = slice(h * DH, (h + 1) * DH)
                load(BQ[o, o], a["L2_gnn_Wq"][h])
                load(BK[o, o], a["L2_gnn_Wk"][h])
                load(BV[o, o], a["L2_gnn_Wv"][h])
                load(BWL[o, o], a["L2_gnn_wkl_w"])
                load(BVL[o, o], a["L2_gnn_wvl_w"])
                load(headc[o, h:h + 1], a["L2_gnn_wkl_b"].unsqueeze(1))
                load(rows[:, R_["B_VL"], o], a["L2_gnn_wvl_b"].unsqueeze(0).broadcast_to([P, DH]))

        @block.scalar
        def _(act):
            act.wait_ge(started, 1)
            act.wait_ge(loaded, n_loads[0])
            st["MEAN_FILLED"] = fill(act, st["mean_tab"], st["mean_start"], st["mean_filled"])

        @block.gpsimd
        def _(pool):
            nc.gpsimd.memset(ident[:], 0.0).then_inc(idz, 1)
            pool.wait_ge(idz, 1)
            nc.gpsimd.affine_select(out=ident[:], in_=ident[:], compare_op=ALU.not_equal, fill=1.0, base=0,
                                    pattern=[[-1, P]], channel_multiplier=1).then_inc(idz, 1)

        evac = [0]

        @block.vector
        def _(dve):
            nc.vector.memset(st["mean_start"][:, :, 0:65], 0.0)
            nc.vector.memset(st["mean_start"][:, :, 65:66], 1.0).then_inc(started, 1)
            for t in (BQ[:], BK[:], BV[:], BWL[:], BVL[:], headc[:], st["w_gate"][0][0:D, D:P],
                      st["w_gate"][1][0:D, D:P], st["w_att"][:], st["w_out"][:],
                      st["w_sage"][0][:], st["w_sage"][1][:]):
                ins = nc.vector.memset(t, 0.0)
            nc.vector.memset(st["half"][:], 0.5)
            nc.vector.memset(st["eps"][:], LN_EPS)
            nc.vector.memset(st["one"][:], 1.0)
            ins = nc.vector.memset(CR[:], -1.0 / D)
            ins.then_inc(zeroed, 1)
            dve.wait_ge(zeroed, 1)
            dve.wait_ge(idz, 2)
            dve.wait_ge(loaded, n_loads[0])
            nc.vector.tensor_tensor(CR[:], CR[:], ident[0:D, 0:D], ALU.add).then_inc(made, 1)
            nc.vector.tensor_tensor(rows[:, R_["B_TMP"], :], rows[:, R_["B_TMP"], :], rows[:, R_["B_TMP2"], :],
                                    ALU.add).then_inc(made, 1)
            dve.wait_ge(made, 2)
            nc.vector.reduce_sum(rows[:, R_["B_TMP2"], 0:1], rows[:, R_["B_TMP"], :], AX_X).then_inc(made, 1)
            dve.wait_ge(made, 3)
            nc.vector.tensor_scalar(rows[:, R_["B_TMP2"], 1:2], rows[:, R_["B_TMP2"], 0:1], -1.0 / D, None,
                                    ALU.mult).then_inc(made, 1)
            dve.wait_ge(made, 4)
            nc.vector.tensor_scalar(rows[:, R_["B_MEAN"], :], rows[:, R_["B_TMP"], :],
                                    rows[:, R_["B_TMP2"], 1:2], None, ALU.add).then_inc(made, 1)

            def take(dst, src, add=None, scale=None):
                evac[0] += 1
                dve.wait_ge(mm, evac[0])
                if add is not None:
                    ins = nc.vector.tensor_tensor(dst, src, add, ALU.add)
                elif scale is not None:
                    ins = nc.vector.tensor_scalar(dst, src, scale, None, ALU.mult)
                else:
                    ins = nc.vector.tensor_copy(dst, src)
                ins.then_inc(ev, 1)

            b = bank[0]
            take(SA[:], b[0:D, 0:D], add=ident[0:D, 0:D])
            take(st["w_self"][0:D, :], b[0:D, 0:D])
            take(st["w_self"][D:P, :], b[0:D, 0:D])
            for i in (0, 1):
                take(SA[:], b[0:D, 0:D])
                take(st["w_mix"][i][0:D, :], b[0:D, 0:D])
                take(st["w_mix"][i][D:P, :], b[0:D, 0:D])
                bi = R_["B_MIX1"] + i
                take(rows[:, bi, :], b[:, 0:D], add=rows[:, bi, :])
            for i in (0, 1):
                take(st["w_sage"][i][0:D, 0:D], b[0:D, 0:D])
                take(st["w_sage"][i][D:P, D:P], b[0:D, 0:D])
                take(rows[:, R_["B_SAGE1"] + i, :], b[:, 0:D])
            take(SA[:], b[0:D, 0:D])
            take(st["w_att"][D:P, 0:D], b[0:D, 0:D], scale=0.25)
            take(st["w_att"][D:P, D:D + H], b[0:D, 0:H], scale=0.25)
            take(st["w_att"][0:D, D + H:2 * D + H], b[0:D, 0:D])
            take(st["w_att"][0:D, 2 * D + H:3 * D + H], b[0:D, 0:D])
            take(st["w_att_out"][D:P, :], b[0:D, 0:D])
            take(SA[:], b[0:D, 0:D])
            take(st["w_out"][0:D, 0:D], b[0:D, 0:D])
            take(st["w_out"][D:P, D:P], b[0:D, 0:D])
            take(rows[:, R_["B_OUT"], :], b[:, 0:D])

        @block.tensor
        def _(pe):
            n = [0]
            b = bank[0]
            pe.wait_ge(made, 5)

            def mul(out, lhsT, rhs):
                if n[0]:
                    pe.wait_ge(ev, n[0])
                nc.tensor.matmul(out, lhsT, rhs, start=True, stop=True).then_inc(mm, 1)
                n[0] += 1

            idn = ident[0:D, 0:D]
            mul(b[0:D, 0:D], idn, W["self"][:])
            mul(b[0:D, 0:D], SA[:], CR[:])
            mul(b[0:D, 0:D], W["neigh"][:], CR[:])
            for i in (1, 2):
                mul(b[0:D, 0:D], W[f"ws{i}"][:], idn)
                mul(b[0:D, 0:D], SA[:], W[f"wl{i}"][:])
                mul(b[0:D, 0:D], idn, W[f"wl{i}"][:])
                mul(b[:, 0:D], cols[:, i - 1:i].broadcast_to([D, P]), W[f"wl{i}"][:])
            for i in (1, 2):
                mul(b[0:D, 0:D], W[f"lin{i}"][:], W[f"w{i}"][:])
                mul(b[0:D, 0:D], W[f"lin{i}"][:], W[f"w{i}"][:])
                mul(b[:, 0:D], cols[:, i + 1:i + 2].broadcast_to([D, P]), W[f"w{i}"][:])
            mul(b[0:D, 0:D], BWL[:], idn)
            mul(b[0:D, 0:D], BQ[:], SA[:])
            mul(b[0:D, 0:H], BQ[:], headc[:])
            mul(b[0:D, 0:D], BK[:], idn)
            mul(b[0:D, 0:D], BV[:], idn)
            mul(b[0:D, 0:D], idn, BVL[:])
            mul(b[0:D, 0:D], OW[:], idn)
            mul(b[0:D, 0:D], SA[:], CR[:])
            mul(b[0:D, 0:D], SA[:], CR[:])
            mul(b[:, 0:D], cols[:, 4:5].broadcast_to([D, P]), CR[:])


def prepare_edges(nc, a, st):
    FULL, REST, TILES, N, earlier = (st[k] for k in ("FULL", "REST", "TILES", "N", "earlier"))
    with Phase(nc, "pe") as ph:
        src_i, dst_i = ph.sb("src_i", [P, TILES], I32), ph.sb("dst_i", [P, TILES], I32)
        iota_i = ph.sb("iota_i", [P, G], I32)
        cleared, loaded, masks = ph.sems("cleared loaded masks")
        block = ph.ctx.enter_context(nc.Block())
        n_loads = [0]

        @block.sync
        def _(sp):
            sp.wait_ge(cleared, 1)
            for dst, name in ((src_i, "src"), (st["src_g"], "src"), (dst_i, "dst"), (st["dst_g"], "dst"),
                              (st["w_mean"], "edge_weight1"), (st["w_edge"], "edge_weight")):
                v = a[name] if len(a[name].shape) == 1 else a[name].rearrange("e o -> (e o)")
                sp.dma_start(dst[0:FULL, :], v[0:FULL * TILES].rearrange("(p t) -> p t", t=TILES)).then_inc(loaded, 16)
                n_loads[0] += 16
                if REST:
                    sp.dma_start(dst[FULL:FULL + 1, 0:REST], v[FULL * TILES:E_of(a)].unsqueeze(0)).then_inc(loaded, 16)
                    n_loads[0] += 16

        @block.gpsimd
        def _(pool):
            nc.gpsimd.memset(earlier[:], 1.0).then_inc(masks, 1)
            nc.gpsimd.iota(iota_i[:], pattern=[[P, G]], base=N, channel_multiplier=1).then_inc(masks, 1)
            pool.wait_ge(masks, 1)
            for q in range(G):
                nc.gpsimd.affine_select(out=earlier[:, q, :], in_=earlier[:, q, :], compare_op=ALU.is_gt,
                                        fill=0.0, base=q * P, pattern=[[-1, G * P]],
                                        channel_multiplier=1).then_inc(masks, 1)

        @block.vector
        def _(dve):
            for t, v in ((src_i, N + G * P), (dst_i, N + G * P), (st["src_g"], 0), (st["dst_g"], 0),
                         (st["w_mean"], 0.0), (st["w_edge"], 0.0)):
                ins = nc.vector.memset(t[:], v)
            ins.then_inc(cleared, 1)
            dve.wait_ge(loaded, n_loads[0])
            dve.wait_ge(masks, 2)
            nc.vector.tensor_copy(st["scrap_row"][:], iota_i[:])
            nc.vector.tensor_copy(st["src_key"][:], src_i[:])
            nc.vector.tensor_copy(st["dst_key"][:], dst_i[:])
            nc.vector.tensor_scalar(st["src_g2"][:], st["src_g"][:], 2.0, None, ALU.mult)
            nc.vector.tensor_scalar(st["dst_g2"][:], st["dst_g"][:], 2.0, None, ALU.mult)


def fill(eng, tab, src, filled, pace=None):
    rows, width = tab.shape
    per, n = rows // P, 0
    body = tab[0:per * P].rearrange("(p r) w -> p (r w)", p=P)
    for r in range(0, per, FILL):
        k = min(FILL, per - r)
        if pace:
            pace(r // FILL)
        eng.dma_start(body[:, r * width:(r + k) * width],
                      src[:, 0:k, :].rearrange("p r w -> p (r w)")).then_inc(filled, 16)
        n += 16
    if rows > per * P:
        eng.dma_start(tab[per * P:rows], src[0:rows - per * P, 0, :]).then_inc(filled, 16)
        n += 16
    return n


def E_of(a):
    return a["src"].shape[0]


class Blocks:

    def __init__(self, nc, ph, st, key, width):
        self.nc, self.st, self.key, self.width = nc, st, key, width
        self.keys = [ph.sb(f"keys{s}", [P, G]) for s in (0, 1)]
        self.match = [ph.sb(f"match{s}", [P, G, G * P]) for s in (0, 1)]
        self.payload = [ph.sb(f"payload{s}", [P, G, width]) for s in (0, 1)]

    def turn_keys(self, bank, s):
        for q in range(G):
            ins = self.nc.tensor.transpose(bank[:, q * P:(q + 1) * P],
                                           self.keys[s][:, q:q + 1].broadcast_to([P, P]), self.st["ident"][:])
        return ins

    def make_match(self, bank, s):
        for q in range(G):
            ins = self.nc.vector.tensor_scalar(self.match[s][:, q, :], bank[:], self.keys[s][:, q:q + 1], None,
                                               ALU.is_equal)
        return ins

    def segment_sums(self, bank, s, tiles=range(G)):
        w = self.width
        for u in tiles:
            for t in range(G):
                ins = self.nc.tensor.matmul(bank[:, u * w:(u + 1) * w], self.match[s][:, t, u * P:(u + 1) * P],
                                            self.payload[s][:, t, :], start=(t == 0), stop=(t == G - 1))
        return ins

    def stage(self, n, s, copies):
        cols = bass.ds(n * G, G)
        ins = self.nc.vector.tensor_copy(self.keys[s][:], self.key[:, cols])
        for dst, src in copies:
            ins = self.nc.vector.tensor_copy(dst[:], src[:, cols])
        return ins


class Leaders:

    def __init__(self, nc, ph, st, tag):
        self.nc, self.st = nc, st
        self.before, self.lead, self.diff = (ph.sb(f"{tag}_{n}", [P, G]) for n in ("before", "lead", "diff"))
        self.junk = ph.sb(f"{tag}_junk", [P, G, G * P])

    STEPS = 4

    def find(self, steps, match, keys, outs):
        nc, scrap = self.nc, self.st["scrap_row"]
        for q in range(G):
            w = (q + 1) * P
            ins = nc.vector.tensor_tensor_reduce(self.junk[:, q, 0:w], match[:, q, 0:w], self.st["earlier"][:, q, 0:w],
                                                 1.0, 0.0, ALU.mult, ALU.add, self.before[:, q:q + 1])
        steps.then(ins)
        steps.then(nc.vector.tensor_scalar(self.lead[:], self.before[:], 0.0, None, ALU.is_equal))
        steps.then(nc.vector.tensor_tensor(self.diff[:], keys[:], scrap[:], ALU.subtract))
        steps.then(nc.vector.tensor_tensor(self.diff[:], self.diff[:], self.lead[:], ALU.mult))
        for dst in outs:
            ins = nc.vector.tensor_tensor(dst, self.diff[:], scrap[:], ALU.add)
        return ins


def put_indices(nc, act, n, i, s, copies, gathered, per, indexed):
    if not fresh(n):
        act.wait_ge(gathered, per * i)
    for dst, src in copies:
        ins = nc.scalar.activation(dst[:], src[:, bass.ds(n * G, G)], ACT.Copy)
    ins.then_inc(indexed, 1)


def gather_rows(nc, out_cols, table, index, sem, passed):
    hold(nc.gpsimd, passed)
    for dst, q in out_cols:
        nc.gpsimd.indirect_dma_start(dst, None, table, bass.IndirectOffsetOnAxis(ap=index[:, q:q + 1], axis=0)
                                     ).then_inc(sem, 16)


def mean_and_weight_max(nc, a, st):
    BLOCKS, bank, x = st["BLOCKS"], st["bank"], a["x"]
    with Phase(nc, "mean") as ph:
        bl = Blocks(nc, ph, st, st["dst_key"], 65)
        ld = Leaders(nc, ph, st, "dst")
        xs = [ph.sb(f"xs{s}", [P, G, D]) for s in (0, 1)]
        state, new = ([ph.sb(f"{n}{s}", [P, G, 66]) for s in (0, 1)] for n in ("state", "new"))
        weight = [ph.sb(f"weight{s}", [P, G]) for s in (0, 1)]
        src_i, dst_i, put_i = ([ph.sb(f"{n}{s}", [P, G], I32) for s in (0, 1)] for n in ("src_i", "dst_i", "put_i"))
        top, junk = ph.sb("top", [P, G]), ph.sb("junk", [P, G, G * P])
        indexed, staged, turned, matched, paid, summed, topped, updated, chain = ph.sems(
            "indexed staged turned matched paid summed topped updated chain")
        gathered, state_in, scattered = ([ph.sem(f"{n}{s}") for s in (0, 1)] for n in
                                         ("gathered", "state_in", "scattered"))
        mlp = EdgeMlp(nc, a, ph, st)
        attn_start = ph.sb("attn_start", [P, FILL, 72])
        zeros_put, started, filled = ph.sems("zeros_put started filled")
        block = ph.ctx.enter_context(nc.Block())
        key_t, weight_t, sums = bank[0:2], bank[2:4], bank[4:6]

        @block.sync
        def _(sp):
            mlp.load(sp)
            sp.wait_ge(started, 1)

            def pace(k):
                sp.wait_ge(updated, min(2 * k + 1, BLOCKS))

            n = fill(sp, st["attn_tab"], attn_start, filled, pace)
            for tab in (st["gate1_tab"], st["gate2_tab"], st["sage1_tab"], st["sage2_tab"]):
                scrap = tab[2 * st["N"]:2 * st["NT"]].rearrange("(p r) w -> p r w", p=P)
                sp.dma_start(scrap, attn_start[:, 0:2 * SCRAP // P, 0:tab.shape[1]]).then_inc(filled, 16)
                n += 16
            sp.wait_ge(filled, n)

        @block.gpsimd
        def _(pool):
            def x_rows(s, part):
                gather_rows(nc, [(xs[s][:, q, :], q) for q in part], x, src_i[s], gathered[s], ph.passed)

            def step(n, i, s, first, last):
                more = there(n + 2, BLOCKS)
                if more:
                    pool.wait_ge(indexed, n + 3)
                    pool.wait_ge(paid, n + 1)
                    x_rows(s, (0, 1))
                pool.wait_ge(staged, n + 1)
                if not fresh(n, 1):
                    pool.wait_ge(scattered[1 - s], 64 * last_use(i, s))
                gather_rows(nc, [(state[s][:, q, :], q) for q in range(G)], st["mean_tab"], dst_i[s], state_in[s],
                            ph.passed)
                if more:
                    x_rows(s, (2, 3))
                pool.wait_ge(updated, n + 1)
                hold(pool, ph.passed)
                for q in range(G):
                    nc.gpsimd.indirect_dma_start(
                        st["mean_tab"], bass.IndirectOffsetOnAxis(ap=put_i[s][:, q:q + 1], axis=0),
                        new[s][:, q, :], None).then_inc(scattered[s], 16)

            mlp.clear(pool)
            for s in (0, 1):
                pool.wait_ge(indexed, s + 1)
                x_rows(s, range(G))
            pool.wait_ge(st["mean_filled"], st["MEAN_FILLED"])
            over_pairs(pool, BLOCKS, step)
            for s in (0, 1):
                pool.wait_ge(scattered[s], 64 * (BLOCKS // 2))

        @block.vector
        def _(dve):
            steps = Steps(dve, chain, Leaders.STEPS)

            def stage(n, s):
                bl.stage(n, s, ((weight[s], st["w_edge"]), (dst_i[s], st["dst_g"]))).then_inc(staged, 1)

            def step(n, i, s, first, last):
                steps.turn(n)
                mlp.vector_before(dve, i, s, first)
                dve.wait_ge(turned, n + 1)
                if not first:
                    dve.wait_ge(summed, n - 1)
                bl.make_match(key_t[s], s).then_inc(matched, 1)
                dve.wait_ge(gathered[s], 64 * (i + 1))
                nc.vector.tensor_tensor(bl.payload[s][:, :, 0:D], xs[s][:],
                                        bcast(st["w_mean"][:, bass.ds(n * G, G)], D), ALU.mult).then_inc(paid, 1)
                dve.wait_ge(matched, n + 1)
                hold(dve, ph.passed)
                for q in range(G):
                    ins = nc.vector.tensor_tensor_reduce(junk[:, q, :], bl.match[s][:, q, :], weight_t[s][:], 1.0, 1.0,
                                                         ALU.mult, ALU.max, top[:, q:q + 1])
                ins.then_inc(topped, 1)
                if not first:
                    dve.wait_ge(scattered[s], 64 * i)
                ld.find(steps, bl.match[s], bl.keys[s], (
                    put_i[s][:], st["dst_put"][:, bass.ds(n * G, G)]))
                steps.end()
                mlp.vector(dve, i, s, first)
                dve.wait_ge(summed, n + 1)
                dve.wait_ge(state_in[s], 64 * (i + 1))
                dve.wait_ge(topped, n + 1)
                nc.vector.tensor_tensor(new[s][:, :, 0:65], sums[s][:, 0:G * 65].rearrange("p (t w) -> p t w", w=65),
                                        state[s][:, :, 0:65], ALU.add)
                nc.vector.tensor_tensor(new[s][:, :, 65], state[s][:, :, 65], top[:], ALU.max).then_inc(updated, 1)
                if not last:
                    stage(n + 2, s)

            nc.vector.memset(attn_start[:], 0.0).then_inc(zeros_put, 1)
            dve.wait_ge(zeros_put, 1)
            nc.vector.memset(attn_start[:, :, 68:72], -BIG).then_inc(started, 1)
            for s in (0, 1):
                nc.vector.memset(bl.payload[s][:], 1.0)
                stage(s, s)
            over_pairs(dve, BLOCKS, step)
            mlp.last_keep(dve)
            nc.vector.tensor_scalar(st["dst_put2"][:], st["dst_put"][:], 2.0, 1.0, ALU.mult, ALU.add)

        @block.scalar
        def _(act):
            act.preload_act_table_set("natural_log_exp_and_others")

            def step(n, i, s, first, last):
                if there(n + 2, BLOCKS):
                    index(*ahead(n, i, s, 2))
                mlp.scalar(act, i, s, first)

            def index(n, i, s):
                put_indices(nc, act, n, i, s, ((src_i[s], st["src_g"]),), gathered[s], 64, indexed)

            for s in (0, 1):
                index(s, 0, s)
            over_pairs(act, BLOCKS, step)

        @block.tensor
        def _(pe):
            def turn(n, s):
                pe.wait_ge(staged, n + 1)
                bl.turn_keys(key_t[s], s)
                for q in range(G):
                    ins = nc.tensor.transpose(weight_t[s][:, q * P:(q + 1) * P],
                                              weight[s][:, q:q + 1].broadcast_to([P, P]), st["ident"][:])
                ins.then_inc(turned, 1)

            def step(n, i, s, first, last):
                if not (last and s == 1):
                    turn(n + 1, 1 - s)
                mlp.tensor_before(pe, i, s, first)
                pe.wait_ge(matched, n + 1)
                pe.wait_ge(paid, n + 1)
                if not first:
                    pe.wait_ge(updated, n - 1)
                bl.segment_sums(sums[s], s).then_inc(summed, 1)
                mlp.tensor_after(pe, i, s, first)

            turn(0, 0)
            over_pairs(pe, BLOCKS, step)


def n_is(n, value, first):
    return first and n == value


class EdgeMlp:

    def __init__(self, nc, a, ph, st):
        self.nc, self.a, self.st = nc, a, st
        assert GT == 2 * G
        self.attr = ph.sb("attr", [P, st["TILES"] * EF])
        self.w1, self.w2 = ph.sb("mlp_w1", [P, 2, P]), ph.sb("mlp_w2", [P, 2, P])
        self.small1, self.small2 = ph.sb("mlp_small1", [P, 2, EF]), ph.sb("mlp_small2", [P, 2, EF])
        self.diagonal = ph.sb("mlp_diagonal", [P, GT, EF])
        self.b1, self.b2 = ph.sb("mlp_b1", [P, 2]), ph.sb("mlp_b2", [P, GT, 2, EF])
        self.stage_t, self.attr_t = ph.sb("mlp_stage", [P, P]), ph.sb("mlp_attr_t", [P, P])
        self.z, self.e, self.soft = (ph.sb(f"mlp_{n}", [P, 2, P]) for n in ("z", "e", "soft"))
        (self.masked, self.made, self.cleared, self.loaded, self.staged, self.turned, self.copied, self.first_mm,
         self.z_done, self.ln_done,
         self.soft_done, self.second_mm, self.kept, self.chain) = ph.sems(
             "mmasked mmade mcleared mloaded mstaged mturned mcopied mfirst_mm mz_done mln_done msoft_done "
             "msecond_mm mkept mchain")
        self.loads = 16 * (1 + (st["REST"] > 0) + 8)

    def load(self, sp):
        st, a = self.st, self.a
        FULL, REST, TILES = st["FULL"], st["REST"], st["TILES"]

        def load(dst, src):
            sp.dma_start(dst, src).then_inc(self.loaded, 16)

        sp.wait_ge(self.cleared, 1)
        v = a["edge_attr_16"]
        load(self.attr[0:FULL, :], v[0:FULL * TILES].rearrange("(p t) f -> p (t f)", t=TILES))
        if REST:
            load(self.attr[FULL:FULL + 1, 0:REST * EF], v[FULL * TILES:E_of(a)].rearrange("(o t) f -> o (t f)", o=1))
        for k, n in ((0, "k"), (1, "v")):
            for w, layer in ((self.small1, 1), (self.small2, 2)):
                load(w[:, k, :], a[f"L2_gnn_w{n}{layer}_w"].unsqueeze(0).broadcast_to([GT, EF, EF]))
            load(self.b1[:, k:k + 1], a[f"L2_gnn_w{n}1_b"].unsqueeze(0).broadcast_to([GT, EF]))
            load(self.b2[:, :, k, :], a[f"L2_gnn_w{n}2_b"].unsqueeze(0).unsqueeze(0).broadcast_to([P, GT, EF]))

    def clear(self, pool):
        gp = self.nc.gpsimd
        gp.memset(self.attr[:], 0.0).then_inc(self.cleared, 1)
        gp.memset(self.diagonal[:], 1.0).then_inc(self.masked, 1)
        pool.wait_ge(self.masked, 1)
        gp.affine_select(out=self.diagonal[:], in_=self.diagonal[:], compare_op=ALU.is_ge, fill=0.0, base=0,
                         pattern=[[-EF, GT], [0, EF]], channel_multiplier=1).then_inc(self.masked, 1)
        pool.wait_ge(self.masked, 2)
        gp.affine_select(out=self.diagonal[:], in_=self.diagonal[:], compare_op=ALU.is_ge, fill=0.0, base=EF - 1,
                         pattern=[[EF, GT], [0, EF]], channel_multiplier=-1).then_inc(self.masked, 1)

    def make_weights(self, dve):
        dve.wait_ge(self.loaded, self.loads)
        dve.wait_ge(self.masked, 3)
        for small, w in ((self.small1, self.w1), (self.small2, self.w2)):
            for k in (0, 1):
                ins = self.nc.vector.tensor_tensor(
                    w[:, k, :].rearrange("p (t f) -> p t f", f=EF), self.diagonal[:],
                    small[:, k, :].unsqueeze(1).broadcast_to([P, GT, EF]), ALU.mult)
        ins.then_inc(self.made, 1)

    def vector_before(self, dve, g, s, first):
        nc = self.nc
        if s == 0:
            if first:
                self.make_weights(dve)
            else:
                dve.wait_ge(self.turned, g)
            nc.vector.tensor_copy(self.stage_t[:], self.attr[:, bass.ds(g * P, P)]).then_inc(self.staged, 1)

    def vector(self, dve, g, s, first):
        nc = self.nc
        if s == 0:
            if not first:
                dve.wait_ge(self.second_mm, g)
                self.keep(g - 1)
        else:
            dve.wait_ge(self.ln_done, g + 1)
            nc.vector.scalar_tensor_tensor(out=self.soft[:], in0=self.z[:], scalar=0.0, in1=self.e[:], op0=ALU.max,
                                           op1=ALU.add).then_inc(self.soft_done, 1)

    def keep(self, g):
        bank = self.st["bank"][6]
        for k in (0, 1):
            ins = self.nc.vector.tensor_tensor(
                self.st["edge_kv"][:, bass.ds(g * GT, GT), k * EF:(k + 1) * EF],
                bank[:, k * P:(k + 1) * P].rearrange("p (t f) -> p t f", f=EF), self.b2[:, :, k, :], ALU.add)
        ins.then_inc(self.kept, 1)

    def scalar(self, act, g, s, first):
        nc, bank = self.nc, self.st["bank"]
        if s == 0:
            act.wait_ge(self.turned, g + 1)
            nc.scalar.activation(self.attr_t[:], bank[7][:, 2 * P:3 * P], ACT.Copy).then_inc(self.copied, 1)
        else:
            act.wait_ge(self.first_mm, g + 1)
            if not first:
                act.wait_ge(self.soft_done, g)
            for k in (0, 1):
                ins = nc.scalar.activation(self.z[:, k, :], bank[7][:, k * P:(k + 1) * P], ACT.Identity,
                                           bias=self.b1[:, k:k + 1])
            ins.then_inc(self.z_done, 1)
            act.wait_ge(self.z_done, g + 1)
            nc.scalar.activation(self.e[:], self.z[:], ACT.Abs).then_inc(self.chain, 1)
            act.wait_ge(self.chain, g * 2 + 1)
            nc.scalar.activation(self.e[:], self.e[:], ACT.Exp, scale=-1.0).then_inc(self.chain, 1)
            act.wait_ge(self.chain, g * 2 + 2)
            nc.scalar.activation(self.e[:], self.e[:], ACT.Ln, bias=self.st["half"][:], scale=0.5
                                 ).then_inc(self.ln_done, 1)

    def tensor_before(self, pe, g, s, first):
        nc, bank = self.nc, self.st["bank"]
        if s == 0:
            pe.wait_ge(self.staged, g + 1)
            if not first:
                pe.wait_ge(self.z_done, g)
            nc.tensor.transpose(bank[7][:, 2 * P:3 * P], self.stage_t[:], self.st["ident"][:]).then_inc(self.turned, 1)

    def tensor_after(self, pe, g, s, first):
        nc, bank = self.nc, self.st["bank"]
        if s == 0:
            if first:
                pe.wait_ge(self.made, 1)
            pe.wait_ge(self.copied, g + 1)
            for k in (0, 1):
                ins = nc.tensor.matmul(bank[7][:, k * P:(k + 1) * P], self.w1[:, k, :], self.attr_t[:], start=True,
                                       stop=True)
            ins.then_inc(self.first_mm, 1)
        else:
            pe.wait_ge(self.soft_done, g + 1)
            if not first:
                pe.wait_ge(self.kept, g)
            for k in (0, 1):
                ins = nc.tensor.matmul(bank[6][:, k * P:(k + 1) * P], self.soft[:, k, :], self.w2[:, k, :], start=True,
                                       stop=True)
            ins.then_inc(self.second_mm, 1)

    def last_keep(self, dve):
        dve.wait_ge(self.second_mm, self.st["BLOCKS"] // 2)
        self.keep(self.st["BLOCKS"] // 2 - 1)


def gated_sums(nc, st, tag, table, weight):
    BLOCKS, bank, ident = st["BLOCKS"], st["bank"], st["ident"]
    lead = tag == "g1"
    with Phase(nc, tag) as ph:
        bl = Blocks(nc, ph, st, st["dst_key"], D)
        ends = [ph.sb(f"ends{s}", [P, G, P]) for s in (0, 1)]
        ends_t = [ph.sb(f"ends_t{s}", [P, G * P]) for s in (0, 1)]
        gate = [ph.sb(f"gate{s}", [P, G, D]) for s in (0, 1)]
        sums_sb = [ph.sb(f"sums_sb{s}", [P, G * D]) for s in (0, 1)]
        src_i, dst_i, put_i = ([ph.sb(f"{n}{s}", [P, G], I32) for s in (0, 1)] for n in ("src_i", "dst_i", "put_i"))
        (indexed, staged, turned, matched, ends_turned, ends_copied, produced, gated, paid, summed, copied) = ph.sems(
            "indexed staged turned matched ends_turned ends_copied produced gated paid summed copied")
        gathered, scattered = ([ph.sem(f"{n}{s}") for s in (0, 1)] for n in ("gathered", "scattered"))
        key_t, ends_b, kqv_b, sums = bank[0:2], bank[2], bank[3:5], bank[5:7]
        if lead:
            src_keys = ph.sb("src_keys", [P, G])
            src_match = ph.sb("src_match", [P, G, G * P])
            ld = Leaders(nc, ph, st, "src")
            src_staged, src_turned, chain = ph.sems("src_staged src_turned chain")
        block = ph.ctx.enter_context(nc.Block())

        @block.gpsimd
        def _(pool):
            def rows_of(s):
                gather_rows(nc, [(ends[s][:, q, 0:D], q) for q in range(G)], table, dst_i[s], gathered[s], ph.passed)
                gather_rows(nc, [(ends[s][:, q, D:P], q) for q in range(G)], table, src_i[s], gathered[s], ph.passed)

            def step(n, i, s, first, last):
                if there(n + 2, BLOCKS):
                    pool.wait_ge(indexed, n + 3)
                    pool.wait_ge(ends_turned, n + 1)
                    rows_of(s)
                pool.wait_ge(copied, n + 1)
                if not (first and s == 0):
                    pool.wait_ge(scattered[1 - s], 64 * last_use(i, s))
                hold(pool, ph.passed)
                for q in range(G):
                    nc.gpsimd.indirect_dma_start(
                        table, bass.IndirectOffsetOnAxis(ap=put_i[s][:, q:q + 1], axis=0),
                        sums_sb[s][:, q * D:(q + 1) * D], None, compute_op=ALU.add).then_inc(scattered[s], 16)

            for s in (0, 1):
                pool.wait_ge(indexed, s + 1)
                rows_of(s)
            over_pairs(pool, BLOCKS, step)
            for s in (0, 1):
                pool.wait_ge(scattered[s], 64 * (BLOCKS // 2))

        @block.vector
        def _(dve):
            if lead:
                steps = Steps(dve, chain, Leaders.STEPS + 1)

            def stage(n, s):
                bl.stage(n, s, ()).then_inc(staged, 1)

            def step(n, i, s, first, last):
                dve.wait_ge(turned, n + 1)
                if not first:
                    dve.wait_ge(summed, n - 1)
                bl.make_match(key_t[s], s).then_inc(matched, 1)
                dve.wait_ge(gated, n + 1)
                nc.vector.tensor_tensor(bl.payload[s][:], gate[s][:],
                                        kqv_b[s][:].rearrange("p (t w) -> p t w", w=P)[:, :, D:P], ALU.mult
                                        ).then_inc(paid, 1)
                if lead:
                    steps.turn(n)
                    dve.wait_ge(src_turned, n + 1)
                    for q in range(G):
                        w = (q + 1) * P
                        ins = nc.vector.tensor_scalar(src_match[:, q, 0:w], bank[7][:, 0:w], src_keys[:, q:q + 1],
                                                      None, ALU.is_equal)
                    steps.then(ins)
                    ld.find(steps, src_match, src_keys, (st["src_put"][:, bass.ds(n * G, G)],))
                    steps.end()
                    if not (last and s == 1):
                        nc.vector.tensor_copy(src_keys[:], st["src_key"][:, bass.ds(n * G + G, G)]
                                              ).then_inc(src_staged, 1)
                if not last:
                    dve.wait_ge(matched, n + 1)
                    stage(n + 2, s)

            if lead:
                nc.vector.tensor_copy(src_keys[:], st["src_key"][:, 0:G]).then_inc(src_staged, 1)
            for s in (0, 1):
                stage(s, s)
            over_pairs(dve, BLOCKS, step)

        @block.scalar
        def _(act):
            def index(n, i, s):
                put_indices(nc, act, n, i, s, ((src_i[s], st["src_g2"]), (dst_i[s], st["dst_g2"])), gathered[s], 128,
                            indexed)

            def step(n, i, s, first, last):
                if there(n + 2, BLOCKS):
                    index(*ahead(n, i, s, 2))
                act.wait_ge(ends_turned, n + 1)
                if not first:
                    act.wait_ge(produced, n - 1)
                nc.scalar.activation(ends_t[s][:], ends_b[:], ACT.Copy).then_inc(ends_copied, 1)
                act.wait_ge(produced, n + 1)
                if not first:
                    act.wait_ge(paid, n - 1)
                nc.scalar.activation(gate[s][:], kqv_b[s][:].rearrange("p (t w) -> p t w", w=P)[:, :, 0:D],
                                     ACT.Sigmoid).then_inc(gated, 1)
                act.wait_ge(summed, n + 1)
                if not first:
                    act.wait_ge(scattered[s], 64 * i)
                nc.scalar.activation(put_i[s][:], st["dst_put2"][:, bass.ds(n * G, G)], ACT.Copy)
                nc.scalar.activation(sums_sb[s][:], sums[s][:, 0:G * D], ACT.Copy).then_inc(copied, 1)

            for s in (0, 1):
                index(s, 0, s)
            over_pairs(act, BLOCKS, step)

        @block.tensor
        def _(pe):
            def turn(n, s):
                pe.wait_ge(staged, n + 1)
                bl.turn_keys(key_t[s], s).then_inc(turned, 1)

            def step(n, i, s, first, last):
                if not (last and s == 1):
                    turn(n + 1, 1 - s)
                pe.wait_ge(gathered[s], 128 * (i + 1))
                if not n_is(n, 0, first):
                    pe.wait_ge(ends_copied, n)
                for q in range(G):
                    ins = nc.tensor.transpose(ends_b[:, q * P:(q + 1) * P], ends[s][:, q, :], ident[:])
                ins.then_inc(ends_turned, 1)
                pe.wait_ge(ends_copied, n + 1)
                if not first:
                    pe.wait_ge(paid, n - 1)
                for q in range(G):
                    ins = nc.tensor.matmul(kqv_b[s][:, q * P:(q + 1) * P], ends_t[s][:, q * P:(q + 1) * P], weight[:],
                                           start=True, stop=True)
                ins.then_inc(produced, 1)
                if lead:
                    pe.wait_ge(src_staged, n + 1)
                    for q in range(G):
                        ins = nc.tensor.transpose(bank[7][:, q * P:(q + 1) * P],
                                                  src_keys[:, q:q + 1].broadcast_to([P, P]), ident[:])
                    ins.then_inc(src_turned, 1)
                pe.wait_ge(matched, n + 1)
                pe.wait_ge(paid, n + 1)
                if not first:
                    pe.wait_ge(copied, n - 1)
                bl.segment_sums(sums[s], s).then_inc(summed, 1)

            turn(0, 0)
            over_pairs(pe, BLOCKS, step)


def sage_sums(nc, st, tag, table):
    BLOCKS, bank = st["BLOCKS"], st["bank"]
    W = D + 1
    with Phase(nc, tag) as ph:
        bl = Blocks(nc, ph, st, st["dst_key"], W)
        xs = [ph.sb(f"xs{s}", [P, G, W]) for s in (0, 1)]
        sums_sb = [ph.sb(f"sums_sb{s}", [P, G * W]) for s in (0, 1)]
        src_i, put_i = ([ph.sb(f"{n}{s}", [P, G], I32) for s in (0, 1)] for n in ("src_i", "put_i"))
        indexed, staged, turned, matched, paid, summed, copied = ph.sems(
            "indexed staged turned matched paid summed copied")
        gathered, scattered = ([ph.sem(f"{n}{s}") for s in (0, 1)] for n in ("gathered", "scattered"))
        key_t, sums = bank[0:2], bank[2:4]
        block = ph.ctx.enter_context(nc.Block())

        @block.gpsimd
        def _(pool):
            def rows_of(s):
                gather_rows(nc, [(xs[s][:, q, :], q) for q in range(G)], table, src_i[s], gathered[s], ph.passed)

            def step(n, i, s, first, last):
                pool.wait_ge(copied, n + 1)
                if not (first and s == 0):
                    pool.wait_ge(scattered[1 - s], 64 * last_use(i, s))
                hold(pool, ph.passed)
                for q in range(G):
                    nc.gpsimd.indirect_dma_start(
                        table, bass.IndirectOffsetOnAxis(ap=put_i[s][:, q:q + 1], axis=0),
                        sums_sb[s][:, q * W:(q + 1) * W], None, compute_op=ALU.add).then_inc(scattered[s], 16)
                if there(n + 3, BLOCKS):
                    pool.wait_ge(indexed, n + 4)
                    pool.wait_ge(paid, n + 2)
                    rows_of(1 - s)

            for n in (0, 1, 2):
                pool.wait_ge(indexed, n + 1)
                if not fresh(n):
                    pool.wait_ge(paid, n - 1)
                rows_of(n % 2)
            over_pairs(pool, BLOCKS, step)
            for s in (0, 1):
                pool.wait_ge(scattered[s], 64 * (BLOCKS // 2))

        @block.vector
        def _(dve):
            def stage(n, s):
                bl.stage(n, s, ()).then_inc(staged, 1)

            def step(n, i, s, first, last):
                w = st["w_exp"][:, bass.ds(n * G, G)]
                dve.wait_ge(turned, n + 1)
                if not first:
                    dve.wait_ge(summed, n - 1)
                bl.make_match(key_t[s], s).then_inc(matched, 1)
                dve.wait_ge(gathered[s], 64 * (i + 1))
                nc.vector.tensor_copy(bl.payload[s][:, :, D], w)
                nc.vector.tensor_tensor(bl.payload[s][:, :, 0:D], xs[s][:, :, 0:D], bcast(w, D), ALU.mult
                                        ).then_inc(paid, 1)
                if not last:
                    dve.wait_ge(matched, n + 1)
                    stage(n + 2, s)

            for s in (0, 1):
                stage(s, s)
            over_pairs(dve, BLOCKS, step)

        @block.scalar
        def _(act):
            def index(n, i, s):
                put_indices(nc, act, n, i, s, ((src_i[s], st["src_g2"]),), gathered[s], 64, indexed)

            def step(n, i, s, first, last):
                if there(n + 3, BLOCKS):
                    index(*ahead(n, i, s, 3))
                act.wait_ge(summed, n + 1)
                if not first:
                    act.wait_ge(scattered[s], 64 * i)
                nc.scalar.activation(put_i[s][:], st["dst_put2"][:, bass.ds(n * G, G)], ACT.Copy)
                nc.scalar.activation(sums_sb[s][:], sums[s][:, 0:G * W], ACT.Copy).then_inc(copied, 1)

            for n in (0, 1, 2):
                index(n, n // 2, n % 2)
            over_pairs(act, BLOCKS, step)

        @block.tensor
        def _(pe):
            def turn(n, s):
                pe.wait_ge(staged, n + 1)
                bl.turn_keys(key_t[s], s).then_inc(turned, 1)

            def step(n, i, s, first, last):
                if not (last and s == 1):
                    turn(n + 1, 1 - s)
                pe.wait_ge(matched, n + 1)
                pe.wait_ge(paid, n + 1)
                if not first:
                    pe.wait_ge(copied, n - 1)
                bl.segment_sums(sums[s], s).then_inc(summed, 1)

            turn(0, 0)
            over_pairs(pe, BLOCKS, step)


def first_node(st, n):
    return min(n * CHUNK, st["N"] - CHUNK) if isinstance(n, int) else n * CHUNK


def loads(sp, ph, st, load, used):
    CHUNKS = st["CHUNKS"]

    def step(n, i, s, first, last):
        if there(n + 2, CHUNKS):
            for sem, per in used:
                sp.wait_ge(sem, n * per + per)
                hold(sp, ph.passed)
            load(s, first_node(st, n + 2))

    for s in (0, 1):
        load(s, first_node(st, s))
    over_pairs(sp, CHUNKS, step)


def stores(pool, ph, st, store, ready, stored, beside=None):
    CHUNKS = st["CHUNKS"]

    def step(n, i, s, first, last):
        if beside:
            beside(n, i, s)
        pool.wait_ge(ready, n + 1)
        if not there(n + 1, CHUNKS):
            pool.wait_ge(stored[0], 16 * (i + 1))
        hold(pool, ph.passed)
        store(s, first_node(st, n)).then_inc(stored[s], 16)

    over_pairs(pool, CHUNKS, step)
    for s in (0, 1):
        pool.wait_ge(stored[s], 16 * (CHUNKS // 2))


class Residual:

    def __init__(self, ph, st, rows, table, res_in, used):
        self.ph, self.st, self.rows, self.table, self.res_in, self.used = ph, st, rows, table, res_in, used

    def load(self, pool, n, s):
        pool.dma_start(self.rows[s][:], x_of(self.table, first_node(self.st, n))).then_inc(self.res_in[s], 16)

    def start(self, pool):
        for s in (0, 1):
            self.load(pool, s, s)

    def beside(self, pool, n, s):
        if there(n + 2, self.st["CHUNKS"]):
            pool.wait_ge(self.used, n + 1)
            hold(pool, self.ph.passed)
            self.load(pool, n + 2, s)


def table_rows(tab, row, per=1):
    return tab[bass.ds(row * per, CHUNK * per)].rearrange("(p r) w -> p (r w)", p=P)


def x_of(tab, row):
    return tab[bass.ds(row * 2, CHUNK * 2)].rearrange("(p r two) w -> p r two w", p=P, two=2)[:, :, 0, 0:D]


def over_rows(ap):
    return ap.unsqueeze(1).broadcast_to([P, R, ap.shape[1]])


class Norm:

    def __init__(self, nc, ph, st, tag, by_log=False):
        self.nc, self.by_log, self.eps = nc, by_log, st["eps"]
        self.sum, self.mean, self.var, self.root, self.rstd = (
            ph.sb(f"{tag}_{n}", [P, R]) for n in ("sum", "mean", "var", "root", "rstd"))
        self.square = ph.sb(f"{tag}_square", [P, R, D])
        self.centred, self.squared, self.summed, self.rooted, self.act_chain = ph.sems(
            f"{tag}_centred {tag}_squared {tag}_summed {tag}_rooted {tag}_act_chain")

    def steps(self):
        return 0 if self.by_log else 1

    def take_mean(self, steps, v):
        steps.then(self.nc.vector.reduce_sum(self.sum[:], v, AX_X))
        steps.then(self.nc.vector.tensor_scalar(self.mean[:], self.sum[:], -1.0 / D, None, ALU.mult))
        self.nc.vector.tensor_tensor(v, v, bcast(self.mean[:], D), ALU.add).then_inc(self.centred, 1)

    def squares(self, act, n, v, ready=None):
        act.wait_ge(ready or self.centred, n + 1)
        self.nc.scalar.activation(self.square[:], v, ACT.Square).then_inc(self.squared, 1)

    def take_root(self, act, n):
        nc = self.nc
        act.wait_ge(self.summed, n + 1)
        if self.by_log:
            nc.scalar.activation(self.root[:], self.var[:], ACT.Ln, scale=1.0 / D, bias=self.eps[:]
                                 ).then_inc(self.act_chain, 1)
            act.wait_ge(self.act_chain, n + 1)
            nc.scalar.activation(self.rstd[:], self.root[:], ACT.Exp, scale=-0.5).then_inc(self.rooted, 1)
        else:
            nc.scalar.activation(self.root[:], self.var[:], ACT.Sqrt, scale=1.0 / D, bias=self.eps[:]
                                 ).then_inc(self.rooted, 1)

    def sum_squares(self, dve, n):
        dve.wait_ge(self.squared, n + 1)
        self.nc.vector.reduce_sum(self.var[:], self.square[:], AX_X).then_inc(self.summed, 1)

    def scale(self, dve, steps, n, v, out):
        dve.wait_ge(self.rooted, n + 1)
        if not self.by_log:
            steps.then(self.nc.vector.reciprocal(self.rstd[:], self.root[:]))
        return self.nc.vector.tensor_tensor(out, v, bcast(self.rstd[:], D), ALU.mult)


class Product:

    def __init__(self, nc, ph, st, tag, width, turn_banks, out_banks):
        self.nc, self.st, self.passed = nc, st, ph.passed
        self.pair = P // width
        self.turns = R // self.pair * P // 512
        self.width = width * self.pair
        self.turn_banks, self.out_banks = turn_banks, out_banks
        self.rows_t = [[ph.sb(f"{tag}_t{s}{h}", [self.width, 512]) for h in range(self.turns)] for s in (0, 1)]
        self.turned, self.copied, self.done = ph.sems(f"{tag}_turned {tag}_copied {tag}_done")
        self.slots = len(turn_banks) // self.turns

    def turn_bank(self, s, h):
        return self.turn_banks[(s * self.turns if self.slots == 2 else 0) + h]

    def turn(self, pe, n, s, rows, ready):
        pe.wait_ge(ready[0], ready[1])
        if not fresh(n, self.slots):
            pe.wait_ge(self.copied, (n + 1 - self.slots) * self.turns)
        hold(pe, self.passed)
        for h in range(self.turns):
            for r in range(512 // P):
                q = (h * (512 // P) + r) * self.pair
                block = rows[:, q, :] if self.pair == 1 else flat(rows[:, q:q + self.pair, :])
                ins = self.nc.tensor.transpose(self.turn_bank(s, h)[0:self.width, r * P:(r + 1) * P], block,
                                               self.st["ident"][:])
            ins.then_inc(self.turned, 1)

    def copy(self, act, n, s):
        for h in range(self.turns):
            act.wait_ge(self.turned, n * self.turns + h + 1)
            if not fresh(n):
                act.wait_ge(self.done, n - 1)
            self.nc.scalar.activation(self.rows_t[s][h][:], self.turn_bank(s, h)[0:self.width, :], ACT.Copy
                                      ).then_inc(self.copied, 1)

    def multiply(self, pe, n, s, weight, read):
        k, w = len(self.out_banks), D * self.pair
        b = self.out_banks[s if k == 2 else 0]
        if not fresh(n, k):
            pe.wait_ge(read, n + 1 - k)
        for h in range(self.turns):
            pe.wait_ge(self.copied, n * self.turns + h + 1)
            for r in range(512 // P):
                q = h * (512 // P) + r
                ins = self.nc.tensor.matmul(b[:, q * w:(q + 1) * w], self.rows_t[s][h][:, r * P:(r + 1) * P], weight,
                                            start=True, stop=True)
        ins.then_inc(self.done, 1)

    def result(self, s):
        b = self.out_banks[s if len(self.out_banks) == 2 else 0]
        return b[:].rearrange("p (r d) -> p r d", d=D)


def product_program(pe, st, pr, rows, ready, weight, read):
    def turn(n, i, s):
        for sem, value in ready(n, i, s)[:-1]:
            pe.wait_ge(sem, value)
        pr.turn(pe, n, s, rows[s], ready(n, i, s)[-1])

    def step(n, i, s, first, last):
        if there(n + 1, st["CHUNKS"]):
            turn(*ahead(n, i, s, 1))
        pr.multiply(pe, n, s, weight, read)

    turn(0, 0, 0)
    over_pairs(pe, st["CHUNKS"], step)


def flat(ap):
    return ap.rearrange("p r d -> p (r d)")


def dense_mean(nc, a, st):
    CHUNKS, BLOCKS, bank = st["CHUNKS"], st["BLOCKS"], st["bank"]
    assert CHUNKS == BLOCKS
    with Phase(nc, "d0") as ph:
        x, agg = ([ph.sb(f"{n}{s}", [P, R, w]) for s in (0, 1)] for n, w in (("x", D), ("agg", 66)))
        both = [ph.sb(f"both{s}", [P, R, P]) for s in (0, 1)]
        out = [ph.sb(f"out{s}", [P, R, P]) for s in (0, 1)]
        v = [ph.sb(f"v{s}", [P, R, D]) for s in (0, 1)]
        recip = ph.sb("recip", [P, R])
        max_of = [ph.sb(f"max_of{s}", [P, G]) for s in (0, 1)]
        max_i = [ph.sb(f"max_i{s}", [P, G], I32) for s in (0, 1)]
        pr = Product(nc, ph, st, "p", P, bank[0:4], bank[4:6])
        ln = Norm(nc, ph, st, "n")
        x_put, scaled, added, normed, chain_a, chain_b, max_staged, max_used, self_arg = ph.sems(
            "x_put scaled added normed chain_a chain_b max_staged max_used self_arg")
        loaded, stored, max_in = ([ph.sem(f"{n}{s}") for s in (0, 1)] for n in ("loaded", "stored", "max_in"))
        block = ph.ctx.enter_context(nc.Block())

        @block.sync
        def _(sp):
            def load(s, row):
                sp.dma_start(flat(x[s][:]), table_rows(a["x"], row)).then_inc(loaded[s], 16)
                sp.dma_start(flat(agg[s][:]), table_rows(st["mean_tab"], row)).then_inc(loaded[s], 16)

            loads(sp, ph, st, load, ((scaled, 1), (x_put, 1)))

        @block.gpsimd
        def _(pool):
            maxima = st["mean_tab"].rearrange("n (w o) -> (n w) o", o=1)

            def gather(n, i, s):
                pool.wait_ge(max_staged, n + 1)
                gather_rows(nc, [(max_of[s][:, q:q + 1], q) for q in range(G)], maxima, max_i[s], max_in[s], ph.passed)

            def store(s, row):
                return pool.dma_start(table_rows(st["gate1_tab"], row, 2), flat(out[s][:]))

            def gather_next(n, i, s):
                if there(n + 1, CHUNKS):
                    gather(*ahead(n, i, s, 1))

            gather(0, 0, 0)
            stores(pool, ph, st, store, normed, stored, beside=gather_next)

        @block.vector
        def _(dve):
            steps_a, steps_b = Steps(dve, chain_a, 2), Steps(dve, chain_b, ln.steps())

            def stage_max(n, s):
                nc.vector.tensor_scalar(max_i[s][:], st["dst_g"][:, bass.ds(n * G, G)], 66.0, 65.0, ALU.mult, ALU.add
                                        ).then_inc(max_staged, 1)

            def scale(n, i, s):
                steps_a.turn(n)
                dve.wait_ge(loaded[s], 32 * (i + 1))
                if not fresh(n):
                    dve.wait_ge(pr.turned, n * 2 - 2)
                if not fresh(n, 1):
                    dve.wait_ge(scaled, n)
                cols = bass.ds(n * R, R)
                nc.vector.tensor_copy(st["degree"][:, cols], agg[s][:, :, 64])
                nc.vector.tensor_copy(st["self_exp"][:, cols], agg[s][:, :, 65])
                steps_a.then(nc.vector.tensor_scalar(recip[:], agg[s][:, :, 64], 1.0, None, ALU.max))
                steps_a.then(nc.vector.reciprocal(recip[:], recip[:]))
                nc.vector.tensor_tensor(both[s][:, :, D:P], agg[s][:, :, 0:D], bcast(recip[:], D), ALU.mult
                                        ).then_inc(scaled, 1)
                steps_a.end()

            def add(n, i, s):
                dve.wait_ge(pr.done, n + 1)
                if not fresh(n):
                    dve.wait_ge(normed, n - 1)
                nc.vector.tensor_tensor(v[s][:], pr.result(s), over_rows(st["rows"][:, st["B_MEAN"], :]), ALU.add
                                        ).then_inc(added, 1)

            def step(n, i, s, first, last):
                steps_b.turn(n)
                if there(n + 1, CHUNKS):
                    add(*ahead(n, i, s, 1))
                ln.sum_squares(dve, n)
                if there(n + 4, CHUNKS):
                    scale(*ahead(n, i, s, 4))
                if not fresh(n):
                    dve.wait_ge(stored[s], 16 * i)
                ln.scale(dve, steps_b, n, v[s][:], out[s][:, :, 0:D]).then_inc(normed, 1)
                steps_b.end()
                dve.wait_ge(max_in[s], 64 * (i + 1))
                cols = bass.ds(n * G, G)
                nc.vector.tensor_tensor(st["w_exp"][:, cols], st["w_edge"][:, cols], max_of[s][:], ALU.subtract
                                        ).then_inc(max_used, 1)
                if there(n + 2, CHUNKS):
                    dve.wait_ge(max_used, n + 1)
                    stage_max(n + 2, s)

            for s in (0, 1):
                nc.vector.memset(out[s][:, :, D:P], 0.0)
                stage_max(s, s)
            for n in range(4):
                scale(n, n // 2, n % 2)
            add(0, 0, 0)
            over_pairs(dve, CHUNKS, step)
            nc.vector.tensor_scalar(st["self_exp"][:], st["self_exp"][:], -1.0, 1.0, ALU.mult, ALU.add
                                    ).then_inc(self_arg, 1)

        @block.scalar
        def _(act):
            act.preload_act_table_set("sqrt_and_others")

            def put_x(n, i, s):
                act.wait_ge(loaded[s], 32 * (i + 1))
                if not fresh(n):
                    act.wait_ge(pr.turned, n * 2 - 2)
                nc.scalar.activation(both[s][:, :, 0:D], x[s][:], ACT.Copy).then_inc(x_put, 1)

            def step(n, i, s, first, last):
                if not fresh(n, 1):
                    act.wait_ge(ln.summed, n)
                ln.squares(act, n, v[s][:], added)
                if there(n + 2, CHUNKS):
                    pr.copy(act, n + 2, s)
                ln.take_root(act, n)
                if there(n + 4, CHUNKS):
                    put_x(*ahead(n, i, s, 4))

            put_x(0, 0, 0)
            put_x(1, 0, 1)
            pr.copy(act, 0, 0)
            put_x(2, 1, 0)
            pr.copy(act, 1, 1)
            put_x(3, 1, 1)
            over_pairs(act, CHUNKS, step)
            act.wait_ge(self_arg, 1)
            nc.scalar.activation(st["self_exp"][:], st["self_exp"][:], ACT.Exp)
            nc.scalar.activation(st["w_exp"][:], st["w_exp"][:], ACT.Exp)

        @block.tensor
        def _(pe):
            product_program(pe, st, pr, both, lambda n, i, s: ((scaled, n + 1), (x_put, n + 1)), st["w_self"][:],
                            added)


def dense_gate(nc, st, tag, table, which, residual, dest):
    CHUNKS, bank = st["CHUNKS"], st["bank"]
    final = residual is not None
    W = D if final else P
    with Phase(nc, tag) as ph:
        both = [ph.sb(f"both{s}", [P, R, P]) for s in (0, 1)]
        out = [ph.sb(f"out{s}", [P, R, W]) for s in (0, 1)]
        v = [ph.sb(f"v{s}", [P, R, D]) for s in (0, 1)]
        res = [ph.sb(f"res{s}", [P, R, D]) for s in (0, 1)]
        pr = Product(nc, ph, st, "p", P, bank[0:4], bank[4:6])
        ln = Norm(nc, ph, st, "n")
        added, mixed, finished, chain, chain_m = ph.sems("added mixed finished chain chain_m")
        loaded, stored, res_in = ([ph.sem(f"{n}{s}") for s in (0, 1)] for n in ("loaded", "stored", "res_in"))
        bias = over_rows(st["rows"][:, st["B_MIX1"] + which, :])
        block = ph.ctx.enter_context(nc.Block())

        @block.sync
        def _(sp):
            def load(s, row):
                sp.dma_start(flat(both[s][:]), table_rows(table, row, 2)).then_inc(loaded[s], 16)

            loads(sp, ph, st, load, ((pr.turned, 2),))

        @block.gpsimd
        def _(pool):
            def store(s, row):
                return pool.dma_start(table_rows(dest, row, W // D), flat(out[s][:]))

            more = Residual(ph, st, res, residual, res_in, mixed)
            if final:
                more.start(pool)
            stores(pool, ph, st, store, finished, stored,
                   beside=(lambda n, i, s: more.beside(pool, n, s)) if final else None)

        @block.vector
        def _(dve):
            steps, steps_m = Steps(dve, chain, ln.steps()), Steps(dve, chain_m, 2)

            def add(n, i, s):
                dve.wait_ge(pr.done, n + 1)
                if not fresh(n):
                    dve.wait_ge(finished, n - 1)
                nc.vector.tensor_tensor(v[s][:], pr.result(s), bias, ALU.add).then_inc(added, 1)
                if final:
                    dve.wait_ge(added, n + 1)
                    dve.wait_ge(res_in[s], 16 * (i + 1))
                    nc.vector.scalar_tensor_tensor(out=v[s][:], in0=v[s][:], scalar=0.0, in1=res[s][:], op0=ALU.max,
                                                   op1=ALU.add).then_inc(mixed, 1)

            def centre(n, s):
                steps_m.turn(n)
                dve.wait_ge(mixed, n + 1)
                ln.take_mean(steps_m, v[s][:])
                steps_m.end()

            def step(n, i, s, first, last):
                if not final:
                    add(n, i, s)
                    return
                more = there(n + 1, CHUNKS)
                if more:
                    add(*ahead(n, i, s, 1))
                ln.sum_squares(dve, n)
                if more:
                    centre(n + 1, 1 - s)
                else:
                    dve.wait_ge(finished, n)
                steps.turn(n)
                if not fresh(n):
                    dve.wait_ge(stored[s], 16 * i)
                ln.scale(dve, steps, n, v[s][:], out[s][:]).then_inc(finished, 1)
                steps.end()

            if final:
                add(0, 0, 0)
                centre(0, 0)
            else:
                for s in (0, 1):
                    nc.vector.memset(out[s][:, :, D:P], 0.0)
            over_pairs(dve, CHUNKS, step)

        @block.scalar
        def _(act):
            act.preload_act_table_set("sqrt_and_others")

            def step(n, i, s, first, last):
                if final:
                    if not fresh(n, 1):
                        act.wait_ge(ln.summed, n)
                    ln.squares(act, n, v[s][:])
                else:
                    act.wait_ge(added, n + 1)
                    if not fresh(n):
                        act.wait_ge(stored[s], 16 * i)
                    nc.scalar.activation(out[s][:, :, 0:D], v[s][:], ACT.Relu).then_inc(finished, 1)
                if there(n + 2, CHUNKS):
                    pr.copy(act, n + 2, s)
                if final:
                    ln.take_root(act, n)

            pr.copy(act, 0, 0)
            pr.copy(act, 1, 1)
            over_pairs(act, CHUNKS, step)

        @block.tensor
        def _(pe):
            product_program(pe, st, pr, both, lambda n, i, s: ((loaded[s], 16 * (i + 1)),), st["w_mix"][which][:],
                            added)


def attention_sums(nc, st):
    BLOCKS, bank, ident = st["BLOCKS"], st["bank"], st["ident"]
    HW = DH + 1
    W = H * HW
    QW = 3 * D + H
    with Phase(nc, "att") as ph:
        bl = Blocks(nc, ph, st, st["src_key"], W)
        ends = [ph.sb(f"ends{s}", [P, G, P]) for s in (0, 1)]
        ends_t = ph.sb("ends_t", [P, G * P])
        far_key = [ph.sb(f"far_key{s}", [P, G]) for s in (0, 1)]
        qkv = ph.sb("qkv", [P, G, QW])
        state, new = ([ph.sb(f"{n}{s}", [P, G, W + H]) for s in (0, 1)] for n in ("state", "new"))
        src_i, dst_i, row_i, put_i = ([ph.sb(f"{n}{s}", [P, G], I32) for s in (0, 1)]
                                      for n in ("src_i", "dst_i", "row_i", "put_i"))
        away = [ph.sb(f"away{s}", [P, G, G * P]) for s in (0, 1)]
        junk = [ph.sb(f"junk{k}", [P, G, G * P]) for k in (0, 1)]
        prod, vals = ph.sb("prod", [P, G, D]), ph.sb("vals", [P, G, D])
        logit, ex_arg, ex = (ph.sb(n, [P, G, H]) for n in ("logit", "ex_arg", "ex"))
        top = [ph.sb(f"top{s}", [P, G, H]) for s in (0, 1)]
        diff, factor = ph.sb("diff", [P, 2, G, H]), ph.sb("factor", [P, 2, G, H])
        old_part, new_part = ph.sb("old_part", [P, G, W]), ph.sb("new_part", [P, G, W])
        (indexed, staged, turned, matched, away_done, ends_turned, ends_copied, produced, qkv_copied, logits, qkv_used,
         logit_turned, head_max, ex_ready, ex_done, paid, summed, differences, factors, updated, chain_f, chain_b,
         chain_u) = ph.sems(
            "indexed staged turned matched away_done ends_turned ends_copied produced qkv_copied logits qkv_used "
            "logit_turned head_max ex_ready ex_done paid summed differences factors updated chain_f chain_b chain_u")
        gathered, state_in, scattered = ([ph.sem(f"{n}{s}") for s in (0, 1)] for n in
                                         ("gathered", "state_in", "scattered"))
        key_t, ends_b, qkv_b, logit_t, sums = bank[0], bank[1], bank[2:4], bank[4:6], bank[6:8]
        block = ph.ctx.enter_context(nc.Block())

        @block.gpsimd
        def _(pool):
            def dst_rows(s):
                gather_rows(nc, [(ends[s][:, q, 0:D], q) for q in range(G)], st["attn_x"], dst_i[s],
                            gathered[s], ph.passed)

            def src_rows(s):
                gather_rows(nc, [(ends[s][:, q, D:P], q) for q in range(G)], st["attn_x"], src_i[s],
                            gathered[s], ph.passed)

            def step(n, i, s, first, last):
                more = there(n + 2, BLOCKS)
                if more:
                    pool.wait_ge(indexed, n + 3)
                    pool.wait_ge(ends_turned, n + 1)
                    dst_rows(s)
                pool.wait_ge(staged, n + 1)
                if not fresh(n, 1):
                    pool.wait_ge(scattered[1 - s], 64 * last_use(i, s))
                gather_rows(nc, [(state[s][:, q, :], q) for q in range(G)], st["attn_tab"], row_i[s], state_in[s],
                            ph.passed)
                if more:
                    src_rows(s)
                pool.wait_ge(updated, n + 1)
                hold(pool, ph.passed)
                for q in range(G):
                    nc.gpsimd.indirect_dma_start(
                        st["attn_tab"], bass.IndirectOffsetOnAxis(ap=put_i[s][:, q:q + 1], axis=0),
                        new[s][:, q, :], None).then_inc(scattered[s], 16)

            for s in (0, 1):
                pool.wait_ge(indexed, s + 1)
                dst_rows(s)
                src_rows(s)
            over_pairs(pool, BLOCKS, step)
            for s in (0, 1):
                pool.wait_ge(scattered[s], 64 * (BLOCKS // 2))

        @block.vector
        def _(dve):
            steps_f, steps_b, steps_u = Steps(dve, chain_f, 3), Steps(dve, chain_b, 1), Steps(dve, chain_u, 2)

            def heads(ap):
                return ap.rearrange("p t (h c) -> p t h c", h=H)

            def over_heads(ap):
                return ap.unsqueeze(2).broadcast_to([P, G, H, EF])

            def per_head(ap, w):
                return ap.unsqueeze(3).broadcast_to([P, G, H, w])

            def front(n):
                steps_f.turn(n)
                kv = st["edge_kv"][:, bass.ds(n * G, G), :]
                dve.wait_ge(qkv_copied, n + 1)
                steps_f.then(nc.vector.tensor_tensor(heads(prod[:]), heads(qkv[:, :, D + H:2 * D + H]),
                                                     over_heads(kv[:, :, 0:EF]), ALU.mult))
                steps_f.then(nc.vector.tensor_tensor(prod[:], prod[:], qkv[:, :, 0:D], ALU.mult))
                steps_f.then(nc.vector.reduce_sum(logit[:], heads(prod[:]), AX_X))
                nc.vector.tensor_tensor(logit[:], logit[:], qkv[:, :, D:D + H], ALU.add).then_inc(logits, 1)
                nc.vector.tensor_tensor(heads(vals[:]), heads(qkv[:, :, 2 * D + H:QW]),
                                        over_heads(kv[:, :, EF:2 * EF]), ALU.mult).then_inc(qkv_used, 1)
                steps_f.end()

            def find_max(n, s, part):
                dve.wait_ge(away_done, n + 1)
                for h in part:
                    dve.wait_ge(logit_turned, n * H + h + 1)
                    hold(dve, ph.passed)
                    for q in range(G):
                        ins = nc.vector.tensor_tensor_reduce(junk[h % 2][:, q, :], logit_t[h % 2][:],
                                                             away[s][:, q, :], 1.0, -2.0 * BIG, ALU.subtract,
                                                             ALU.max, top[s][:, q, h:h + 1])
                    ins.then_inc(head_max, 1)

            def pay(n, s):
                steps_b.turn(n)
                if not fresh(n):
                    dve.wait_ge(summed, n - 1)
                dve.wait_ge(head_max, n * H + H)
                nc.vector.tensor_tensor(ex_arg[:], logit[:], top[s][:], ALU.subtract).then_inc(ex_ready, 1)
                dve.wait_ge(ex_done, n + 1)
                dve.wait_ge(qkv_used, n + 1)
                out = heads(bl.payload[s][:])
                steps_b.then(nc.vector.tensor_copy(out[:, :, :, DH], ex[:]))
                nc.vector.tensor_tensor(out[:, :, :, 0:DH], heads(vals[:]), per_head(ex[:], DH), ALU.mult
                                        ).then_inc(paid, 1)
                steps_b.end()

            def update(n, i, s, first):
                steps_u.turn(n)
                dve.wait_ge(state_in[s], 64 * (i + 1))
                if not first:
                    dve.wait_ge(scattered[s], 64 * i)
                old, row = state[s], new[s]
                steps_u.then(nc.vector.tensor_tensor(row[:, :, W:W + H], old[:, :, W:W + H], top[s][:], ALU.max))
                nc.vector.tensor_tensor(diff[:, 0], old[:, :, W:W + H], row[:, :, W:W + H], ALU.subtract)
                nc.vector.tensor_tensor(diff[:, 1], top[s][:], row[:, :, W:W + H], ALU.subtract
                                        ).then_inc(differences, 1)
                dve.wait_ge(factors, n + 1)
                nc.vector.tensor_tensor(heads(old_part[:]), heads(old[:, :, 0:W]), per_head(factor[:, 0], HW), ALU.mult)
                dve.wait_ge(summed, n + 1)
                steps_u.then(nc.vector.tensor_tensor(
                    heads(new_part[:]), heads(sums[s][:, 0:G * W].rearrange("p (t w) -> p t w", w=W)),
                    per_head(factor[:, 1], HW), ALU.mult))
                nc.vector.tensor_tensor(row[:, :, 0:W], old_part[:], new_part[:], ALU.add).then_inc(updated, 1)
                steps_u.end()

            def step(n, i, s, first, last):
                find_max(n, s, (2, 3))
                pay(n, s)
                if there(n + 1, BLOCKS):
                    front(n + 1)
                    find_max(n + 1, 1 - s, (0, 1))
                update(n, i, s, first)

            front(0)
            find_max(0, 0, (0, 1))
            over_pairs(dve, BLOCKS, step)

        @block.scalar
        def _(act):
            act.preload_act_table_set("natural_log_exp_and_others")

            def index(n, i, s):
                put_indices(nc, act, n, i, s, ((src_i[s], st["src_g"]), (dst_i[s], st["dst_g"])), gathered[s], 128,
                            indexed)

            def stage(n, i, s):
                if not fresh(n):
                    act.wait_ge(state_in[s], 64 * i)
                    act.wait_ge(turned, n - 1)
                    act.wait_ge(away_done, n - 1)
                    hold(act, ph.passed)
                cols = bass.ds(n * G, G)
                nc.scalar.activation(row_i[s][:], st["src_g"][:, cols], ACT.Copy)
                nc.scalar.activation(far_key[s][:], st["src_key"][:, cols], ACT.Copy, scale=-BIG)
                nc.scalar.activation(bl.keys[s][:], st["src_key"][:, cols], ACT.Copy).then_inc(staged, 1)

            def copies(n):
                act.wait_ge(ends_turned, n + 1)
                if not fresh(n, 1):
                    act.wait_ge(produced, n)
                nc.scalar.activation(ends_t[:], ends_b[:], ACT.Copy).then_inc(ends_copied, 1)
                act.wait_ge(produced, n + 1)
                if not fresh(n, 1):
                    act.wait_ge(qkv_used, n)
                for k in (0, 1):
                    ins = nc.scalar.activation(qkv[:, 2 * k:2 * k + 2, :],
                                               qkv_b[k][:, 0:2 * QW].rearrange("p (t w) -> p t w", w=QW), ACT.Copy)
                ins.then_inc(qkv_copied, 1)

            def put_away(n, s):
                act.wait_ge(turned, n + 1)
                act.wait_ge(staged, n + 1)
                if not fresh(n):
                    act.wait_ge(head_max, (n - 1) * H)
                for q in range(G):
                    ins = nc.scalar.activation(away[s][:, q, :], key_t[:], ACT.Abs, scale=BIG,
                                               bias=far_key[s][:, q:q + 1])
                ins.then_inc(away_done, 1)

            def match(n, s):
                act.wait_ge(away_done, n + 1)
                if not fresh(n):
                    act.wait_ge(summed, n - 1)
                for q in range(G):
                    ins = nc.scalar.activation(bl.match[s][:, q, :], away[s][:, q, :], ACT.Relu, scale=-1.0 / BIG,
                                               bias=st["one"][:])
                ins.then_inc(matched, 1)

            def step(n, i, s, first, last):
                if there(n + 2, BLOCKS):
                    index(*ahead(n, i, s, 2))
                if there(n + 1, BLOCKS):
                    copies(n + 1)
                act.wait_ge(ex_ready, n + 1)
                if not fresh(n, 1):
                    act.wait_ge(paid, n)
                nc.scalar.activation(ex[:], ex_arg[:], ACT.Exp).then_inc(ex_done, 1)
                if there(n + 1, BLOCKS):
                    put_away(n + 1, 1 - s)
                    match(n + 1, 1 - s)
                if not fresh(n):
                    act.wait_ge(scattered[s], 64 * i)
                nc.scalar.activation(put_i[s][:], st["src_put"][:, bass.ds(n * G, G)], ACT.Copy)
                act.wait_ge(differences, n + 1)
                if not fresh(n, 1):
                    act.wait_ge(updated, n)
                nc.scalar.activation(factor[:], diff[:], ACT.Exp).then_inc(factors, 1)
                if there(n + 2, BLOCKS):
                    stage(*ahead(n, i, s, 2))

            for s in (0, 1):
                index(s, 0, s)
                stage(s, 0, s)
            copies(0)
            put_away(0, 0)
            match(0, 0)
            over_pairs(act, BLOCKS, step)

        @block.tensor
        def _(pe):
            def front(n, i, s, first):
                pe.wait_ge(gathered[s], 128 * (i + 1))
                if not first:
                    pe.wait_ge(ends_copied, n)
                for q in range(G):
                    ins = nc.tensor.transpose(ends_b[:, q * P:(q + 1) * P], ends[s][:, q, :], ident[:])
                ins.then_inc(ends_turned, 1)
                pe.wait_ge(staged, n + 1)
                if not first:
                    pe.wait_ge(away_done, n)
                bl.turn_keys(key_t, s).then_inc(turned, 1)
                pe.wait_ge(ends_copied, n + 1)
                if not first:
                    pe.wait_ge(qkv_copied, n)
                for q in range(G):
                    ins = nc.tensor.matmul(qkv_b[q // 2][:, q % 2 * QW:(q % 2 + 1) * QW], ends_t[:, q * P:(q + 1) * P],
                                           st["w_att"][:], start=True, stop=True)
                ins.then_inc(produced, 1)

            def turn_logits(n, part):
                pe.wait_ge(logits, n + 1)
                for h in part:
                    if not (fresh(n, 1) and h < 2):
                        pe.wait_ge(head_max, n * H + h - 1)
                    for q in range(G):
                        ins = nc.tensor.transpose(logit_t[h % 2][:, q * P:(q + 1) * P],
                                                  logit[:, q, h:h + 1].broadcast_to([P, P]), ident[:])
                    ins.then_inc(logit_turned, 1)

            def step(n, i, s, first, last):
                more = there(n + 1, BLOCKS)
                if more:
                    front(n + 1, i + s, 1 - s, False)
                pe.wait_ge(matched, n + 1)
                pe.wait_ge(paid, n + 1)
                if not first:
                    pe.wait_ge(updated, n - 1)
                bl.segment_sums(sums[s], s, (0,))
                if more:
                    turn_logits(n + 1, (0, 1))
                bl.segment_sums(sums[s], s, (1, 2, 3)).then_inc(summed, 1)
                if more:
                    turn_logits(n + 1, (2, 3))

            front(0, 0, 0, True)
            turn_logits(0, range(H))
            over_pairs(pe, BLOCKS, step)


def dense_attention(nc, st):
    CHUNKS, bank, rows = st["CHUNKS"], st["bank"], st["rows"]
    HW = DH + 1
    with Phase(nc, "da") as ph:
        x, agg, res = ([ph.sb(f"{n}{s}", [P, R, w]) for s in (0, 1)] for n, w in (("x", D), ("agg", 72), ("res", D)))
        both = [ph.sb(f"both{s}", [P, R, P]) for s in (0, 1)]
        out = [ph.sb(f"out{s}", [P, R, 130]) for s in (0, 1)]
        v = [ph.sb(f"v{s}", [P, R, D]) for s in (0, 1)]
        weighed = [ph.sb(f"weighed{s}", [P, R, D]) for s in (0, 1)]
        part = [ph.sb(f"part{s}", [P, R, H]) for s in (0, 1)]
        recip = ph.sb("recip", [P, R, H])
        z, e, soft, bias = (ph.sb(n, [P, R, D]) for n in ("z", "e", "soft", "bias"))
        p1 = Product(nc, ph, st, "p1", P, bank[0:2], bank[4:6])
        p2 = Product(nc, ph, st, "p2", D, bank[2:4], bank[6:8])
        ln1 = Norm(nc, ph, st, "n1", by_log=True)
        ln2 = Norm(nc, ph, st, "n2", by_log=True)
        (x_put, scaled, biased, added1, added2, weighing, logged, softened, res_moved, res_used, finished, chain_a,
         chain_b,
         chain_c, chain_m, chain_l) = ph.sems(
             "x_put scaled biased added1 added2 weighing logged softened res_moved res_used finished chain_a chain_b "
             "chain_c chain_m chain_l")
        loaded, stored, res_in = ([ph.sem(f"{n}{s}") for s in (0, 1)] for n in ("loaded", "stored", "res_in"))
        block = ph.ctx.enter_context(nc.Block())

        def heads(ap):
            return ap.rearrange("p r (h c) -> p r h c", h=H)

        def per_head(ap):
            return ap.unsqueeze(3).broadcast_to([P, R, H, DH])

        @block.sync
        def _(sp):
            def load(n, s):
                if not fresh(n):
                    sp.wait_ge(scaled, n - 1)
                    sp.wait_ge(x_put, n - 1)
                row = first_node(st, n)
                sp.dma_start(flat(x[s][:]), table_rows(st["attn_x"], row)).then_inc(loaded[s], 16)
                sp.dma_start(flat(agg[s][:]), table_rows(st["attn_tab"], row)).then_inc(loaded[s], 16)

            def load_res(n, s):
                sp.dma_start(flat(res[s][:]), table_rows(st["attn_x"], first_node(st, n))).then_inc(res_in[s], 16)

            def step(n, i, s, first, last):
                if there(n + 6, CHUNKS):
                    load(n + 6, s)
                if there(n + 2, CHUNKS):
                    sp.wait_ge(res_used, n + 1)
                    load_res(n + 2, s)
                sp.wait_ge(finished, n + 1)
                if not there(n + 1, CHUNKS):
                    sp.wait_ge(stored[0], 16 * (i + 1))
                sp.dma_start(table_rows(st["sage1_tab"], first_node(st, n), 2), flat(out[s][:])
                             ).then_inc(stored[s], 16)

            for n in (0, 1):
                load(n, n)
                load_res(n, n)
            for n in (2, 3, 4, 5):
                load(n, n % 2)
            over_pairs(sp, CHUNKS, step, tail=8)
            for s in (0, 1):
                sp.wait_ge(stored[s], 16 * (CHUNKS // 2))

        @block.gpsimd
        def _(pool):
            steps_b = Steps(pool, chain_b, 1)

            def put_x(n, i, s):
                pool.wait_ge(loaded[s], 32 * (i + 1))
                if not fresh(n):
                    pool.wait_ge(p1.turned, n * 2 - 2)
                hold(pool, ph.passed)
                nc.gpsimd.tensor_copy(both[s][:, :, 0:D], x[s][:]).then_inc(x_put, 1)

            def make_bias(n, i, s):
                steps_b.turn(n)
                pool.wait_ge(scaled, n + 1)
                if not fresh(n, 1):
                    pool.wait_ge(added1, n)
                steps_b.then(nc.gpsimd.tensor_tensor(heads(bias[:]), per_head(part[s][:]),
                                                     heads(over_rows(rows[:, st["B_VL"], :])), ALU.mult))
                nc.gpsimd.tensor_tensor(bias[:], bias[:], over_rows(rows[:, st["B_CEN"], :]), ALU.add
                                        ).then_inc(biased, 1)
                steps_b.end()

            def move_res(n, i, s):
                pool.wait_ge(res_in[s], 16 * (i + 1))
                nc.gpsimd.tensor_tensor(res[s][:], res[s][:], over_rows(rows[:, st["B_LNB"], :]), ALU.add
                                        ).then_inc(res_moved, 1)

            def weigh(n, i, s):
                pool.wait_ge(added2, n + 1)
                if not fresh(n):
                    pool.wait_ge(res_used, n - 1)
                nc.gpsimd.tensor_tensor(weighed[s][:], v[s][:], over_rows(rows[:, st["B_LNG"], :]), ALU.mult
                                        ).then_inc(weighing, 1)

            def step(n, i, s, first, last):
                if there(n + 3, CHUNKS):
                    make_bias(*ahead(n, i, s, 3))
                if there(n + 4, CHUNKS):
                    put_x(*ahead(n, i, s, 4))
                if there(n + 1, CHUNKS):
                    move_res(*ahead(n, i, s, 1))
                    weigh(*ahead(n, i, s, 1))

            put_x(0, 0, 0)
            make_bias(0, 0, 0)
            put_x(1, 0, 1)
            put_x(2, 1, 0)
            make_bias(1, 0, 1)
            put_x(3, 1, 1)
            make_bias(2, 1, 0)
            move_res(0, 0, 0)
            weigh(0, 0, 0)
            over_pairs(pool, CHUNKS, step)

        @block.vector
        def _(dve):
            steps_a, steps_c, steps_m = Steps(dve, chain_a, 2), Steps(dve, chain_c, 1), Steps(dve, chain_m, 2)

            def scale(n, i, s):
                steps_a.turn(n)
                dve.wait_ge(loaded[s], 32 * (i + 1))
                if not fresh(n):
                    dve.wait_ge(p1.turned, n * 2 - 2)
                    dve.wait_ge(biased, n - 1)
                if not fresh(n, 1):
                    dve.wait_ge(scaled, n)
                hd = agg[s][:, :, 0:H * HW].rearrange("p r (h c) -> p r h c", c=HW)
                steps_a.then(nc.vector.tensor_scalar(recip[:], hd[:, :, :, DH], 1e-16, None, ALU.add))
                steps_a.then(nc.vector.reciprocal(recip[:], recip[:]))
                nc.vector.tensor_tensor(part[s][:], hd[:, :, :, DH], recip[:], ALU.mult)
                nc.vector.tensor_tensor(heads(both[s][:, :, D:P]), hd[:, :, :, 0:DH], per_head(recip[:]), ALU.mult
                                        ).then_inc(scaled, 1)
                steps_a.end()

            def add1(n, i, s):
                dve.wait_ge(biased, n + 1)
                dve.wait_ge(p1.done, n + 1)
                if not fresh(n, 1):
                    dve.wait_ge(softened, n)
                nc.vector.tensor_tensor(z[:], p1.result(s), bias[:], ALU.add).then_inc(added1, 1)

            def soften(n, i, s):
                dve.wait_ge(logged, n + 1)
                if not fresh(n, 1):
                    dve.wait_ge(p2.turned, n)
                nc.vector.scalar_tensor_tensor(out=soft[:], in0=z[:], scalar=0.0, in1=e[:], op0=ALU.max, op1=ALU.add
                                               ).then_inc(softened, 1)

            def add2(n, i, s):
                dve.wait_ge(p2.done, n + 1)
                if not fresh(n):
                    dve.wait_ge(finished, n - 1)
                nc.vector.tensor_tensor(v[s][:], p2.result(s), over_rows(rows[:, st["B_OUT"], :]), ALU.add
                                        ).then_inc(added2, 1)

            def norm1(n, i, s):
                steps_c.turn(n)
                steps_m.turn(n)
                dve.wait_ge(weighing, n + 1)
                steps_c.then(ln1.scale(dve, steps_c, n, weighed[s][:], v[s][:]))
                dve.wait_ge(res_moved, n + 1)
                nc.vector.tensor_tensor(v[s][:], v[s][:], res[s][:], ALU.add).then_inc(res_used, 1)
                dve.wait_ge(res_used, n + 1)
                ln2.take_mean(steps_m, v[s][:])
                steps_c.end()
                steps_m.end()

            def finish(n, i, s):
                if not fresh(n):
                    dve.wait_ge(stored[s], 16 * i)
                ln2.scale(dve, None, n, v[s][:], out[s][:, :, 0:D]).then_inc(finished, 1)

            def step(n, i, s, first, last):
                if there(n + 2, CHUNKS):
                    add1(*ahead(n, i, s, 2))
                if not fresh(n, 1):
                    finish(n - 1, i + s - 1, 1 - s)
                ln1.sum_squares(dve, n)
                if there(n + 4, CHUNKS):
                    scale(*ahead(n, i, s, 4))
                if there(n + 2, CHUNKS):
                    soften(*ahead(n, i, s, 2))
                norm1(n, i, s)
                if there(n + 1, CHUNKS):
                    add2(*ahead(n, i, s, 1))
                ln2.sum_squares(dve, n)

            for s in (0, 1):
                nc.vector.memset(out[s][:, :, D:130], 0.0)
            scale(0, 0, 0)
            scale(1, 0, 1)
            add1(0, 0, 0)
            scale(2, 1, 0)
            soften(0, 0, 0)
            add1(1, 0, 1)
            scale(3, 1, 1)
            soften(1, 0, 1)
            add2(0, 0, 0)
            over_pairs(dve, CHUNKS, step)
            finish(CHUNKS - 1, CHUNKS // 2 - 1, 1)

        @block.scalar
        def _(act):
            act.preload_act_table_set("natural_log_exp_and_others")

            def log_part(n):
                act.wait_ge(added1, n + 1)
                if not fresh(n, 1):
                    act.wait_ge(softened, n)
                nc.scalar.activation(e[:], z[:], ACT.Abs).then_inc(chain_l, 1)
                act.wait_ge(chain_l, n * 2 + 1)
                nc.scalar.activation(e[:], e[:], ACT.Exp, scale=-1.0).then_inc(chain_l, 1)
                act.wait_ge(chain_l, n * 2 + 2)
                nc.scalar.activation(e[:], e[:], ACT.Ln, bias=st["half"][:], scale=0.5).then_inc(logged, 1)

            def step(n, i, s, first, last):
                ln1.squares(act, n, v[s][:], added2)
                if there(n + 2, CHUNKS):
                    log_part(n + 2)
                ln1.take_root(act, n)
                if there(n + 3, CHUNKS):
                    p1.copy(act, n + 3, 1 - s)
                ln2.squares(act, n, v[s][:])
                if there(n + 2, CHUNKS):
                    p2.copy(act, n + 2, s)
                ln2.take_root(act, n)

            p1.copy(act, 0, 0)
            log_part(0)
            p1.copy(act, 1, 1)
            p2.copy(act, 0, 0)
            log_part(1)
            p1.copy(act, 2, 0)
            p2.copy(act, 1, 1)
            over_pairs(act, CHUNKS, step)

        @block.tensor
        def _(pe):
            def turn1(n, s):
                pe.wait_ge(scaled, n + 1)
                p1.turn(pe, n, s, both[s], (x_put, n + 1))

            def multiply1(n, s):
                p1.multiply(pe, n, s, st["w_att_out"][:], added1)

            def turn2(n, s):
                p2.turn(pe, n, s, soft, (softened, n + 1))

            def multiply2(n, s):
                p2.multiply(pe, n, s, st["w_out"][:], added2)

            def step(n, i, s, first, last):
                if there(n + 3, CHUNKS):
                    turn1(n + 3, 1 - s)
                if there(n + 1, CHUNKS):
                    multiply2(n + 1, 1 - s)
                if there(n + 2, CHUNKS):
                    turn2(n + 2, s)
                if there(n + 3, CHUNKS):
                    multiply1(n + 3, 1 - s)

            turn1(0, 0)
            multiply1(0, 0)
            turn1(1, 1)
            turn2(0, 0)
            multiply1(1, 1)
            turn1(2, 0)
            multiply2(0, 0)
            turn2(1, 1)
            multiply1(2, 0)
            over_pairs(pe, CHUNKS, step)


def dense_sage(nc, st, tag, table, which, residual, dest):
    CHUNKS, bank = st["CHUNKS"], st["bank"]
    final = residual is not None
    W = D if final else 130
    K = D + 1
    with Phase(nc, tag) as ph:
        both = [ph.sb(f"both{s}", [P, R, 2 * K]) for s in (0, 1)]
        own, mix, out, v, more = ([ph.sb(f"{n}{s}", [P, R, w]) for s in (0, 1)] for n, w in (
            ("own", D), ("mix", D), ("out", W), ("v", D), ("more", D)))
        bias = ph.sb("bias", [P, R, D])
        total, deg1 = ph.sb("total", [P, R]), ph.sb("deg1", [P, R])
        pr = Product(nc, ph, st, "p", D, bank[0:2], bank[4:6])
        ln = Norm(nc, ph, st, "n")
        owned, mixed, added, more_ready, more_used, finished, chain, chain_n, chain_m, chain_b = ph.sems(
            "owned mixed added more_ready more_used finished chain chain_n chain_m chain_b")
        loaded, stored, res_in = ([ph.sem(f"{n}{s}") for s in (0, 1)] for n in ("loaded", "stored", "res_in"))
        block = ph.ctx.enter_context(nc.Block())

        @block.sync
        def _(sp):
            def load(n, s):
                if not fresh(n):
                    sp.wait_ge(mixed, n - 1)
                    hold(sp, ph.passed)
                sp.dma_start(flat(both[s][:]), table_rows(table, first_node(st, n), 2)).then_inc(loaded[s], 16)

            def load_res(n, s):
                if final:
                    if not fresh(n):
                        sp.wait_ge(more_used, n - 1)
                        hold(sp, ph.passed)
                    sp.dma_start(more[s][:], x_of(residual, first_node(st, n))).then_inc(res_in[s], 16)

            def step(n, i, s, first, last):
                if there(n + 2, CHUNKS):
                    load_res(n + 2, s)
                if there(n + 6, CHUNKS):
                    load(n + 6, s)
                sp.wait_ge(finished, n + 1)
                if not there(n + 1, CHUNKS):
                    sp.wait_ge(stored[0], 16 * (i + 1))
                sp.dma_start(table_rows(dest, first_node(st, n), 1 if final else 2), flat(out[s][:])
                             ).then_inc(stored[s], 16)

            for n in (0, 1):
                load(n, n)
                load_res(n, n)
            for n in (2, 3, 4, 5):
                load(n, n % 2)
            over_pairs(sp, CHUNKS, step, tail=8)
            for s in (0, 1):
                sp.wait_ge(stored[s], 16 * (CHUNKS // 2))

        @block.gpsimd
        def _(pool):
            steps_b = Steps(pool, chain_b, 1)

            def scale_own(n, i, s):
                pool.wait_ge(loaded[s], 16 * (i + 1))
                if not fresh(n):
                    pool.wait_ge(mixed, n - 1)
                nc.gpsimd.tensor_tensor(own[s][:], both[s][:, :, 0:D], bcast(st["self_exp"][:, bass.ds(n * R, R)], D),
                                        ALU.mult).then_inc(owned, 1)

            def make_more(n, i, s):
                pool.wait_ge(mixed, n + 1)
                if not fresh(n):
                    pool.wait_ge(more_used, n - 1)
                share = bcast(st["share"][:, bass.ds(n * R, R)], D)
                row = over_rows(st["rows"][:, st["B_SAGE1"] + which, :])
                if final:
                    if not fresh(n, 1):
                        pool.wait_ge(more_ready, n)
                    steps_b.turn(n)
                    steps_b.then(nc.gpsimd.tensor_tensor(bias[:], row, share, ALU.mult))
                    pool.wait_ge(res_in[s], 16 * (i + 1))
                    nc.gpsimd.tensor_tensor(more[s][:], more[s][:], bias[:], ALU.add).then_inc(more_ready, 1)
                    steps_b.end()
                else:
                    nc.gpsimd.tensor_tensor(more[s][:], row, share, ALU.mult).then_inc(more_ready, 1)

            def step(n, i, s, first, last):
                if there(n + 4, CHUNKS):
                    scale_own(*ahead(n, i, s, 4))
                if there(n + 2, CHUNKS):
                    make_more(*ahead(n, i, s, 2))

            scale_own(0, 0, 0)
            scale_own(1, 0, 1)
            make_more(0, 0, 0)
            make_more(1, 0, 1)
            scale_own(2, 1, 0)
            scale_own(3, 1, 1)
            over_pairs(pool, CHUNKS, step)

        @block.vector
        def _(dve):
            steps, steps_n, steps_m = (
                Steps(dve, chain, ln.steps()), Steps(dve, chain_n, 2), Steps(dve, chain_m, 4))

            def mix_rows(n, i, s):
                dve.wait_ge(loaded[s], 16 * (i + 1))
                dve.wait_ge(owned, n + 1)
                if not fresh(n):
                    dve.wait_ge(pr.turned, n - 1)
                if not final:
                    if not fresh(n, 1):
                        dve.wait_ge(mixed, n)
                    steps_m.turn(n)
                    cols = bass.ds(n * R, R)
                    rho = st["rho"][:, cols]
                    nc.vector.tensor_scalar(deg1[:], st["degree"][:, cols], 1.0, None, ALU.add)
                    steps_m.then(nc.vector.tensor_tensor(total[:], both[s][:, :, 2 * K - 1], st["self_exp"][:, cols],
                                                         ALU.add))
                    steps_m.then(nc.vector.tensor_scalar(rho, total[:], 1e-16, None, ALU.add))
                    steps_m.then(nc.vector.tensor_tensor(rho, rho, deg1[:], ALU.mult))
                    hold(dve, ph.passed)
                    steps_m.then(nc.vector.reciprocal(rho, rho))
                    nc.vector.tensor_tensor(st["share"][:, cols], rho, total[:], ALU.mult)
                    steps_m.end()
                nc.vector.tensor_tensor(mix[s][:], own[s][:], both[s][:, :, K:K + D], ALU.add).then_inc(mixed, 1)

            def add(n, i, s):
                dve.wait_ge(pr.done, n + 1)
                if not fresh(n):
                    dve.wait_ge(finished, n - 1)
                nc.vector.tensor_tensor(v[s][:], pr.result(s),
                                        bcast(st["rho"][:, bass.ds(n * R, R)], D), ALU.mult).then_inc(added, 1)
                dve.wait_ge(added, n + 1)
                dve.wait_ge(more_ready, n + 1)
                nc.vector.tensor_tensor(v[s][:], v[s][:], more[s][:], ALU.add).then_inc(more_used, 1)

            def centre(n, s):
                steps_n.turn(n)
                dve.wait_ge(more_used, n + 1)
                ln.take_mean(steps_n, v[s][:])
                steps_n.end()

            def step(n, i, s, first, last):
                following = there(n + 1, CHUNKS)
                if not final:
                    add(n, i, s)
                elif following:
                    add(*ahead(n, i, s, 1))
                if final:
                    ln.sum_squares(dve, n)
                    if following:
                        centre(n + 1, 1 - s)
                    else:
                        dve.wait_ge(finished, n)
                if there(n + 4, CHUNKS):
                    mix_rows(*ahead(n, i, s, 4))
                if final:
                    steps.turn(n)
                    if not fresh(n):
                        dve.wait_ge(stored[s], 16 * i)
                    ln.scale(dve, steps, n, v[s][:], out[s][:]).then_inc(finished, 1)
                    steps.end()

            if not final:
                for s in (0, 1):
                    nc.vector.memset(out[s][:, :, D:W], 0.0)
            for n in range(4):
                mix_rows(n, n // 2, n % 2)
            if final:
                add(0, 0, 0)
                centre(0, 0)
            over_pairs(dve, CHUNKS, step)

        @block.scalar
        def _(act):
            act.preload_act_table_set("sqrt_and_others")

            def step(n, i, s, first, last):
                if final:
                    ln.squares(act, n, v[s][:])
                else:
                    act.wait_ge(more_used, n + 1)
                    if not fresh(n):
                        act.wait_ge(stored[s], 16 * i)
                    nc.scalar.activation(out[s][:, :, 0:D], v[s][:], ACT.Relu).then_inc(finished, 1)
                if there(n + 2, CHUNKS):
                    pr.copy(act, n + 2, s)
                if final:
                    ln.take_root(act, n)

            pr.copy(act, 0, 0)
            pr.copy(act, 1, 1)
            over_pairs(act, CHUNKS, step)

        @block.tensor
        def _(pe):
            product_program(pe, st, pr, mix, lambda n, i, s: ((mixed, n + 1),), st["w_sage"][which][:], added)


INPUTS = ["x", "src", "dst", "edge_attr_16", "edge_weight", "edge_weight1"] + [f"L0_gnn_{n}" for n in (
    "W_self", "b_self", "W_neigh", "b_neigh")] + [f"L1_gnn_{n}" for n in (
        "Wk1", "Wq1", "Wv1", "Ws1", "b1", "Wl1", "bl1", "Wk2", "Wq2", "Wv2", "Ws2", "b2", "Wl2", "bl2")] + [
            f"L2_gnn_{n}" for n in (
                "Wk", "Wq", "Wv", "wk1_w", "wk1_b", "wk2_w", "wk2_b", "wkl_w", "wkl_b", "wv1_w", "wv1_b", "wv2_w",
                "wv2_b", "wvl_w", "wvl_b", "cen_w", "cen_b", "out_w", "out_b", "ln_g", "ln_b")] + [
                    f"L3_gnn_{n}" for n in ("lin1_w", "lin1_b", "W1", "lin2_w", "lin2_b", "W2")]


def kernel(**inputs):
    import numpy as np
    import concourse.bacc as bacc
    from concourse.bass_utils import run_bass_kernel_spmd

    nc = bacc.Bacc("TRN2", target_bir_lowering=False, num_devices=1)
    arrays, aps = {}, {}
    for name in INPUTS:
        arr = np.ascontiguousarray(inputs[name])
        arrays[f"in_{name}"] = arr
        aps[name] = nc.dram_tensor(f"in_{name}", arr.shape, mybir.dt.from_np(arr.dtype), kind="ExternalInput").ap()
    shape = arrays["in_x"].shape
    out = nc.dram_tensor("out_0", shape, F32, kind="ExternalOutput").ap()
    gnn_program(nc, aps, out)
    got = run_bass_kernel_spmd(nc, [arrays], core_ids=[0])
    return got.results[0]["out_0"]
```
